# Optimizing a Trainium2 kernel written in Bass

```python
import numpy as np
import jax
import jax.numpy as jnp

def _softmax(x, axis=-1):
    return jax.nn.softmax(x, axis=axis)

def _gelu(x):
    return jax.nn.gelu(x, approximate=True)

def _silu(x):
    return jax.nn.silu(x)

def _sigmoid(x):
    return jax.nn.sigmoid(x)

def _layernorm(x, axis=-1, eps=1e-05):
    m = jnp.mean(x, axis=axis, keepdims=True)
    v = jnp.var(x, axis=axis, keepdims=True)
    return (x - m) / jnp.sqrt(v + eps)

def _scatter_add(tgt, idx, src, axis=0):
    return tgt.at[idx].add(src)

def _segment_sum(src, seg, n):
    return jax.ops.segment_sum(src, seg, n)
kernel_name = 'mk_gnn_resnorm_d1_gnn_r32_07449a'

def setup_inputs(seed: int=0):
    np.random.seed(seed)
    _w = jnp.asarray

    def _rec_inputs():
        import jax
        import jax.numpy as jnp
        _gk = jax.random.key(seed)
        x = -0.0003713 + 1 * jax.random.normal(jax.random.fold_in(_gk, 1), (3125, 128), jnp.float32)
        src = jax.random.randint(jax.random.fold_in(_gk, 2), (50000,), 0, 3125, jnp.int32)
        dst = jnp.minimum((3125 * jax.random.uniform(jax.random.fold_in(_gk, 3), (50000,)) ** 2.0).astype(jnp.int32), 99999)
        _o = jnp.argsort(dst, stable=True)
        src = src[_o]
        dst = dst[_o]
        edge_attr_4 = 0.000669165 + 0.999965 * jax.random.normal(jax.random.fold_in(_gk, 11), (50000, 4), jnp.float32)
        return (x, src, dst, edge_attr_4)
    x, src, dst, edge_attr_4 = _rec_inputs()

    def _L0_gnn_setup():
        import jax, jax.numpy as jnp
        import numpy as np
        N_NODES = 3125
        N_EDGES = 18750
        D = 128
        H = 256
        RAW = 4
        STEPS = 4
        EPS = 1e-05

        def _swish(v):
            return v * jax.nn.sigmoid(v)

        def _layernorm(v, g, b):
            m = jnp.mean(v, axis=-1, keepdims=True)
            var = jnp.var(v, axis=-1, keepdims=True)
            return (v - m) * jax.lax.rsqrt(var + EPS) * g + b
        key = jax.random.key(seed)
        ks = jax.random.split(key, 16)

        def w(k, shape, fan_in):
            return jax.random.normal(k, shape, dtype=jnp.float32) / np.sqrt(fan_in)
        x = jax.random.normal(ks[0], (N_NODES, D), dtype=jnp.float32)
        edge_index = jax.random.randint(ks[1], (2, N_EDGES), 0, N_NODES, dtype=jnp.int32)
        edge_attr_raw = jax.random.normal(ks[2], (N_EDGES, RAW), dtype=jnp.float32)
        return {'x': x, 'edge_index': edge_index, 'edge_attr_raw': edge_attr_raw, 'enc_W': w(ks[3], (RAW, D), RAW), 'enc_b': jnp.zeros((D,), jnp.float32), 'eW1': w(ks[4], (3 * D, H), 3 * D), 'eb1': jnp.zeros((H,), jnp.float32), 'eW2': w(ks[5], (H, D), H), 'eb2': jnp.zeros((D,), jnp.float32), 'eg': jnp.ones((D,), jnp.float32), 'ebeta': jnp.zeros((D,), jnp.float32), 'nW1': w(ks[6], (2 * D, H), 2 * D), 'nb1': jnp.zeros((H,), jnp.float32), 'nW2': w(ks[7], (H, D), H), 'nb2': jnp.zeros((D,), jnp.float32), 'ng': jnp.ones((D,), jnp.float32), 'nbeta': jnp.zeros((D,), jnp.float32)}
    _L0_gnn_all = _L0_gnn_setup()
    _L0_gnn_in = {k: v for k, v in _L0_gnn_all.items() if k in ('enc_W', 'enc_b', 'eW1', 'eb1', 'eW2', 'eb2', 'eg', 'ebeta', 'nW1', 'nb1', 'nW2', 'nb2', 'ng', 'nbeta')}
    del _L0_gnn_all
    return {'x': x, 'src': src, 'dst': dst, 'edge_attr_4': edge_attr_4, 'L0_gnn_enc_W': _L0_gnn_in['enc_W'], 'L0_gnn_enc_b': _L0_gnn_in['enc_b'], 'L0_gnn_eW1': _L0_gnn_in['eW1'], 'L0_gnn_eb1': _L0_gnn_in['eb1'], 'L0_gnn_eW2': _L0_gnn_in['eW2'], 'L0_gnn_eb2': _L0_gnn_in['eb2'], 'L0_gnn_eg': _L0_gnn_in['eg'], 'L0_gnn_ebeta': _L0_gnn_in['ebeta'], 'L0_gnn_nW1': _L0_gnn_in['nW1'], 'L0_gnn_nb1': _L0_gnn_in['nb1'], 'L0_gnn_nW2': _L0_gnn_in['nW2'], 'L0_gnn_nb2': _L0_gnn_in['nb2'], 'L0_gnn_ng': _L0_gnn_in['ng'], 'L0_gnn_nbeta': _L0_gnn_in['nbeta']}

def reference(x, src, dst, edge_attr_4, L0_gnn_enc_W, L0_gnn_enc_b, L0_gnn_eW1, L0_gnn_eb1, L0_gnn_eW2, L0_gnn_eb2, L0_gnn_eg, L0_gnn_ebeta, L0_gnn_nW1, L0_gnn_nb1, L0_gnn_nW2, L0_gnn_nb2, L0_gnn_ng, L0_gnn_nbeta):
    import jax
    import jax.numpy as jnp

    def _L0_gnn_ref(x, edge_index, edge_attr_raw, enc_W, enc_b, eW1, eb1, eW2, eb2, eg, ebeta, nW1, nb1, nW2, nb2, ng, nbeta):
        import jax, jax.numpy as jnp
        import numpy as np
        N_NODES = 3125
        N_EDGES = 18750
        D = 128
        H = 256
        RAW = 4
        STEPS = 4
        EPS = 1e-05

        def _swish(v):
            return v * jax.nn.sigmoid(v)

        def _layernorm(v, g, b):
            m = jnp.mean(v, axis=-1, keepdims=True)
            var = jnp.var(v, axis=-1, keepdims=True)
            return (v - m) * jax.lax.rsqrt(var + EPS) * g + b
        src = edge_index[0]
        dst = edge_index[1]
        edge_attr = _swish(edge_attr_raw @ enc_W + enc_b)
        for _ in range(STEPS):
            e_in = jnp.concatenate([edge_attr, x[src], x[dst]], axis=-1)
            e_upd = _layernorm(_swish(e_in @ eW1 + eb1) @ eW2 + eb2, eg, ebeta)
            edge_attr = edge_attr + e_upd
            agg = jax.ops.segment_sum(edge_attr, dst, num_segments=N_NODES)
            n_in = jnp.concatenate([x, agg], axis=-1)
            x = x + _layernorm(_swish(n_in @ nW1 + nb1) @ nW2 + nb2, ng, nbeta)
        return x
    edge_index = jnp.stack([src, dst])
    x = _layernorm(x + _L0_gnn_ref(x, edge_index, edge_attr_4, L0_gnn_enc_W, L0_gnn_enc_b, L0_gnn_eW1, L0_gnn_eb1, L0_gnn_eW2, L0_gnn_eb2, L0_gnn_eg, L0_gnn_ebeta, L0_gnn_nW1, L0_gnn_nb1, L0_gnn_nW2, L0_gnn_nb2, L0_gnn_ng, L0_gnn_nbeta), axis=-1)
    return x

_drawn_inputs = setup_inputs


def setup_inputs(seed=0):
    import zlib

    import numpy as np

    out = dict(_drawn_inputs(seed))
    spreads = {'L0_gnn_enc_b': (0.0, 0.1),
     'L0_gnn_eb1': (0.0, 0.1),
     'L0_gnn_eb2': (0.0, 0.1),
     'L0_gnn_eg': (1.0, 0.2),
     'L0_gnn_ebeta': (0.0, 0.1),
     'L0_gnn_nb1': (0.0, 0.738),
     'L0_gnn_nb2': (0.0, 0.487),
     'L0_gnn_ng': (1.0, 0.2),
     'L0_gnn_nbeta': (0.0, 0.1)}
    factors = {}
    for name, (base, spread) in spreads.items():
        noise = np.random.default_rng([zlib.crc32(name.encode()), seed]).standard_normal(out[name].shape)
        drawn = base * np.exp(spread * noise) if base else spread * noise
        out[name] = jnp.asarray(drawn.astype(out[name].dtype))
    for name, factor in factors.items():
        out[name] = (out[name] * factor).astype(out[name].dtype)
    return out
```

```python
from contextlib import ExitStack

import concourse.bass as bass
from concourse import mybir

F32, F16, F8, I32 = mybir.dt.float32, mybir.dt.float16, mybir.dt.float8e4, mybir.dt.int32
ALU = mybir.AluOpType
ACT = mybir.ActivationFunctionType
AX = mybir.AxisListType
ds = bass.ds

P = 128
N, E = 3125, 50000
D, H, RAW, STEPS, EPS = 128, 256, 4, 4, 1e-5
TPG = 4
GE = TPG * P
G1 = -(-E // GE)
NT = -(-N // P)
NPAD = NT * P
G2 = (E + NT * (GE - 1)) // GE
G2 += G2 % 2
BIG = float(1 << 20)
LAST = E - (G1 - 1) * GE
CH = 5
NCH = NT // CH
CW = CH * P
EP, EC = 125, 400
RSQRT_SEED = float(0x5F3759DF)
FIRST = 3
NEWTON = 3
NEWTON_OPS = 2 + 3 * NEWTON


def build_program(nc, x_in, src_in, dst_in, attr_in, enc_W, enc_b, eW1, eb1, eW2, eb2, eg, ebeta,
                  nW1, nb1, nW2, nb2, ng, nbeta, out):
    ctx = ExitStack()
    with ctx:
        def sb(name, shape, dt):
            return ctx.enter_context(nc.sbuf_tensor(name, shape, dt))

        def sem(name):
            return ctx.enter_context(nc.semaphore(name))

        def dram(name, shape, dt):
            return nc.dram_tensor(name, shape, dt, kind="Internal").ap()

        p_table = dram("p_table", [NPAD, 2 * H], F16)
        q_table = dram("q_table", [NPAD, 2 * H], F16)
        onehot = dram("onehot", [G2, P, GE // 4], F32)
        onehot_t = dram("onehot_t", [G2, P, GE // 4], F32)
        state = dram("state", [G2, P, TPG * 2 * D], F16)
        x_rows = dram("x_rows", [NPAD, D], F32)
        x_cols = dram("x_cols", [D, NPAD], F32)
        degree = dram("degree", [P, NPAD], F32)
        rel_rows = dram("rel_rows", [G2, GE], F16)
        attr_p = dram("attr_p", [G2 * GE, RAW], F32)
        records = dram("records", [G2 * GE, 8], I32)

        scratch = sb("scratch", [P, 26624 // 4 + 15616], F32)
        agg = sb("agg", [P, NPAD], F32)
        idx_all = sb("idx_all", [P, G2, TPG], I32)
        rel_all = sb("rel_all", [P, TPG, P], F32)
        win = sb("win", [1, P], I32)
        flag = sb("flag", [1, 1], I32)
        w1_hi = sb("w1_hi", [P, H], F16)
        w1_lo = sb("w1_lo", [P, H], F16)
        w2_hi = sb("w2_hi", [P, 2, D], F16)
        w2_lo = sb("w2_lo", [P, 2, D], F16)
        v_bias = sb("v_bias", [64, GE], F16)
        g_row = sb("g_row", [P, D], F32)
        nw1 = sb("nw1", [P, 2, H], F32)
        nw2 = sb("nw2", [P, 2, D], F32)
        w_pq = sb("w_pq", [P, 2, H], F32)
        nb1_col = sb("nb1_col", [P, 2], F32)
        u_bias = sb("u_bias", [64, D], F16)
        ng_row = sb("ng_row", [P, D], F32)
        nbeta_row = sb("nbeta_row", [P, D], F32)
        p_bias = sb("p_bias", [64, H], F16)
        p_bias32 = sb("p_bias32", [1, H], F32)
        beta_w1 = sb("beta_w1", [1, H], F32)
        beta_col = sb("beta_col", [P, 1], F32)
        beta_sum = sb("beta_sum", [P, 1], F32)
        ones16 = sb("ones16", [P, P], F16)
        ident16 = sb("ident16", [P, P], F16)
        ident32 = sb("ident32", [P, P], F32)
        node_iota = sb("node_iota", [P, P], F16)
        part_iota = sb("part_iota", [P, 1], F32)
        enc_bd = sb("enc_bd", [TPG * RAW + 1, TPG, D], F32)

        arena = sb("arena", [P, 13000], F32)
        cut = [0]

        def take(words, dt=F32):
            a = cut[0]
            cut[0] += words
            assert cut[0] <= 13000, cut[0]
            v = arena[:, a:a + words]
            return v if dt == F32 else v.bitcast(dt)

        h32 = [take(2 * GE).rearrange("p (k e) -> p k e", k=2) for _ in range(2)]
        hh = [take(GE, F16).rearrange("p (k e) -> p k e", k=2) for _ in range(2)]
        hl = [take(GE, F16).rearrange("p (k e) -> p k e", k=2) for _ in range(2)]
        st_in = [take(GE, F16).rearrange("p (t c) -> p t c", t=TPG) for _ in range(2)]
        st_out = [take(GE, F16).rearrange("p (t c) -> p t c", t=TPG) for _ in range(2)]
        resid = [take(GE) for _ in range(2)]
        e_new = [take(GE) for _ in range(2)]
        sq = take(GE)
        rows = [take(TPG * H, F16).rearrange("p (t c) -> p t c", t=TPG) for _ in range(2)]
        q_win = [take(H, F16) for _ in range(2)]
        eT = [take(GE, F16).rearrange("p (k e) -> p k e", k=2) for _ in range(2)]
        oh = [take(GE // 4, F8) for _ in range(2)]
        oht = [take(GE // 4, F8) for _ in range(2)]
        ssq = take(8)
        nv = take(8)
        nt = take(8)
        idx_now = [take(TPG, I32) for _ in range(2)]
        edge_words = cut[0]
        cut[0] = 0
        xc = take(CW).rearrange("p (t f) -> p t f", t=CH)
        xTc = take(CW)
        hN = take(2 * CW).rearrange("p (k e) -> p k e", k=2)
        un = take(CW).rearrange("p (t f) -> p t f", t=CH)
        x0c = take(CW).rearrange("p (t f) -> p t f", t=CH)
        xTn = take(CW)
        sqn = take(D)
        stn = take(8)
        nvn = take(8)
        ntn = take(8)
        bst = take(CH * 6).rearrange("p (t s) -> p t s", t=CH)
        bag = take(CH * 2).rearrange("p (t s) -> p t s", t=CH)
        pq = [take(2 * H, F16).rearrange("p (s k e) -> p s k e", s=2, k=2) for _ in range(2)]
        cut[0] = 0
        at_in = [take(TPG * RAW + 1) for _ in range(2)]
        atT = [take(P) for _ in range(2)]
        e0 = [take(GE) for _ in range(2)]
        st0 = [take(GE, F16).rearrange("p (t c) -> p t c", t=TPG) for _ in range(2)]
        rel_b = [take(GE // 2, F16) for _ in range(2)]
        rel_now = [take(TPG) for _ in range(2)]
        oh0 = [take(GE // 4, F8) for _ in range(2)]
        oht0 = [take(GE // 4, F8) for _ in range(2)]
        d_grp = take(GE)
        s_grp = take(GE)
        d_int = take(GE, I32)
        s_int = take(GE, I32)
        rel16 = take(GE // 2, F16)
        tmpw = take(GE)
        tmpv = take(GE)
        red = take(16)
        zero = take(GE)
        cut[0] = 0
        gp = scratch[:, 0:15616]
        gcut = [0]

        def gtake(words, dt=F32):
            a = gcut[0]
            gcut[0] += words
            assert gcut[0] <= 15616
            v = gp[:, a:a + words]
            return v if dt == F32 else v.bitcast(dt)

        g_rec = gtake(EC * 8, I32).rearrange("p (e w) -> p e w", w=8)
        g_dst = gtake(EC, I32)
        g_src = gtake(EC, I32)
        g_attr = gtake(EC * RAW, I32).rearrange("p (e w) -> p e w", w=RAW)
        g_q = gtake(EC)
        g_mask = gtake(EC)
        g_scan = gtake(EC)
        g_acc = gtake(EC)
        g_pos = gtake(EC, I32)
        g_ones = gtake(EC)
        g_cnt = gtake(NT)
        g_tot = gtake(NT)
        g_off = gtake(NT)
        g_int = gtake(NT, I32)
        g_tri = gtake(P)
        g_fill = gtake(8 * 8, I32)
        g_stage = [gtake(8, I32) for _ in range(2)]
        g_spos = [gtake(2, I32)[:, 0:1] for _ in range(2)]
        g2 = scratch[:, 15616:].bitcast(I32)
        g_all = g2[0:G2, 0:GE * 8].rearrange("p (e w) -> p e w", w=8)
        g_attr2 = g2[0:G2, GE * 8:GE * 12].rearrange("p (e w) -> p e w", w=RAW)

        psum = ctx.enter_context(nc.psum_tensor("psum", [P, 8, 512], F32))

        def ps_h(k):
            return psum[:, 2 * k:2 * k + 2, :]

        def ps_v(k):
            return psum[:, 4 + k, :]

        ps_t = psum[:, 6, :].bitcast(F16)
        ps_a = psum[:, 7, :]

        class Sems:

            def __init__(self, prefix):
                self.prefix, self.made = prefix, {}

            def __call__(self, name):
                if name not in self.made:
                    self.made[name] = sem(f"{self.prefix}_{name}")
                return self.made[name]

        SU = Sems("setup")
        GS = Sems("general")
        Z = Sems("init")
        E1, E2 = Sems("edge"), Sems("edge2")
        ND = Sems("node")
        fenced = sem("fenced")
        phase = sem("phase")

        block = ctx.enter_context(nc.Block())

        def later(i):
            return not (isinstance(i, int) and i == 0)

        def fence(eng):
            eng.sem_inc(fenced, 1)

        def newton(dve, v, y, tmp, chain, base):
            n = [0]

            def done(i):
                i.then_inc(chain, 1)
                n[0] += 1
                dve.wait_ge(chain, base + n[0])

            done(dve.tensor_scalar(v, v, 1.0 / D, EPS, ALU.mult, ALU.add))
            done(dve.tensor_scalar(y.bitcast(I32), v.bitcast(I32), -0.5, RSQRT_SEED, ALU.mult, ALU.add))
            for _ in range(NEWTON):
                done(dve.tensor_tensor(tmp, y, y, ALU.mult))
                done(dve.scalar_tensor_tensor(tmp, tmp, -0.5, v, ALU.mult, ALU.mult))
                done(dve.scalar_tensor_tensor(y, tmp, 1.5, y, ALU.add, ALU.mult))
            assert n[0] == NEWTON_OPS

        def setup_sp(sp):
            def load(dst, src, name="w"):
                sp.dma_start(dst, src).then_inc(SU(name), 16)

            sp.wait_ge(SU("pads"), 2)
            load(d_int[0:G1 - 1, :], dst_in[0:(G1 - 1) * GE].rearrange("(g e) -> g e", e=GE), "dst")
            load(d_int[G1 - 1:G1, 0:LAST], dst_in[(G1 - 1) * GE:E].rearrange("(g e) -> g e", g=1), "dst")
            load(s_int[0:G1 - 1, :], src_in[0:(G1 - 1) * GE].rearrange("(g e) -> g e", e=GE), "src")
            load(s_int[G1 - 1:G1, 0:LAST], src_in[(G1 - 1) * GE:E].rearrange("(g e) -> g e", g=1), "src")
            load(w_pq[:, 0, :], eW1[D:2 * D, :], "w")
            load(w_pq[:, 1, :], eW1[2 * D:3 * D, :], "w")
            load(tmpw[:, 0:H], eW1[0:D, :], "w")
            load(tmpv[:, 0:2 * D].rearrange("p (k f) -> p k f", k=2), eW2.rearrange("(k p) f -> p k f", k=2), "w")
            load(nw1[:, :, :], nW1.rearrange("(k p) f -> p k f", k=2), "w")
            load(nw2[:, :, :], nW2.rearrange("(k p) f -> p k f", k=2), "w")
            load(g_row[:, :], eg.partition_broadcast(P), "w")
            load(ng_row[:, :], ng.partition_broadcast(P), "w")
            load(nbeta_row[:, :], nbeta.partition_broadcast(P), "w")
            for k in range(2):
                load(nb1_col[:, k:k + 1], nb1[k * P:(k + 1) * P].rearrange("(p a) -> p a", a=1), "w")
            load(beta_col[:, :], ebeta.rearrange("(p a) -> p a", a=1), "w")
            load(p_bias32[:, :], eb1.rearrange("(a f) -> a f", a=1), "w")
            load(tmpv[0:1, 2 * D:3 * D], eb2.rearrange("(a f) -> a f", a=1), "w")
            load(tmpv[0:1, 3 * D:4 * D], nb2.rearrange("(a f) -> a f", a=1), "w")
            sp.wait_ge(SU("zeroed"), 1)
            for t in range(TPG):
                load(enc_bd[t * RAW:(t + 1) * RAW, t, :], enc_W, "w")
                load(enc_bd[TPG * RAW:TPG * RAW + 1, t, :], enc_b.rearrange("(a f) -> a f", a=1), "w")
            sp.dma_start(x_rows[0:N, :], x_in).then_inc(SU("xrows"), 16)
            sp.dma_start(x_rows[N:NPAD, :], zero[0:NPAD - N, 0:D]).then_inc(SU("xrows"), 16)
            sp.wait_ge(SU("xrows"), 32)
            sp.wait_ge(SU("flag"), 1)
            with sp.If(sp.value_load(flag[0:1, 0:1], min_val=0, max_val=1) > 0):
                general_sp(sp)
            with sp.Else():
                na = E * RAW
                sp.dma_start(attr_p[0:E, :].rearrange("e w -> (e w)").rearrange("(a b) -> a b", a=100),
                             attr_in.rearrange("e w -> (e w)").rearrange("(a b) -> a b", a=100)).then_inc(SU("attr"), 16)
                sp.dma_start(attr_p[E:G1 * GE, :].rearrange("e w -> (e w)").rearrange("(a b) -> a b", a=16),
                             zero[0:16, 0:(G1 * GE - E) * RAW // 16]).then_inc(SU("attr"), 16)
                sp.wait_ge(SU("attr"), 32)
            sp.wait_ge(SU("rel"), 1)
            sp.dma_start(rel_rows[:, :], rel16[0:G2, :]).then_inc(SU("relrow"), 16)
            sp.wait_ge(SU("relrow"), 16)
            sp.wait_ge(SU("cols"), 3)
            sp.wait_ge(SU("weights"), 1)
            sp.sem_inc(phase, 1)

        NW = 16 * (15 + 2 * TPG)

        def general_sp(sp):
            sp.dma_start(g_dst[0:EP, :], dst_in.rearrange("(p e) -> p e", p=EP)).then_inc(GS("in"), 16)
            sp.dma_start(g_src[0:EP, :], src_in.rearrange("(p e) -> p e", p=EP)).then_inc(GS("in"), 16)
            sp.dma_start(g_attr[0:EP, :, :], attr_in.rearrange("(p e) w -> p e w", p=EP).bitcast(I32)).then_inc(GS("in"), 16)
            sp.wait_ge(GS("fill"), 1)
            rows_a = records.rearrange("(a b) w -> a (b w)", b=8)
            for a in range(0, G2 * GE // 8, P):
                n = min(P, G2 * GE // 8 - a)
                sp.dma_start(rows_a[a:a + n, :], g_fill[0:n, :]).then_inc(GS("filled"), 16)
            sp.wait_ge(GS("filled"), 16 * len(range(0, G2 * GE // 8, P)))
            sp.sem_inc(GS("ready"), 1)
            sp.wait_ge(GS("sorted"), 1)
            sp.dma_start(g_all, records.rearrange("(g e) w -> g e w", e=GE)).then_inc(GS("back"), 16)
            sp.wait_ge(GS("attr"), 1)
            sp.dma_start(attr_p.rearrange("(g e) w -> g e w", e=GE).bitcast(I32), g_attr2).then_inc(GS("attr_out"), 16)
            sp.wait_ge(GS("attr_out"), 16)

        def setup_pool(pool):
            pool.memset(d_int[:, :], 1 << 20).then_inc(SU("pads"), 1)
            pool.memset(s_int[:, :], 0).then_inc(SU("pads"), 1)
            pool.memset(enc_bd[:, :, :], 0.0).then_inc(SU("zeroed"), 1)
            pool.memset(ones16[:, :], 1.0).then_inc(SU("const"), 1)
            pool.memset(ident32[:, :], 0.0).then_inc(SU("ident"), 1)
            pool.iota(part_iota[:, :], pattern=[[0, 1]], base=0, channel_multiplier=1,
                      allow_small_or_imprecise_dtypes=True).then_inc(SU("const"), 1)
            pool.iota(node_iota[:, :], pattern=[[1, P]], base=0, channel_multiplier=0,
                      allow_small_or_imprecise_dtypes=True).then_inc(SU("const"), 1)
            pool.wait_ge(SU("ident"), 1)
            pool.affine_select(out=ident32[:, :], in_=ident32[:, :], compare_op=ALU.not_equal, fill=1.0,
                               base=0, pattern=[[-1, P]], channel_multiplier=1).then_inc(SU("ident"), 1)
            pool.wait_ge(SU("flag"), 1)
            with pool.If(pool.value_load(flag[0:1, 0:1], min_val=0, max_val=1) > 0):
                general_pool(pool)
            with pool.Else():
                pool.nop()

        def general_pool(pool):
            pool.memset(g_tri[:, :], 1.0).then_inc(GS("tri"), 1)
            pool.wait_ge(GS("tri"), 1)
            pool.affine_select(out=g_tri[:, :], in_=g_tri[:, :], compare_op=ALU.is_ge, fill=0.0,
                               base=-1, pattern=[[1, P]], channel_multiplier=-1).then_inc(GS("tri"), 1)
            pool.wait_ge(GS("pos"), 1)
            pool.wait_ge(GS("ready"), 1)
            def column_pair(j):
                for k in range(2):
                    if later(j):
                        pool.wait_ge(GS(f"put{k}"), 16 * j)
                    pool.tensor_copy(g_stage[k], g_rec[:, ds(2 * j + k, 1), :].rearrange("p a w -> p (a w)")).then_inc(GS("staged"), 1)
                    pool.tensor_copy(g_spos[k], g_pos[:, ds(2 * j + k, 1)]).then_inc(GS("staged"), 1)
                    pool.wait_ge(GS("staged"), 4 * j + 2 * k + 2)
                    fence(pool)
                    pool.indirect_dma_start(out=records, out_offset=bass.IndirectOffsetOnAxis(ap=g_spos[k][0:EP, :], axis=0),
                                            in_=g_stage[k][0:EP, :], in_offset=None).then_inc(GS(f"put{k}"), 16)

            column_pair(0)
            with pool.Fori(1, EC // 2) as j:
                column_pair(j)
            for k in range(2):
                pool.wait_ge(GS(f"put{k}"), 16 * (EC // 2))
            pool.sem_inc(GS("sorted"), 1)

        def setup_dve(dve):
            chain = SU("dve")
            n = [0]

            def done(i):
                i.then_inc(chain, 1)
                n[0] += 1
                dve.wait_ge(chain, n[0])

            done(dve.memset(red, 0.0))
            dve.memset(zero, 0.0).then_inc(SU("dvezero"), 1)
            done(dve.memset(p_bias[:, :], 0.0))
            done(dve.memset(v_bias[:, :], 0.0))
            done(dve.memset(u_bias[:, :], 0.0))
            done(dve.memset(agg[:, :], 0.0))
            done(dve.memset(rel_all[:, :, :], 0.0))
            done(dve.memset(beta_sum[:, :], 0.0))
            dve.wait_ge(SU("dst"), 32)
            dve.wait_ge(SU("ident"), 2)
            done(dve.tensor_copy(ident16[:, :], ident32[:, :]))
            done(dve.tensor_copy(d_grp, d_int))
            done(dve.tensor_reduce(red[:, 0:1], d_grp, AX.X, ALU.min))
            done(dve.tensor_scalar(red[:, 0:1], red[:, 0:1], float(N - P), None, ALU.min))
            done(dve.tensor_reduce(red[0:G1, 1:2], d_grp[0:G1, 0:LAST], AX.X, ALU.max))
            done(dve.tensor_reduce(red[0:G1 - 1, 2:3], d_grp[0:G1 - 1, LAST:GE], AX.X, ALU.max))
            done(dve.tensor_tensor(red[0:G1, 1:2], red[0:G1, 1:2], red[0:G1, 2:3], ALU.max))
            done(dve.tensor_tensor(red[0:G1, 3:4], red[0:G1, 1:2], red[0:G1, 0:1], ALU.subtract))
            dve.sem_inc(SU("width"), 1)
            dve.wait_ge(SU("widthT"), 1)
            done(dve.tensor_reduce(red[0:1, 4:5], psum[0:1, 0, 0:G1], AX.X, ALU.max))
            dve.tensor_scalar(flag[0:1, 0:1], red[0:1, 4:5], float(P - 1), None, ALU.is_gt).then_inc(SU("flag"), 1)
            dve.wait_ge(SU("flag"), 1)
            dve.wait_ge(SU("w"), NW)
            done(dve.tensor_copy(w1_hi[:, :], tmpw[:, 0:H]))
            done(dve.tensor_tensor(w1_lo[:, :], tmpw[:, 0:H], w1_hi[:, :], ALU.subtract))
            w2 = tmpv[:, 0:2 * D].rearrange("p (k f) -> p k f", k=2)

            def centre(w, cols):
                done(dve.tensor_reduce(cols, w, AX.X, ALU.add))
                done(dve.tensor_scalar(cols, cols, -1.0 / D, None, ALU.mult))

            centre(w2, red[:, 5:7])
            for k in range(2):
                done(dve.tensor_scalar(w2[:, k, :], w2[:, k, :], red[:, 5 + k:6 + k], None, ALU.add))
            done(dve.tensor_copy(w2_hi[:, :, :], w2))
            done(dve.tensor_tensor(w2_lo[:, :, :], w2, w2_hi[:, :, :], ALU.subtract))
            centre(nw2[:, :, :], red[:, 7:9])
            for k in range(2):
                done(dve.tensor_scalar(nw2[:, k, :], nw2[:, k, :], red[:, 7 + k:8 + k], None, ALU.add))
            for row, bias, reps in ((2, v_bias, TPG), (3, u_bias, 1)):
                b = tmpv[0:1, row * D:(row + 1) * D]
                centre(b, red[0:1, 9:10])
                done(dve.tensor_scalar(b, b, red[0:1, 9:10], None, ALU.add))
                for r in range(reps):
                    done(dve.tensor_copy(bias[0:1, r * D:(r + 1) * D], b))
                for r in range(reps):
                    done(dve.tensor_tensor(d_row[0:1, 0:D], b, bias[0:1, 0:D], ALU.subtract))
                    done(dve.tensor_copy(bias[32:33, r * D:(r + 1) * D], d_row[0:1, 0:D]))
            dve.wait_ge(SU("betaw"), 1)
            done(dve.tensor_copy(beta_w1[:, :], psum[0:1, 1, 0:H]))
            pair_p_bias(done, dve)
            dve.sem_inc(SU("weights"), 1)
            with dve.If(dve.value_load(flag[0:1, 0:1], min_val=0, max_val=1) > 0):
                general_dve(dve)
            with dve.Else():
                dve.nop()
            c2 = SU("dve2")
            m = [0]

            def done2(i):
                i.then_inc(c2, 1)
                m[0] += 1
                dve.wait_ge(c2, m[0])

            dve.wait_ge(SU("src"), 32)
            done2(dve.tensor_copy(d_grp, d_int))
            done2(dve.tensor_copy(s_grp, s_int))
            done2(dve.tensor_reduce(red[:, 0:1], d_grp, AX.X, ALU.min))
            done2(dve.tensor_scalar(red[:, 0:1], red[:, 0:1], float(N - P), None, ALU.min))
            done2(dve.tensor_scalar(d_grp, d_grp, red[:, 0:1], 255.0, ALU.subtract, ALU.min))
            dve.tensor_copy(rel16.rearrange("g (t p) -> g t p", t=TPG),
                            d_grp.rearrange("g (p t) -> g t p", t=TPG)).then_inc(SU("rel"), 1)
            dve.sem_inc(SU("grp"), 1)
            dve.wait_ge(SU("relT"), 1)
            dve.tensor_copy(rel_all[:, :, 0:G2], psum[:, 2, :].rearrange("p (t g) -> p t g", t=TPG)[:, :, 0:G2]).then_inc(SU("cols"), 1)
            dve.wait_ge(SU("srcT"), 1)
            dve.tensor_copy(idx_all[:, :, :].rearrange("p g t -> p t g"),
                            psum[:, 3, :].rearrange("p (t g) -> p t g", t=TPG)[:, :, 0:G2]).then_inc(SU("cols"), 1)
            dve.wait_ge(SU("winT"), 1)
            dve.tensor_copy(win[0:1, 0:G2], psum[0:1, 0, 128:128 + G2]).then_inc(SU("cols"), 1)

        d_row = sb("d_row", [1, H], F32)

        def pair_p_bias(done, dve):
            done(dve.tensor_copy(p_bias[0:1, :], p_bias32[:, :]))
            done(dve.tensor_tensor(d_row[:, :], p_bias32[:, :], p_bias[0:1, :], ALU.subtract))
            done(dve.tensor_copy(p_bias[32:33, :], d_row[:, :]))

        def general_dve(dve):
            c = GS("dve")
            n = [0]

            def done(i):
                i.then_inc(c, 1)
                n[0] += 1
                dve.wait_ge(c, n[0])

            fill = g_fill.rearrange("p (e w) -> p e w", w=8)
            done(dve.memset(fill, 0))
            dve.memset(fill[:, :, 1:2], 1 << 20).then_inc(GS("fill"), 1)
            done(dve.memset(g_rec, 0))
            done(dve.memset(g_pos, 0))
            done(dve.memset(g_ones, 1.0))
            done(dve.memset(g_acc, 0.0))
            dve.wait_ge(GS("in"), 48)
            done(dve.tensor_copy(g_rec[0:EP, :, 0:1].rearrange("p e w -> p (e w)"), g_src[0:EP, :]))
            done(dve.tensor_copy(g_rec[0:EP, :, 1:2].rearrange("p e w -> p (e w)"), g_dst[0:EP, :]))
            done(dve.tensor_copy(g_rec[0:EP, :, 2:2 + RAW], g_attr[0:EP, :, :]))
            done(dve.tensor_scalar(g_dst[0:EP, :], g_dst[0:EP, :], 7, None, ALU.logical_shift_right))
            done(dve.tensor_copy(g_q[0:EP, :], g_dst[0:EP, :]))
            for b in range(NT):
                done(dve.tensor_scalar(g_mask[0:EP, :], g_q[0:EP, :], float(b), None, ALU.is_equal))
                done(dve.tensor_tensor_scan(g_scan[0:EP, :], g_ones[0:EP, :], g_mask[0:EP, :], 0.0, ALU.mult, ALU.add))
                done(dve.tensor_copy(g_cnt[0:EP, b:b + 1], g_scan[0:EP, EC - 1:EC]))
                done(dve.tensor_tensor(g_scan[0:EP, :], g_scan[0:EP, :], g_mask[0:EP, :], ALU.mult))
                done(dve.tensor_tensor(g_acc[0:EP, :], g_acc[0:EP, :], g_scan[0:EP, :], ALU.add))
            dve.sem_inc(GS("counts"), 1)
            dve.wait_ge(GS("sums"), 1)
            done(dve.tensor_scalar(g_tot[0:EP, :], psum[0:EP, 1, 0:NT], float(GE - 1), None, ALU.add))
            done(dve.tensor_copy(g_int[0:EP, :], g_tot[0:EP, :]))
            done(dve.tensor_scalar(g_int[0:EP, :], g_int[0:EP, :], 9, 9, ALU.logical_shift_right, ALU.logical_shift_left))
            done(dve.tensor_copy(g_tot[0:EP, :], g_int[0:EP, :]))
            done(dve.tensor_tensor_scan(g_off[0:EP, :], g_ones[0:EP, 0:NT], g_tot[0:EP, :], 0.0, ALU.mult, ALU.add))
            done(dve.tensor_tensor(g_off[0:EP, :], g_off[0:EP, :], g_tot[0:EP, :], ALU.subtract))
            done(dve.tensor_tensor(g_off[0:EP, :], g_off[0:EP, :], psum[0:EP, 0, 0:NT], ALU.add))
            for b in range(NT):
                done(dve.tensor_scalar(g_mask[0:EP, :], g_q[0:EP, :], float(b), g_off[0:EP, b:b + 1], ALU.is_equal, ALU.mult))
                done(dve.tensor_tensor(g_acc[0:EP, :], g_acc[0:EP, :], g_mask[0:EP, :], ALU.add))
            dve.tensor_scalar(g_pos[0:EP, :], g_acc[0:EP, :], -1.0, None, ALU.add).then_inc(GS("pos"), 1)
            dve.wait_ge(GS("back"), 16)
            dve.tensor_copy(g_attr2, g_all[:, :, 2:2 + RAW]).then_inc(GS("attr"), 1)
            done(dve.tensor_copy(d_int[0:G2, :], g_all[:, :, 1:2].rearrange("p e w -> p (e w)")))
            done(dve.tensor_copy(s_int[0:G2, :], g_all[:, :, 0:1].rearrange("p e w -> p (e w)")))

        def setup_pe(pe):
            pe.wait_ge(SU("ident"), 2)
            pe.wait_ge(SU("width"), 1)
            pe.transpose(psum[0:1, 0, 0:P], red[:, 3:4], ident32[:, :]).then_inc(SU("widthT"), 1)
            pe.wait_ge(SU("w"), NW)
            pe.matmul(psum[0:1, 1, 0:H], beta_col[:, :], tmpw[:, 0:H], start=True, stop=True).then_inc(SU("betaw"), 1)
            pe.wait_ge(SU("flag"), 1)
            with pe.If(pe.value_load(flag[0:1, 0:1], min_val=0, max_val=1) > 0):
                pe.wait_ge(GS("counts"), 1)
                pe.wait_ge(GS("tri"), 2)
                pe.matmul(psum[:, 0, 0:NT], g_tri[0:EP, :], g_cnt[0:EP, :], start=True, stop=True)
                pe.matmul(psum[0:EP, 1, 0:NT], g_ones[0:EP, 0:EP], g_cnt[0:EP, :], start=True, stop=True).then_inc(GS("sums"), 1)
            with pe.Else():
                pe.nop()
            pe.wait_ge(SU("grp"), 1)
            for t in range(TPG):
                i = pe.transpose(psum[:, 2, t * P:(t + 1) * P], d_grp.rearrange("g (p t) -> g t p", t=TPG)[:, t, :], ident32[:, :])
            i.then_inc(SU("relT"), 1)
            for t in range(TPG):
                i = pe.transpose(psum[:, 3, t * P:(t + 1) * P], s_grp.rearrange("g (p t) -> g t p", t=TPG)[:, t, :], ident32[:, :])
            i.then_inc(SU("srcT"), 1)
            pe.transpose(psum[0:1, 0, P:2 * P], red[:, 0:1], ident32[:, :]).then_inc(SU("winT"), 1)

        class Init:

            def __init__(self, S, first, last):
                self.S, self.first, self.last = S, first // 2, last // 2

            def loop(self, eng, body):
                for k in range(2):
                    body(eng, self.first, k)
                with eng.Fori(self.first + 1, self.last) as q:
                    for k in range(2):
                        body(eng, q, k)

            def sp(self, sp):
                S = self.S

                def load(q, k):
                    g = 2 * q + k
                    if later(q):
                        sp.wait_ge(S("atT"), 2 * q)
                        fence(sp)
                    sp.dma_start(at_in[k][:, 0:TPG * RAW],
                                 attr_p.rearrange("(g p t) w -> g p (t w)", p=P, t=TPG)[ds(g, 1), :, :].rearrange("a p w -> (a p) w")).then_inc(S(f"at{k}"), 16)
                    if later(q):
                        sp.wait_ge(S("oht"), 2 * q)
                        fence(sp)
                    sp.dma_start(rel_b[k], rel_rows[ds(g, 1), :].rearrange("a e -> (a e)").partition_broadcast(P)).then_inc(S(f"rb{k}"), 16)

                def store(q, k):
                    g = 2 * q + k
                    sp.wait_ge(S("oht"), 2 * q + k + 1)
                    sp.wait_ge(S("oh"), 2 * q + k + 1)
                    fence(sp)
                    for m01, here in ((onehot, oh0), (onehot_t, oht0)):
                        sp.dma_start(m01[ds(g, 1), :, :].rearrange("a p c -> (a p) c"), here[k].bitcast(F32)).then_inc(S(f"oh{k}"), 16)
                    sp.wait_ge(S("lo"), 2 * q + k + 1)
                    fence(sp)
                    sp.dma_start(state[ds(g, 1), :, :].rearrange("a p c -> (a p) c"), st0[k].rearrange("p t c -> p (t c)")).then_inc(S(f"st{k}"), 16)

                for k in range(2):
                    load(self.first, k)
                with sp.Fori(self.first + 1, self.last) as q:
                    for k in range(2):
                        load(q, k)
                    for k in range(2):
                        store(q - 1, k)
                for k in range(2):
                    store(self.last - 1, k)
                for k in range(2):
                    sp.wait_ge(S(f"st{k}"), 16 * self.last)
                    sp.wait_ge(S(f"oh{k}"), 32 * self.last)
                sp.wait_ge(S("deg"), 2 * self.last)

            def pe(self, pe):
                S = self.S

                def body(pe, q, k):
                    m = 2 * q + k
                    pe.wait_ge(S(f"at{k}"), 16 * q + 16)
                    if later(q):
                        pe.wait_ge(S("atc"), m - k)
                    pe.transpose(psum[0:TPG * RAW + 1, k, 0:P], at_in[k], ident32[:, :]).then_inc(S("atT"), 1)
                    pe.wait_ge(S("atc"), m + 1)
                    if later(q):
                        pe.wait_ge(S("enc"), m - k)
                    pe.matmul(psum[:, 2 + k, :], atT[k][0:TPG * RAW + 1, :], enc_bd[:, :, :].rearrange("a t f -> a (t f)"),
                              start=True, stop=True).then_inc(S("encm"), 1)
                    pe.wait_ge(S("oh"), m + 1)
                    if later(q):
                        pe.wait_ge(S("deg"), m - k)
                    fence(pe)
                    for t in range(TPG):
                        i = pe.matmul(psum[:, 4 + k, 0:P], ones16[:, :], oh0[k][:, t * P:(t + 1) * P],
                                      start=t == 0, stop=t == TPG - 1)
                    i.then_inc(S("degm"), 1)

                pe.wait_ge(S("one"), 2)
                self.loop(pe, body)

            def act(self, act):
                S = self.S

                def body(act, q, k):
                    m = 2 * q + k
                    act.wait_ge(S("atT"), m + 1)
                    if later(q):
                        act.wait_ge(S("encm"), m - k)
                    act.copy(atT[k][0:TPG * RAW + 1, :], psum[0:TPG * RAW + 1, k, 0:P]).then_inc(S("atc"), 1)
                    act.wait_ge(S("encm"), m + 1)
                    if later(q):
                        act.wait_ge(S("lo"), m - k)
                    act.activation(e0[k], psum[:, 2 + k, :], ACT.Silu).then_inc(S("enc"), 1)
                    act.wait_ge(S("enc"), m + 1)
                    if later(q):
                        act.wait_ge(S(f"st{k}"), 16 * q)
                    act.copy(st0[k][:, :, 0:D], e0[k].rearrange("p (t f) -> p t f", t=TPG)).then_inc(S("hi"), 1)

                self.loop(act, body)

            def dve(self, dve):
                S = self.S

                def body(dve, q, k):
                    m = 2 * q + k
                    dve.tensor_copy(rel_now[k], rel_all[:, :, ds(m, 1)].rearrange("p t a -> p (t a)")).then_inc(S("rel"), 1)
                    if later(q):
                        dve.wait_ge(S(f"oh{k}"), 32 * q)
                        dve.wait_ge(S("degm"), 2 * q)
                    dve.wait_ge(S("rel"), m + 1)
                    fence(dve)
                    for t in range(TPG):
                        i = dve.tensor_scalar(oh0[k][:, t * P:(t + 1) * P], node_iota[:, :], rel_now[k][:, t:t + 1],
                                              None, ALU.is_equal, saturate=False)
                    i.then_inc(S("oh"), 1)
                    dve.wait_ge(S(f"rb{k}"), 16 * q + 16)
                    fence(dve)
                    dve.tensor_scalar(oht0[k], rel_b[k], part_iota[:, :], None,
                                      ALU.is_equal, saturate=False).then_inc(S("oht"), 1)
                    dve.wait_ge(S("hi"), m + 1)
                    dve.tensor_tensor(st0[k][:, :, D:2 * D], e0[k].rearrange("p (t f) -> p t f", t=TPG),
                                      st0[k][:, :, 0:D], ALU.subtract).then_inc(S("lo"), 1)
                    dve.wait_ge(S("degm"), m + 1)
                    if later(m):
                        dve.wait_ge(S("deg"), m)
                    fence(dve)
                    w = dve.value_load(win[0:1, ds(m, 1)], min_val=0, max_val=N - P)
                    dve.tensor_tensor(agg[:, ds(w, P)], agg[:, ds(w, P)], psum[:, 4 + k, 0:P], ALU.add).then_inc(S("deg"), 1)

                if self.first == 0:
                    for k in range(2):
                        dve.memset(at_in[k][:, TPG * RAW:TPG * RAW + 1], 1.0).then_inc(S("one"), 1)
                self.loop(dve, body)

        I1, I2 = Init(Z, 0, G1), Init(Z, G1, G2)

        class Edge:

            def __init__(self, S, g0, n):
                self.S, self.g0, self.n = S, g0, n
                assert n % 2 == 0

            def loop(self, eng, body, pairs):
                first, last = FIRST, self.n // 2
                for i in range(first):
                    body(i)
                with eng.Fori(first, last) as i:
                    body(i)
                for i in range(last, pairs):
                    body(i)

            def has(self, m, lo=0):
                return not isinstance(m, int) or lo <= m < self.n

            def sp(self, sp, s):
                S, n = self.S, self.n
                c = lambda m: s * n + m
                cp = lambda i: s * (n // 2) + i

                def load(m, k):
                    g = m + self.g0
                    if self.has(m - 2):
                        sp.wait_ge(S("resid"), c(m) - 1)
                        sp.wait_ge(S("transposed"), c(m) - 1)
                        sp.wait_ge(S("h"), c(m) - 1)
                        fence(sp)
                    sp.dma_start(st_in[k].rearrange("p t c -> p (t c)"), state[ds(g, 1), :, :].rearrange("a p c -> (a p) c")).then_inc(S(f"st{k}"), 16)
                    w = sp.value_load(win[0:1, ds(g, 1)], min_val=0, max_val=N - P)
                    sp.dma_start(q_win[k], q_table[ds(w, P), :]).then_inc(S(f"q{k}"), 16)
                    sp.dma_start(oht[k].bitcast(F32), onehot_t[ds(g, 1), :, :].rearrange("a p c -> (a p) c")).then_inc(S(f"q{k}"), 16)

                def store(m, k):
                    sp.wait_ge(S("el"), c(m) + 1)
                    fence(sp)
                    sp.dma_start(state[ds(m + self.g0, 1), :, :].rearrange("a p c -> (a p) c"),
                                 st_out[k].rearrange("p t c -> p (t c)")).then_inc(S(f"out{k}"), 16)

                def load_sum(m, k):
                    if self.has(m - 2):
                        sp.wait_ge(S("sum"), c(m) - 1)
                        fence(sp)
                    sp.dma_start(oh[k].bitcast(F32), onehot[ds(m + self.g0, 1), :, :].rearrange("a p c -> (a p) c")).then_inc(S(f"oh{k}"), 16)

                load(0, 0)
                load(1, 1)

                def body(i):
                    for k in range(2):
                        if self.has(2 * i + 2 + k):
                            load(2 * i + 2 + k, k)
                        if self.has(2 * i - 2 + k):
                            load_sum(2 * i - 2 + k, k)
                            store(2 * i - 2 + k, k)

                first, last = FIRST, n // 2 - 1
                for i in range(first):
                    body(i)
                with sp.Fori(first, last) as i:
                    body(i)
                for i in range(last, n // 2 + 1):
                    body(i)
                for k in range(2):
                    sp.wait_ge(S(f"out{k}"), 16 * cp(n // 2))
                sp.wait_ge(S("added"), c(n))
                fence(sp)

            def pool(self, pool, s):
                S, n = self.S, self.n
                c = lambda m: s * n + m

                def body(i):
                    for k in range(2):
                        m = 2 * i + k
                        if self.has(m - 2):
                            pool.wait_ge(S("src"), c(m) - 1)
                            fence(pool)
                        pool.tensor_copy(idx_now[k], idx_all[:, ds(m + self.g0, 1), :].rearrange("p a t -> p (a t)")).then_inc(S("idx"), 1)
                        pool.wait_ge(S("idx"), c(m) + 1)
                        fence(pool)
                        for t in range(TPG):
                            pool.indirect_dma_start(
                                out=rows[k][:, t, :], out_offset=None, in_=p_table,
                                in_offset=bass.IndirectOffsetOnAxis(ap=idx_now[k][:, t:t + 1], axis=0),
                            ).then_inc(S(f"rows{k}"), 16)

                for i in range(2):
                    body(i)
                with pool.Fori(2, n // 2) as i:
                    body(i)

            def pe(self, pe, s):
                S, n = self.S, self.n
                c = lambda m: s * n + m
                cp = lambda i: s * (n // 2) + i

                def A(m, k, i):
                    if not self.has(m):
                        return
                    pe.wait_ge(S(f"st{k}"), 16 * cp(i) + 16)
                    if self.has(m - 1):
                        pe.wait_ge(S("eT"), c(m))
                    for p in range(2):
                        for t in range(TPG):
                            j = p * TPG + t
                            x = pe.transpose(ps_t[:, j * P:(j + 1) * P], st_in[k][:, t, p * D:(p + 1) * D], ident16[:, :])
                    x.then_inc(S("transposed"), 1)

                def B(m, k, i):
                    if not self.has(m):
                        return
                    pe.wait_ge(S(f"q{k}"), 32 * cp(i) + 32)
                    if self.has(m - 2):
                        pe.wait_ge(S("hh"), c(m) - 1)
                    fence(pe)
                    for half in range(2):
                        for p in range(2):
                            pe.matmul(ps_h(k)[:, half, :], q_win[k][:, p * H + half * D:p * H + half * D + D], oht[k],
                                      start=p == 0, stop=False, skip_group_check=True)
                    pe.wait_ge(S(f"rows{k}"), TPG * 16 * (cp(i) + 1))
                    for t in range(TPG):
                        for half in range(2):
                            for p in range(2):
                                x = pe.matmul(ps_h(k)[:, half, t * P:(t + 1) * P],
                                              rows[k][:, t, p * H + half * D:p * H + half * D + D], ident16[:, :],
                                              start=False, stop=False, skip_group_check=True)
                    x.then_inc(S("src"), 1)
                    pe.wait_ge(S("eT"), c(m) + 1)
                    for half in range(2):
                        cols = slice(half * D, (half + 1) * D)
                        for w, p in ((w1_hi, 0), (w1_hi, 1), (w1_lo, 0)):
                            x = pe.matmul(ps_h(k)[:, half, :], w[:, cols], eT[k][:, p, :],
                                          start=False, stop=w is w1_lo, skip_group_check=True)
                    x.then_inc(S("h"), 1)

                def C(m, k):
                    if not self.has(m):
                        return
                    if self.has(m - 2):
                        pe.wait_ge(S("scaled"), c(m) - 1)
                    pe.matmul(ps_v(k), ones16[0:64, :], v_bias[:, :], start=True, stop=False, skip_group_check=True)
                    pe.wait_ge(S("hl"), c(m) + 1)
                    for t in range(TPG):
                        for half in range(2):
                            for h, w in ((hh, w2_hi), (hh, w2_lo), (hl, w2_hi)):
                                x = pe.matmul(ps_v(k)[:, t * P:(t + 1) * P], h[k][:, half, t * P:(t + 1) * P], w[:, half, :],
                                              start=False, stop=half == 1 and h is hl, skip_group_check=True)
                    x.then_inc(S("v"), 1)

                def Dm(m, k, i):
                    if not self.has(m):
                        return
                    pe.wait_ge(S("el"), c(m) + 1)
                    if self.has(m - 1):
                        pe.wait_ge(S("added"), c(m))
                    pe.wait_ge(S(f"oh{k}"), 16 * cp(i) + 16)
                    fence(pe)
                    for t in range(TPG):
                        for p in range(2):
                            x = pe.matmul(ps_a[:, 0:P], st_out[k][:, t, p * D:(p + 1) * D], oh[k][:, t * P:(t + 1) * P],
                                          start=t == 0 and p == 0, stop=t == TPG - 1 and p == 1, skip_group_check=True)
                    x.then_inc(S("sum"), 1)

                A(0, 0, 0)

                def body(i):
                    B(2 * i, 0, i)
                    C(2 * i - 1, 1)
                    A(2 * i + 1, 1, i)
                    Dm(2 * i - 4, 0, i - 2)
                    B(2 * i + 1, 1, i)
                    C(2 * i, 0)
                    A(2 * i + 2, 0, i + 1)
                    Dm(2 * i - 3, 1, i - 2)

                first, last = FIRST, n // 2 - 1
                for i in range(first):
                    body(i)
                with pe.Fori(first, last) as i:
                    body(i)
                for i in range(last, n // 2 + 2):
                    body(i)

            def act(self, act, s):
                S, n = self.S, self.n
                c = lambda m: s * n + m

                def silu32(m, k):
                    if self.has(m):
                        act.wait_ge(S("h"), c(m) + 1)
                        if self.has(m - 2):
                            act.wait_ge(S("hl"), c(m) - 1)
                        act.activation(h32[k], ps_h(k), ACT.Silu).then_inc(S("h32"), 1)

                def silu16(m, k):
                    if self.has(m):
                        if self.has(m - 2):
                            act.wait_ge(S("v"), c(m) - 1)
                        act.activation(hh[k], ps_h(k), ACT.Silu).then_inc(S("hh"), 1)

                def evac(m, k):
                    if self.has(m):
                        act.wait_ge(S("transposed"), c(m) + 1)
                        if self.has(m - 2):
                            act.wait_ge(S("h"), c(m) - 1)
                        act.copy(eT[k].rearrange("p k e -> p (k e)"), ps_t[:, :]).then_inc(S("eT"), 1)

                def square(m, k):
                    if self.has(m):
                        act.wait_ge(S("v"), c(m) + 1)
                        if self.has(m - 1):
                            act.wait_ge(S("ssq"), c(m))
                        act.activation(sq, ps_v(k), ACT.Square).then_inc(S("sq"), 1)

                def cast(m, k):
                    if self.has(m):
                        act.wait_ge(S("new"), c(m) + 1)
                        if self.has(m - 2):
                            act.wait_ge(S("sum"), c(m) - 1)
                            act.wait_ge(S(f"out{k}"), 16 * (s * (n // 2) + i_of(m, k)))
                        act.copy(st_out[k][:, :, 0:D], e_new[k].rearrange("p (t f) -> p t f", t=TPG)).then_inc(S("eh"), 1)

                def i_of(m, k):
                    return m // 2 if isinstance(m, int) else cast_i[0]

                cast_i = [0]
                evac(0, 0)

                def body(i):
                    cast_i[0] = i - 1
                    silu32(2 * i, 0)
                    square(2 * i - 1, 1)
                    silu16(2 * i, 0)
                    evac(2 * i + 1, 1)
                    cast(2 * i - 2, 0)
                    silu32(2 * i + 1, 1)
                    square(2 * i, 0)
                    silu16(2 * i + 1, 1)
                    evac(2 * i + 2, 0)
                    cast(2 * i - 1, 1)

                first, last = FIRST, n // 2 - 1
                for i in range(first):
                    body(i)
                with act.Fori(first, last) as i:
                    body(i)
                for i in range(last, n // 2 + 1):
                    body(i)

            def dve(self, dve, s):
                S, n = self.S, self.n
                c = lambda m: s * n + m
                cp = lambda i: s * (n // 2) + i
                rs = ssq

                def low(m, k):
                    if self.has(m):
                        dve.wait_ge(S("h32"), c(m) + 1)
                        dve.wait_ge(S("hh"), c(m) + 1)
                        if self.has(m - 2):
                            dve.wait_ge(S("v"), c(m) - 1)
                        dve.tensor_tensor(hl[k], h32[k], hh[k], ALU.subtract).then_inc(S("hl"), 1)

                def sums(m, k):
                    if self.has(m):
                        dve.wait_ge(S("sq"), c(m) + 1)
                        dve.tensor_reduce(nv[:, 4 * k:4 * k + 4], sq.rearrange("p (t f) -> p t f", t=TPG), AX.X, ALU.add).then_inc(S("ssq"), 1)

                def scale(m, k, first):
                    if self.has(m):
                        if self.has(m - 2):
                            dve.wait_ge(S("el"), c(m) - 1)
                        for t in range(TPG):
                            x = dve.scalar_tensor_tensor(e_new[k][:, t * P:(t + 1) * P], ps_v(k)[:, t * P:(t + 1) * P],
                                                         rs[:, 4 * k + t:4 * k + t + 1], g_row[:, :], ALU.mult, ALU.mult)
                        x.then_inc(S("scaled"), 1)

                def add_new(m, k):
                    if self.has(m):
                        dve.wait_ge(S("scaled"), c(m) + 1)
                        dve.wait_ge(S("resid"), c(m) + 1)
                        dve.tensor_tensor(e_new[k], e_new[k], resid[k], ALU.add).then_inc(S("new"), 1)

                def residual(m, k, i):
                    if self.has(m):
                        dve.wait_ge(S(f"st{k}"), 16 * cp(i) + 16)
                        if self.has(m - 2):
                            dve.wait_ge(S("new"), c(m) - 1)
                        dve.tensor_tensor(resid[k].rearrange("p (t f) -> p t f", t=TPG), st_in[k][:, :, 0:D],
                                          st_in[k][:, :, D:2 * D], ALU.add).then_inc(S("resid"), 1)

                def low_new(m, k):
                    if self.has(m):
                        dve.wait_ge(S("eh"), c(m) + 1)
                        dve.tensor_tensor(st_out[k][:, :, D:2 * D], e_new[k].rearrange("p (t f) -> p t f", t=TPG),
                                          st_out[k][:, :, 0:D], ALU.subtract).then_inc(S("el"), 1)

                def add_window(m, k):
                    if self.has(m):
                        dve.wait_ge(S("sum"), c(m) + 1)
                        if self.has(m - 1):
                            dve.wait_ge(S("added"), c(m))
                        fence(dve)
                        w = dve.value_load(win[0:1, ds(m + self.g0, 1)], min_val=0, max_val=N - P)
                        dve.tensor_tensor(agg[:, ds(w, P)], agg[:, ds(w, P)], ps_a[:, 0:P], ALU.add).then_inc(S("added"), 1)

                def body(i):
                    sums(2 * i - 1, 1)
                    if self.has(2 * i - 2):
                        dve.wait_ge(S("ssq"), c(2 * i))
                        if self.has(2 * i - 4):
                            dve.wait_ge(S("scaled"), c(2 * i) - 2)
                        newton(dve, nv, rs, nt, S("newton"), NEWTON_OPS * cp(i - 1))
                    low(2 * i, 0)
                    scale(2 * i - 2, 0, True)
                    add_new(2 * i - 2, 0)
                    residual(2 * i, 0, i)
                    add_window(2 * i - 4, 0)
                    low_new(2 * i - 2, 0)
                    low(2 * i + 1, 1)
                    scale(2 * i - 1, 1, False)
                    add_new(2 * i - 1, 1)
                    residual(2 * i + 1, 1, i)
                    add_window(2 * i - 3, 1)
                    sums(2 * i, 0)
                    low_new(2 * i - 1, 1)

                self.loop(dve, body, self.n // 2 + 2)

        S1, S2 = Edge(E1, 0, G1), Edge(E2, G1, G2 - G1)

        HW_ = CW // 2

        def ps_n(hf, m):
            return psum[:, 2 * hf + m, 0:HW_]

        def ps_u(t):
            return psum[:, 4 + t // 4, (t % 4) * P:(t % 4) * P + P]

        def ps_x(t):
            return psum[:, t % 2, 0:P]

        def ps_p(t):
            return psum[:, 6 + t % 2, :]

        def rows_of(ap, c):
            return ap[ds(c * CW, CW), :].rearrange("(t p) f -> p t f", p=P)

        class Node:

            def __init__(self, S, update, tables, final):
                self.S, self.update, self.tables, self.final = S, update, tables, final
                self.before = NCH if update else 0

            def sp(self, sp, s):
                S = self.S

                def chunk(c):
                    a = s * NCH + c
                    b = a + self.before
                    if self.update:
                        if later(c):
                            sp.wait_ge(S("hid"), 2 * a)
                            fence(sp)
                        sp.dma_start(xTc, x_cols[:, ds(c * CW, CW)]).then_inc(S("ldT"), 16)
                    if later(c):
                        sp.wait_ge(S("xT") if self.tables else S("fin"), CH * b if self.tables else c)
                        fence(sp)
                        sp.wait_ge(S("xst"), 16 * b)
                        fence(sp)
                    sp.dma_start(xc, rows_of(x_rows, c)).then_inc(S("ld"), 16)
                    if self.final:
                        sp.dma_start(x0c[:, 0:CH, :], rows_of(x0_rows, c)).then_inc(S("ld0"), 16)
                        sp.wait_ge(S("fin"), c + 1)
                        fence(sp)
                        sp.dma_start(rows_of(out_pad, c), xc).then_inc(S("xst"), 16)
                    elif self.update:
                        sp.wait_ge(S("xn"), a + 1)
                        fence(sp)
                        sp.dma_start(rows_of(x_rows, c), xc).then_inc(S("xst"), 16)
                    else:
                        sp.sem_inc(S("xst"), 16)
                    if self.tables:
                        for t in range(CH):
                            sp.wait_ge(S("plo"), CH * b + t + 1)
                            fence(sp)
                            for k, table in ((0, p_table), (1, q_table)):
                                sp.dma_start(table[ds(c * CW + t * P, P), :].rearrange("n (s e) -> n s e", s=2),
                                             pq[t % 2][:, :, k, :]).then_inc(S(f"tab{t % 2}"), 16)
                        sp.wait_ge(S("xT"), CH * b + CH)
                        fence(sp)
                        sp.dma_start(x_cols[:, ds(c * CW, CW)], xTn).then_inc(S("xTst"), 16)

                chunk(0)
                with sp.Fori(1, NCH) as c:
                    chunk(c)
                e = s * NCH + NCH + self.before
                sp.wait_ge(S("xst"), 16 * e)
                fence(sp)
                if self.tables:
                    sp.wait_ge(S("xTst"), 16 * e)
                    fence(sp)
                    sp.wait_ge(S("tab0"), 32 * 3 * e)
                    fence(sp)
                    sp.wait_ge(S("tab1"), 32 * 2 * e)
                fence(sp)

            def pe(self, pe, s):
                S = self.S

                def chunk(c):
                    a = s * NCH + c
                    b = a + self.before
                    if self.update:
                        pe.wait_ge(S("ldT"), 16 * a + 16)
                        for hf in range(2):
                            if later(c):
                                pe.wait_ge(S("act1"), 2 * a)
                            fence(pe)
                            for m in range(2):
                                for k in range(2):
                                    rhs = agg[:, ds(c * CW + hf * HW_, HW_)] if k else xTc[:, hf * HW_:(hf + 1) * HW_]
                                    x = pe.matmul(ps_n(hf, m), nw1[:, k, m * P:(m + 1) * P], rhs, start=k == 0, stop=k == 1)
                            x.then_inc(S("hid"), 1)
                        if later(c):
                            pe.wait_ge(S("xn"), a)
                        for t in range(CH):
                            pe.wait_ge(S("act1"), 2 * a + (1 if t < 2 else 2))
                            pe.matmul(ps_u(t), ones16[0:64, :], u_bias[:, :], start=True, stop=False, skip_group_check=True)
                            for k in range(2):
                                x = pe.matmul(ps_u(t), hN[:, k, t * P:(t + 1) * P], nw2[:, k, :], start=False, stop=k == 1,
                                              skip_group_check=True)
                            x.then_inc(S("u"), 1)
                    if self.tables:
                        if self.update:
                            pe.wait_ge(S("xn"), a + 1)
                        else:
                            pe.wait_ge(S("ld"), 16 * b + 16)

                        def turn(t):
                            if t >= 2:
                                pe.wait_ge(S("xT"), CH * b + t - 1)
                            elif later(c):
                                pe.wait_ge(S("xT"), CH * b)
                            pe.transpose(ps_x(t), xc[:, t, :], ident32[:, :]).then_inc(S("xTp"), 1)

                        turn(0)
                        for t in range(CH):
                            if t + 1 < CH:
                                turn(t + 1)
                            pe.wait_ge(S("xT"), CH * b + t + 1)
                            if t >= 2:
                                pe.wait_ge(S("plo"), CH * b + t - 1)
                            elif t == 0 and later(c):
                                pe.wait_ge(S("plo"), CH * b)
                            pe.matmul(ps_p(t), xTn[:, t * P:(t + 1) * P], w_pq[:, :, :].rearrange("p k h -> p (k h)"),
                                      start=True, stop=False, skip_group_check=True)
                            pe.matmul(ps_p(t)[:, 0:H], ones16[0:64, :], p_bias[:, :], start=False, stop=True,
                                      skip_group_check=True).then_inc(S("pq"), 1)

                chunk(0)
                with pe.Fori(1, NCH) as c:
                    chunk(c)

            def act(self, act, s):
                S = self.S

                def chunk(c):
                    a = s * NCH + c
                    b = a + self.before
                    if self.update:
                        if later(c):
                            act.wait_ge(S("u"), CH * a)
                        for hf in range(2):
                            act.wait_ge(S("hid"), 2 * a + hf + 1)
                            for m in range(2):
                                x = act.activation(hN[:, m, hf * HW_:(hf + 1) * HW_], ps_n(hf, m), ACT.Silu, bias=nb1_col[:, m:m + 1])
                            x.then_inc(S("act1"), 1)
                        if later(c):
                            act.wait_ge(S("xn"), a)
                        for t in range(CH):
                            act.wait_ge(S("u"), CH * a + max(t + 1, 4))
                            if t:
                                act.wait_ge(S("usq"), CH * a + t)
                            act.activation(sqn, ps_u(t), ACT.Square, accum_out=stn[:, t:t + 1]).then_inc(S("usq"), 1)
                    if self.tables:
                        if later(c):
                            act.wait_ge(S("xTst"), 16 * b)
                        for t in range(CH):
                            act.wait_ge(S("xTp"), CH * b + t + 1)
                            act.copy(xTn[:, t * P:(t + 1) * P], ps_x(t)).then_inc(S("xT"), 1)
                            if t:
                                self.hi(act, c, b, t - 1)
                        self.hi(act, c, b, CH - 1)

                chunk(0)
                with act.Fori(1, NCH) as c:
                    chunk(c)

            def hi(self, act, c, b, t):
                S = self.S
                act.wait_ge(S("pq"), CH * b + t + 1)
                if later(c) or t >= 2:
                    act.wait_ge(S(f"tab{t % 2}"), 32 * ((3 if t % 2 == 0 else 2) * b + t // 2))
                act.copy(pq[t % 2][:, 0, :, :], ps_p(t).rearrange("p (k h) -> p k h", k=2)).then_inc(S("phi"), 1)

            def dve(self, dve, s):
                S = self.S

                def chunk(c):
                    a = s * NCH + c
                    b = a + self.before
                    if self.update:
                        dve.wait_ge(S("usq"), CH * a + CH)
                        newton(dve, stn[:, 0:CH], nvn[:, 0:CH], ntn[:, 0:CH], S("newton"), NEWTON_OPS * a)
                        for t in range(CH):
                            x = dve.scalar_tensor_tensor(un[:, t, :], ps_u(t), nvn[:, t:t + 1], ng_row[:, :], ALU.mult, ALU.mult)
                        x.then_inc(S(self.cname), 1)
                        dve.wait_ge(S("ld"), 16 * b + 16)
                        nbeta_all = nbeta_row[:, :].unsqueeze(1).to_broadcast([P, CH, D])
                        base = self.dve_ops() * (c if self.final else a)
                        dve.wait_ge(S(self.cname), base + 1)
                        dve.tensor_tensor(un, un, nbeta_all, ALU.add).then_inc(S(self.cname), 1)
                        dve.wait_ge(S(self.cname), base + 2)
                        dve.tensor_tensor(xc, xc, un, ALU.add).then_inc(S("xn"), 1)
                    if self.final:
                        dve.wait_ge(S("xn"), a + 1)
                        dve.wait_ge(S("ld0"), 16 * c + 16)
                        n = [base + 2]

                        def done(i):
                            i.then_inc(S(self.cname), 1)
                            n[0] = n[0] + 1
                            dve.wait_ge(S(self.cname), n[0])
                            fence(dve)

                        done(dve.tensor_tensor(xc, xc, x0c, ALU.add))
                        for t in range(CH):
                            x = dve.bn_stats(bst[:, t, :], xc[:, t, :])
                        done(x)
                        for t in range(CH):
                            x = dve.bn_aggr(bag[:, t, :], bst[:, t, :])
                        done(x)
                        done(dve.tensor_scalar(stn[:, 0:CH], bag[:, :, 1:2].rearrange("p t s -> p (t s)"), float(D), None, ALU.mult))
                        newton(dve, stn[:, 0:CH], nvn[:, 0:CH], ntn[:, 0:CH], S("newton2"), NEWTON_OPS * c)
                        for t in range(CH):
                            x = dve.tensor_scalar(xc[:, t, :], xc[:, t, :], bag[:, t, 0:1], nvn[:, t:t + 1], ALU.subtract, ALU.mult)
                        x.then_inc(S("fin"), 1)
                    if self.tables:
                        for t in range(CH):
                            dve.wait_ge(S("phi"), CH * b + t + 1)
                            dve.tensor_tensor(pq[t % 2][:, 1, :, :], ps_p(t).rearrange("p (k h) -> p k h", k=2),
                                              pq[t % 2][:, 0, :, :], ALU.subtract).then_inc(S("plo"), 1)

                chunk(0)
                with dve.Fori(1, NCH) as c:
                    chunk(c)

            cname = property(lambda self: "step_final" if self.final else "step")

            def dve_ops(self):
                return 6 if self.final else 2

        x0_rows = dram("x0_rows", [NPAD, D], F32)
        out_pad = dram("out_pad", [NPAD, D], F32)
        tables0 = Node(ND, False, True, False)
        node_mid = Node(ND, True, True, False)
        node_end = Node(ND, True, False, True)


        def general_or_not(eng, then):
            with eng.If(eng.value_load(flag[0:1, 0:1], min_val=0, max_val=1) > 0):
                then()
            with eng.Else():
                eng.nop()

        def nothing(eng, *step):
            pass

        def run(eng, setup, tables, init, init_extra, edges, edges_extra, node, last_node, sp=False, dve=False):
            setup(eng)
            eng.wait_ge(phase, 1)
            tables(eng, 0)
            if sp:
                eng.sem_inc(phase, 1)
            eng.wait_ge(phase, 2)
            init(eng)
            if sp:
                eng.sem_inc(phase, 1)
            eng.wait_ge(phase, 3)
            general_or_not(eng, lambda: init_extra(eng))
            if sp:
                eng.dma_start(degree, agg[:, :]).then_inc(SU("deg"), 16)
                eng.wait_ge(SU("deg"), 16)
                eng.sem_inc(phase, 1)

            def step(s, node):
                eng.wait_ge(phase, 4 + 3 * s)
                fence(eng)
                if sp:
                    eng.dma_start(agg[:, :], degree).then_inc(SU("degin"), 16)
                if dve:
                    k = SU("bias")
                    dve_b = s * 5
                    eng.tensor_tensor(beta_sum[:, :], beta_sum[:, :], beta_col[:, :], ALU.add).then_inc(k, 1)
                    eng.tensor_tensor(p_bias32[:, :], p_bias32[:, :], beta_w1[:, :], ALU.add).then_inc(k, 1)
                    eng.wait_ge(k, dve_b + 2)
                    n = [dve_b + 2]

                    def done(i):
                        i.then_inc(k, 1)
                        n[0] = n[0] + 1
                        eng.wait_ge(k, n[0])

                    pair_p_bias(done, eng)
                    eng.wait_ge(SU("degin"), 16 * s + 16)
                    eng.tensor_scalar(agg[:, :], agg[:, :], beta_sum[:, :], None, ALU.mult).then_inc(SU("seeded"), 1)
                    eng.wait_ge(SU("seeded"), s + 1)
                edges(eng, s)
                if sp:
                    eng.sem_inc(phase, 1)
                eng.wait_ge(phase, 4 + 3 * s + 1)
                fence(eng)
                general_or_not(eng, lambda: edges_extra(eng, s))
                if sp:
                    eng.sem_inc(phase, 1)
                eng.wait_ge(phase, 4 + 3 * s + 2)
                fence(eng)
                node(eng, s)
                if sp:
                    eng.sem_inc(phase, 1)

            with eng.Fori(0, STEPS - 1) as s:
                step(s, node)
            step(STEPS - 1, last_node)
            if sp:
                eng.dma_start(out, out_pad[0:N, :]).then_inc(SU("out"), 16)
                eng.wait_ge(SU("out"), 16)

        def setup_sp2(sp):
            sp.dma_start(x0_rows[0:N, :], x_in).then_inc(SU("x0"), 16)
            sp.wait_ge(SU("dvezero"), 1)
            sp.dma_start(x0_rows[N:NPAD, :], zero[0:NPAD - N, 0:D]).then_inc(SU("x0"), 16)
            sp.wait_ge(SU("x0"), 32)
            setup_sp(sp)

        @block.sync
        def _(sp):
            run(sp, setup_sp2, tables0.sp, I1.sp, I2.sp, S1.sp, S2.sp, node_mid.sp, node_end.sp, sp=True)

        @block.gpsimd
        def _(pool):
            run(pool, setup_pool, nothing, nothing, nothing, S1.pool, S2.pool, nothing, nothing)

        @block.vector
        def _(dve):
            run(dve, setup_dve, tables0.dve, I1.dve, I2.dve, S1.dve, S2.dve, node_mid.dve, node_end.dve, dve=True)

        @block.scalar
        def _(act):
            run(act, nothing, tables0.act, I1.act, I2.act, S1.act, S2.act, node_mid.act, node_end.act)

        @block.tensor
        def _(pe):
            run(pe, setup_pe, tables0.pe, I1.pe, I2.pe, S1.pe, S2.pe, node_mid.pe, node_end.pe)


_INS = ['x', 'src', 'dst', 'edge_attr_4', 'L0_gnn_enc_W', 'L0_gnn_enc_b', 'L0_gnn_eW1', 'L0_gnn_eb1',
        'L0_gnn_eW2', 'L0_gnn_eb2', 'L0_gnn_eg', 'L0_gnn_ebeta', 'L0_gnn_nW1', 'L0_gnn_nb1', 'L0_gnn_nW2',
        'L0_gnn_nb2', 'L0_gnn_ng', 'L0_gnn_nbeta']


def kernel(**inputs):
    import numpy as _np
    import concourse.bacc as _bacc
    from concourse import mybir as _mybir
    from concourse.bass_utils import run_bass_kernel_spmd as _run

    nc = _bacc.Bacc("TRN2", target_bir_lowering=False, num_devices=1)
    arrays, args = {}, []
    for name in _INS:
        a = _np.ascontiguousarray(inputs[name])
        arrays[f"in_{name}"] = a
        args.append(nc.dram_tensor(f"in_{name}", a.shape, _mybir.dt.from_np(a.dtype), kind="ExternalInput").ap())
    args.append(nc.dram_tensor("out_0", (N, D), _mybir.dt.float32, kind="ExternalOutput").ap())
    build_program(nc, *args)
    r = _run(nc, [arrays], core_ids=[0])
    return r.results[0]["out_0"]
```

```python
from contextlib import ExitStack

import concourse.bass as bass
from concourse import mybir

F32, F16, F8, I32 = mybir.dt.float32, mybir.dt.float16, mybir.dt.float8e4, mybir.dt.int32
ALU = mybir.AluOpType
ACT = mybir.ActivationFunctionType
AX = mybir.AxisListType
ds = bass.ds

P = 128
N, E = 3125, 50000
D, H, RAW, STEPS, EPS = 128, 256, 4, 4, 1e-5
TPG = 4
GE = TPG * P
G1 = -(-E // GE)
NT = -(-N // P)
NPAD = NT * P
G2 = (E + NT * (GE - 1)) // GE
G2 += G2 % 2
BIG = float(1 << 20)
LAST = E - (G1 - 1) * GE
CH = 5
NCH = NT // CH
CW = CH * P
EP, EC = 125, 400
R = 4
SCRATCH = 15616 + GE * 12
ARENA = SCRATCH + 4400
RSQRT_SEED = float(0x5F3759DF)
NEWTON = 3
NEWTON_OPS = 2 + 3 * NEWTON


def build_program(nc, x_in, src_in, dst_in, attr_in, enc_W, enc_b, eW1, eb1, eW2, eb2, eg, ebeta,
                  nW1, nb1, nW2, nb2, ng, nbeta, out):
    ctx = ExitStack()
    with ctx:
        def sb(name, shape, dt):
            return ctx.enter_context(nc.sbuf_tensor(name, shape, dt))

        def sem(name):
            return ctx.enter_context(nc.semaphore(name))

        def dram(name, shape, dt):
            return nc.dram_tensor(name, shape, dt, kind="Internal").ap()

        p_table = dram("p_table", [NPAD, 2 * H], F16)
        q_table = dram("q_table", [NPAD, 2 * H], F16)
        onehot = dram("onehot", [G2, P, GE // 4], F32)
        onehot_t = dram("onehot_t", [G2, P, GE // 4], F32)
        state = dram("state", [G2, P, TPG * 2 * D], F16)
        x_rows = dram("x_rows", [NPAD, D], F32)
        x_cols = dram("x_cols", [D, NPAD], F32)
        degree = dram("degree", [P, NPAD], F32)
        rel_rows = dram("rel_rows", [G2, GE], F16)
        attr_p = dram("attr_p", [G2 * GE, RAW], F32)
        records = dram("records", [G2 * GE, 8], I32)

        agg = sb("agg", [P, NPAD], F32)
        idx_all = sb("idx_all", [P, G2, TPG], I32)
        rel_all = sb("rel_all", [P, TPG, P], F32)
        win = sb("win", [1, P], I32)
        flag = sb("flag", [1, 1], I32)
        w1_hi = sb("w1_hi", [P, H], F16)
        w1_lo = sb("w1_lo", [P, H], F16)
        w2_hi = sb("w2_hi", [P, 2, D], F16)
        w2_lo = sb("w2_lo", [P, 2, D], F16)
        v_bias = sb("v_bias", [64, GE], F16)
        g_row = sb("g_row", [P, D], F32)
        nw1 = sb("nw1", [P, 2, H], F32)
        nw2 = sb("nw2", [P, 2, D], F32)
        w_pq = sb("w_pq", [P, 2, H], F32)
        nb1_col = sb("nb1_col", [P, 2], F32)
        u_bias = sb("u_bias", [64, D], F16)
        ng_row = sb("ng_row", [P, D], F32)
        nbeta_row = sb("nbeta_row", [P, D], F32)
        p_bias = sb("p_bias", [64, H], F16)
        p_bias32 = sb("p_bias32", [1, H], F32)
        beta_w1 = sb("beta_w1", [1, H], F32)
        beta_col = sb("beta_col", [P, 1], F32)
        beta_sum = sb("beta_sum", [P, 1], F32)
        ones16 = sb("ones16", [P, P], F16)
        ident16 = sb("ident16", [P, P], F16)
        ident32 = sb("ident32", [P, P], F32)
        node_iota = sb("node_iota", [P, P], F16)
        part_iota = sb("part_iota", [P, 1], F32)
        enc_bd = sb("enc_bd", [TPG * RAW + 1, TPG, D], F32)

        arena = sb("arena", [P, ARENA], F32)
        cut = [0]

        def take(words, dt=F32):
            a = cut[0]
            cut[0] += words
            assert cut[0] <= ARENA, cut[0]
            v = arena[:, a:a + words]
            return v if dt == F32 else v.bitcast(dt)

        h32 = [take(2 * GE).rearrange("p (k e) -> p k e", k=2) for _ in range(2)]
        hh = [take(GE, F16).rearrange("p (k e) -> p k e", k=2) for _ in range(2)]
        hl = [take(GE, F16).rearrange("p (k e) -> p k e", k=2) for _ in range(2)]
        st_in = [take(GE, F16).rearrange("p (t c) -> p t c", t=TPG) for _ in range(R)]
        st_out = [take(GE, F16).rearrange("p (t c) -> p t c", t=TPG) for _ in range(R)]
        resid = [take(GE) for _ in range(R)]
        e_new = [take(GE) for _ in range(2)]
        sq = [take(GE) for _ in range(2)]
        rows = [take(TPG * H, F16).rearrange("p (t c) -> p t c", t=TPG) for _ in range(R)]
        q_win = [take(H, F16) for _ in range(R)]
        eT = [take(GE, F16).rearrange("p (k e) -> p k e", k=2) for _ in range(2)]
        oh = [take(GE // 4, F8) for _ in range(R)]
        oht = [take(GE // 4, F8) for _ in range(R)]
        nv = [take(TPG) for _ in range(2)]
        rs = [take(TPG) for _ in range(2)]
        nt = [take(TPG) for _ in range(2)]
        idx_now = [take(TPG, I32) for _ in range(R)]
        cut[0] = 0
        xc = take(CW).rearrange("p (t f) -> p t f", t=CH)
        xTc = take(CW)
        hN = take(2 * CW).rearrange("p (k e) -> p k e", k=2)
        un = take(CW).rearrange("p (t f) -> p t f", t=CH)
        x0c = take(CW).rearrange("p (t f) -> p t f", t=CH)
        xTn = take(CW)
        sqn = take(D)
        stn = take(8)
        nvn = take(8)
        ntn = take(8)
        bst = take(CH * 6).rearrange("p (t s) -> p t s", t=CH)
        bag = take(CH * 2).rearrange("p (t s) -> p t s", t=CH)
        pq = [take(2 * H, F16).rearrange("p (s k e) -> p s k e", s=2, k=2) for _ in range(2)]
        cut[0] = 0
        at_in = [take(TPG * RAW + 1) for _ in range(2)]
        atT = [take(P) for _ in range(2)]
        e0 = [take(GE) for _ in range(2)]
        st0 = [take(GE, F16).rearrange("p (t c) -> p t c", t=TPG) for _ in range(2)]
        rel_b = [take(GE // 2, F16) for _ in range(2)]
        rel_now = [take(TPG) for _ in range(2)]
        oh0 = [take(GE // 4, F8) for _ in range(2)]
        oht0 = [take(GE // 4, F8) for _ in range(2)]
        cut[0] = SCRATCH
        d_grp = take(GE)
        s_grp = take(GE)
        d_int = take(GE, I32)
        s_int = take(GE, I32)
        rel16 = take(GE // 2, F16)
        tmpw = take(GE)
        tmpv = take(GE)
        red = take(16)
        zero = take(GE)
        cut[0] = 0
        gp = arena[:, 0:15616]
        gcut = [0]

        def gtake(words, dt=F32):
            a = gcut[0]
            gcut[0] += words
            assert gcut[0] <= 15616
            v = gp[:, a:a + words]
            return v if dt == F32 else v.bitcast(dt)

        g_rec = gtake(EC * 8, I32).rearrange("p (e w) -> p e w", w=8)
        g_dst = gtake(EC, I32)
        g_src = gtake(EC, I32)
        g_attr = gtake(EC * RAW, I32).rearrange("p (e w) -> p e w", w=RAW)
        g_q = gtake(EC)
        g_mask = gtake(EC)
        g_scan = gtake(EC)
        g_acc = gtake(EC)
        g_pos = gtake(EC, I32)
        g_ones = gtake(EC)
        g_cnt = gtake(NT)
        g_tot = gtake(NT)
        g_off = gtake(NT)
        g_int = gtake(NT, I32)
        g_tri = gtake(P)
        g_fill = gtake(8 * 8, I32)
        g_stage = [gtake(8, I32) for _ in range(2)]
        g_spos = [gtake(2, I32)[:, 0:1] for _ in range(2)]
        g2 = arena[:, 15616:SCRATCH].bitcast(I32)
        g_all = g2[0:G2, 0:GE * 8].rearrange("p (e w) -> p e w", w=8)
        g_attr2 = g2[0:G2, GE * 8:GE * 12].rearrange("p (e w) -> p e w", w=RAW)

        psum = ctx.enter_context(nc.psum_tensor("psum", [P, 8, 512], F32))

        def ps_h(k):
            return psum[:, 2 * k:2 * k + 2, :]

        def ps_v(k):
            return psum[:, 4 + k, :]

        ps_t = psum[:, 6, :].bitcast(F16)
        ps_a = psum[:, 7, :]

        class Sems:

            def __init__(self, prefix):
                self.prefix, self.made = prefix, {}

            def __call__(self, name):
                if name not in self.made:
                    self.made[name] = sem(f"{self.prefix}_{name}")
                return self.made[name]

        SU = Sems("setup")
        GS = Sems("general")
        Z = Sems("init")
        ES = Sems("edge")
        ND = Sems("node")
        fenced = sem("fenced")
        phase = sem("phase")

        block = ctx.enter_context(nc.Block())

        def later(i):
            return not (isinstance(i, int) and i == 0)

        def fence(eng):
            eng.sem_inc(fenced, 1)

        def newton(dve, v, y, tmp, chain, base, a=0, b=NEWTON_OPS):
            for n in range(a, b):
                if n > 0:
                    dve.wait_ge(chain, base + n)
                if n == 0:
                    x = dve.tensor_scalar(v, v, 1.0 / D, EPS, ALU.mult, ALU.add)
                elif n == 1:
                    x = dve.tensor_scalar(y.bitcast(I32), v.bitcast(I32), -0.5, RSQRT_SEED, ALU.mult, ALU.add)
                elif n % 3 == 2:
                    x = dve.tensor_tensor(tmp, y, y, ALU.mult)
                elif n % 3 == 0:
                    x = dve.scalar_tensor_tensor(tmp, tmp, -0.5, v, ALU.mult, ALU.mult)
                else:
                    x = dve.scalar_tensor_tensor(y, tmp, 1.5, y, ALU.add, ALU.mult)
                x.then_inc(chain, 1)

        def setup_sp(sp):
            def load(dst, src, name="w"):
                sp.dma_start(dst, src).then_inc(SU(name), 16)

            sp.wait_ge(SU("pads"), 2)
            load(d_int[0:G1 - 1, :], dst_in[0:(G1 - 1) * GE].rearrange("(g e) -> g e", e=GE), "dst")
            load(d_int[G1 - 1:G1, 0:LAST], dst_in[(G1 - 1) * GE:E].rearrange("(g e) -> g e", g=1), "dst")
            load(s_int[0:G1 - 1, :], src_in[0:(G1 - 1) * GE].rearrange("(g e) -> g e", e=GE), "src")
            load(s_int[G1 - 1:G1, 0:LAST], src_in[(G1 - 1) * GE:E].rearrange("(g e) -> g e", g=1), "src")
            load(w_pq[:, 0, :], eW1[D:2 * D, :], "w")
            load(w_pq[:, 1, :], eW1[2 * D:3 * D, :], "w")
            load(tmpw[:, 0:H], eW1[0:D, :], "w")
            load(tmpv[:, 0:2 * D].rearrange("p (k f) -> p k f", k=2), eW2.rearrange("(k p) f -> p k f", k=2), "w")
            load(nw1[:, :, :], nW1.rearrange("(k p) f -> p k f", k=2), "w")
            load(nw2[:, :, :], nW2.rearrange("(k p) f -> p k f", k=2), "w")
            load(g_row[:, :], eg.partition_broadcast(P), "w")
            load(ng_row[:, :], ng.partition_broadcast(P), "w")
            load(nbeta_row[:, :], nbeta.partition_broadcast(P), "w")
            for k in range(2):
                load(nb1_col[:, k:k + 1], nb1[k * P:(k + 1) * P].rearrange("(p a) -> p a", a=1), "w")
            load(beta_col[:, :], ebeta.rearrange("(p a) -> p a", a=1), "w")
            load(p_bias32[:, :], eb1.rearrange("(a f) -> a f", a=1), "w")
            load(tmpv[0:1, 2 * D:3 * D], eb2.rearrange("(a f) -> a f", a=1), "w")
            load(tmpv[0:1, 3 * D:4 * D], nb2.rearrange("(a f) -> a f", a=1), "w")
            sp.wait_ge(SU("zeroed"), 1)
            for t in range(TPG):
                load(enc_bd[t * RAW:(t + 1) * RAW, t, :], enc_W, "w")
                load(enc_bd[TPG * RAW:TPG * RAW + 1, t, :], enc_b.rearrange("(a f) -> a f", a=1), "w")
            sp.dma_start(x_rows[0:N, :], x_in).then_inc(SU("xrows"), 16)
            sp.dma_start(x_rows[N:NPAD, :], zero[0:NPAD - N, 0:D]).then_inc(SU("xrows"), 16)
            sp.wait_ge(SU("xrows"), 32)
            sp.wait_ge(SU("flag"), 1)
            with sp.If(sp.value_load(flag[0:1, 0:1], min_val=0, max_val=1) > 0):
                general_sp(sp)
            with sp.Else():
                na = E * RAW
                sp.dma_start(attr_p[0:E, :].rearrange("e w -> (e w)").rearrange("(a b) -> a b", a=100),
                             attr_in.rearrange("e w -> (e w)").rearrange("(a b) -> a b", a=100)).then_inc(SU("attr"), 16)
                sp.dma_start(attr_p[E:G1 * GE, :].rearrange("e w -> (e w)").rearrange("(a b) -> a b", a=16),
                             zero[0:16, 0:(G1 * GE - E) * RAW // 16]).then_inc(SU("attr"), 16)
                sp.wait_ge(SU("attr"), 32)
            sp.wait_ge(SU("rel"), 1)
            sp.dma_start(rel_rows[:, :], rel16[0:G2, :]).then_inc(SU("relrow"), 16)
            sp.wait_ge(SU("relrow"), 16)
            sp.wait_ge(SU("cols"), 3)
            sp.wait_ge(SU("weights"), 1)
            sp.sem_inc(phase, 1)

        NW = 16 * (15 + 2 * TPG)

        def general_sp(sp):
            sp.dma_start(g_dst[0:EP, :], dst_in.rearrange("(p e) -> p e", p=EP)).then_inc(GS("in"), 16)
            sp.dma_start(g_src[0:EP, :], src_in.rearrange("(p e) -> p e", p=EP)).then_inc(GS("in"), 16)
            sp.dma_start(g_attr[0:EP, :, :], attr_in.rearrange("(p e) w -> p e w", p=EP).bitcast(I32)).then_inc(GS("in"), 16)
            sp.wait_ge(GS("fill"), 1)
            rows_a = records.rearrange("(a b) w -> a (b w)", b=8)
            for a in range(0, G2 * GE // 8, P):
                n = min(P, G2 * GE // 8 - a)
                sp.dma_start(rows_a[a:a + n, :], g_fill[0:n, :]).then_inc(GS("filled"), 16)
            sp.wait_ge(GS("filled"), 16 * len(range(0, G2 * GE // 8, P)))
            sp.sem_inc(GS("ready"), 1)
            sp.wait_ge(GS("sorted"), 1)
            sp.dma_start(g_all, records.rearrange("(g e) w -> g e w", e=GE)).then_inc(GS("back"), 16)
            sp.wait_ge(GS("attr"), 1)
            sp.dma_start(attr_p.rearrange("(g e) w -> g e w", e=GE).bitcast(I32), g_attr2).then_inc(GS("attr_out"), 16)
            sp.wait_ge(GS("attr_out"), 16)

        def setup_pool(pool):
            pool.memset(d_int[:, :], 1 << 20).then_inc(SU("pads"), 1)
            pool.memset(s_int[:, :], 0).then_inc(SU("pads"), 1)
            pool.memset(enc_bd[:, :, :], 0.0).then_inc(SU("zeroed"), 1)
            pool.memset(ones16[:, :], 1.0).then_inc(SU("const"), 1)
            pool.memset(ident32[:, :], 0.0).then_inc(SU("ident"), 1)
            pool.iota(part_iota[:, :], pattern=[[0, 1]], base=0, channel_multiplier=1,
                      allow_small_or_imprecise_dtypes=True).then_inc(SU("const"), 1)
            pool.iota(node_iota[:, :], pattern=[[1, P]], base=0, channel_multiplier=0,
                      allow_small_or_imprecise_dtypes=True).then_inc(SU("const"), 1)
            pool.wait_ge(SU("ident"), 1)
            pool.affine_select(out=ident32[:, :], in_=ident32[:, :], compare_op=ALU.not_equal, fill=1.0,
                               base=0, pattern=[[-1, P]], channel_multiplier=1).then_inc(SU("ident"), 1)
            pool.wait_ge(SU("flag"), 1)
            with pool.If(pool.value_load(flag[0:1, 0:1], min_val=0, max_val=1) > 0):
                general_pool(pool)
            with pool.Else():
                pool.nop()

        def general_pool(pool):
            pool.memset(g_tri[:, :], 1.0).then_inc(GS("tri"), 1)
            pool.wait_ge(GS("tri"), 1)
            pool.affine_select(out=g_tri[:, :], in_=g_tri[:, :], compare_op=ALU.is_ge, fill=0.0,
                               base=-1, pattern=[[1, P]], channel_multiplier=-1).then_inc(GS("tri"), 1)
            pool.wait_ge(GS("pos"), 1)
            pool.wait_ge(GS("ready"), 1)
            def column_pair(j):
                for k in range(2):
                    if later(j):
                        pool.wait_ge(GS(f"put{k}"), 16 * j)
                    pool.tensor_copy(g_stage[k], g_rec[:, ds(2 * j + k, 1), :].rearrange("p a w -> p (a w)")).then_inc(GS("staged"), 1)
                    pool.tensor_copy(g_spos[k], g_pos[:, ds(2 * j + k, 1)]).then_inc(GS("staged"), 1)
                    pool.wait_ge(GS("staged"), 4 * j + 2 * k + 2)
                    fence(pool)
                    pool.indirect_dma_start(out=records, out_offset=bass.IndirectOffsetOnAxis(ap=g_spos[k][0:EP, :], axis=0),
                                            in_=g_stage[k][0:EP, :], in_offset=None).then_inc(GS(f"put{k}"), 16)

            column_pair(0)
            with pool.Fori(1, EC // 2) as j:
                column_pair(j)
            for k in range(2):
                pool.wait_ge(GS(f"put{k}"), 16 * (EC // 2))
            pool.sem_inc(GS("sorted"), 1)

        def setup_dve(dve):
            chain = SU("dve")
            n = [0]

            def done(i):
                i.then_inc(chain, 1)
                n[0] += 1
                dve.wait_ge(chain, n[0])

            done(dve.memset(red, 0.0))
            dve.memset(zero, 0.0).then_inc(SU("dvezero"), 1)
            done(dve.memset(p_bias[:, :], 0.0))
            done(dve.memset(v_bias[:, :], 0.0))
            done(dve.memset(u_bias[:, :], 0.0))
            done(dve.memset(agg[:, :], 0.0))
            done(dve.memset(rel_all[:, :, :], 0.0))
            done(dve.memset(beta_sum[:, :], 0.0))
            dve.wait_ge(SU("dst"), 32)
            dve.wait_ge(SU("ident"), 2)
            done(dve.tensor_copy(ident16[:, :], ident32[:, :]))
            done(dve.tensor_copy(d_grp, d_int))
            done(dve.tensor_reduce(red[:, 0:1], d_grp, AX.X, ALU.min))
            done(dve.tensor_scalar(red[:, 0:1], red[:, 0:1], float(N - P), None, ALU.min))
            done(dve.tensor_reduce(red[0:G1, 1:2], d_grp[0:G1, 0:LAST], AX.X, ALU.max))
            done(dve.tensor_reduce(red[0:G1 - 1, 2:3], d_grp[0:G1 - 1, LAST:GE], AX.X, ALU.max))
            done(dve.tensor_tensor(red[0:G1, 1:2], red[0:G1, 1:2], red[0:G1, 2:3], ALU.max))
            done(dve.tensor_tensor(red[0:G1, 3:4], red[0:G1, 1:2], red[0:G1, 0:1], ALU.subtract))
            dve.sem_inc(SU("width"), 1)
            dve.wait_ge(SU("widthT"), 1)
            done(dve.tensor_reduce(red[0:1, 4:5], psum[0:1, 0, 0:G1], AX.X, ALU.max))
            dve.tensor_scalar(flag[0:1, 0:1], red[0:1, 4:5], float(P - 1), None, ALU.is_gt).then_inc(SU("flag"), 1)
            dve.wait_ge(SU("flag"), 1)
            dve.wait_ge(SU("w"), NW)
            done(dve.tensor_copy(w1_hi[:, :], tmpw[:, 0:H]))
            done(dve.tensor_tensor(w1_lo[:, :], tmpw[:, 0:H], w1_hi[:, :], ALU.subtract))
            w2 = tmpv[:, 0:2 * D].rearrange("p (k f) -> p k f", k=2)

            def centre(w, cols):
                done(dve.tensor_reduce(cols, w, AX.X, ALU.add))
                done(dve.tensor_scalar(cols, cols, -1.0 / D, None, ALU.mult))

            centre(w2, red[:, 5:7])
            for k in range(2):
                done(dve.tensor_scalar(w2[:, k, :], w2[:, k, :], red[:, 5 + k:6 + k], None, ALU.add))
            done(dve.tensor_copy(w2_hi[:, :, :], w2))
            done(dve.tensor_tensor(w2_lo[:, :, :], w2, w2_hi[:, :, :], ALU.subtract))
            centre(nw2[:, :, :], red[:, 7:9])
            for k in range(2):
                done(dve.tensor_scalar(nw2[:, k, :], nw2[:, k, :], red[:, 7 + k:8 + k], None, ALU.add))
            for row, bias, reps in ((2, v_bias, TPG), (3, u_bias, 1)):
                b = tmpv[0:1, row * D:(row + 1) * D]
                centre(b, red[0:1, 9:10])
                done(dve.tensor_scalar(b, b, red[0:1, 9:10], None, ALU.add))
                for r in range(reps):
                    done(dve.tensor_copy(bias[0:1, r * D:(r + 1) * D], b))
                for r in range(reps):
                    done(dve.tensor_tensor(d_row[0:1, 0:D], b, bias[0:1, 0:D], ALU.subtract))
                    done(dve.tensor_copy(bias[32:33, r * D:(r + 1) * D], d_row[0:1, 0:D]))
            dve.wait_ge(SU("betaw"), 1)
            done(dve.tensor_copy(beta_w1[:, :], psum[0:1, 1, 0:H]))
            pair_p_bias(done, dve)
            dve.sem_inc(SU("weights"), 1)
            with dve.If(dve.value_load(flag[0:1, 0:1], min_val=0, max_val=1) > 0):
                general_dve(dve)
            with dve.Else():
                dve.nop()
            c2 = SU("dve2")
            m = [0]

            def done2(i):
                i.then_inc(c2, 1)
                m[0] += 1
                dve.wait_ge(c2, m[0])

            dve.wait_ge(SU("src"), 32)
            done2(dve.tensor_copy(d_grp, d_int))
            done2(dve.tensor_copy(s_grp, s_int))
            done2(dve.tensor_reduce(red[:, 0:1], d_grp, AX.X, ALU.min))
            done2(dve.tensor_scalar(red[:, 0:1], red[:, 0:1], float(N - P), None, ALU.min))
            done2(dve.tensor_scalar(d_grp, d_grp, red[:, 0:1], 255.0, ALU.subtract, ALU.min))
            dve.tensor_copy(rel16.rearrange("g (t p) -> g t p", t=TPG),
                            d_grp.rearrange("g (p t) -> g t p", t=TPG)).then_inc(SU("rel"), 1)
            dve.sem_inc(SU("grp"), 1)
            dve.wait_ge(SU("relT"), 1)
            dve.tensor_copy(rel_all[:, :, 0:G2], psum[:, 2, :].rearrange("p (t g) -> p t g", t=TPG)[:, :, 0:G2]).then_inc(SU("cols"), 1)
            dve.wait_ge(SU("srcT"), 1)
            dve.tensor_copy(idx_all[:, :, :].rearrange("p g t -> p t g"),
                            psum[:, 3, :].rearrange("p (t g) -> p t g", t=TPG)[:, :, 0:G2]).then_inc(SU("cols"), 1)
            dve.wait_ge(SU("winT"), 1)
            dve.tensor_copy(win[0:1, 0:G2], psum[0:1, 0, 128:128 + G2]).then_inc(SU("cols"), 1)

        d_row = sb("d_row", [1, H], F32)

        def pair_p_bias(done, dve):
            done(dve.tensor_copy(p_bias[0:1, :], p_bias32[:, :]))
            done(dve.tensor_tensor(d_row[:, :], p_bias32[:, :], p_bias[0:1, :], ALU.subtract))
            done(dve.tensor_copy(p_bias[32:33, :], d_row[:, :]))

        def general_dve(dve):
            c = GS("dve")
            n = [0]

            def done(i):
                i.then_inc(c, 1)
                n[0] += 1
                dve.wait_ge(c, n[0])

            fill = g_fill.rearrange("p (e w) -> p e w", w=8)
            done(dve.memset(fill, 0))
            dve.memset(fill[:, :, 1:2], 1 << 20).then_inc(GS("fill"), 1)
            done(dve.memset(g_rec, 0))
            done(dve.memset(g_pos, 0))
            done(dve.memset(g_ones, 1.0))
            done(dve.memset(g_acc, 0.0))
            dve.wait_ge(GS("in"), 48)
            done(dve.tensor_copy(g_rec[0:EP, :, 0:1].rearrange("p e w -> p (e w)"), g_src[0:EP, :]))
            done(dve.tensor_copy(g_rec[0:EP, :, 1:2].rearrange("p e w -> p (e w)"), g_dst[0:EP, :]))
            done(dve.tensor_copy(g_rec[0:EP, :, 2:2 + RAW], g_attr[0:EP, :, :]))
            done(dve.tensor_scalar(g_dst[0:EP, :], g_dst[0:EP, :], 7, None, ALU.logical_shift_right))
            done(dve.tensor_copy(g_q[0:EP, :], g_dst[0:EP, :]))
            for b in range(NT):
                done(dve.tensor_scalar(g_mask[0:EP, :], g_q[0:EP, :], float(b), None, ALU.is_equal))
                done(dve.tensor_tensor_scan(g_scan[0:EP, :], g_ones[0:EP, :], g_mask[0:EP, :], 0.0, ALU.mult, ALU.add))
                done(dve.tensor_copy(g_cnt[0:EP, b:b + 1], g_scan[0:EP, EC - 1:EC]))
                done(dve.tensor_tensor(g_scan[0:EP, :], g_scan[0:EP, :], g_mask[0:EP, :], ALU.mult))
                done(dve.tensor_tensor(g_acc[0:EP, :], g_acc[0:EP, :], g_scan[0:EP, :], ALU.add))
            dve.sem_inc(GS("counts"), 1)
            dve.wait_ge(GS("sums"), 1)
            done(dve.tensor_scalar(g_tot[0:EP, :], psum[0:EP, 1, 0:NT], float(GE - 1), None, ALU.add))
            done(dve.tensor_copy(g_int[0:EP, :], g_tot[0:EP, :]))
            done(dve.tensor_scalar(g_int[0:EP, :], g_int[0:EP, :], 9, 9, ALU.logical_shift_right, ALU.logical_shift_left))
            done(dve.tensor_copy(g_tot[0:EP, :], g_int[0:EP, :]))
            done(dve.tensor_tensor_scan(g_off[0:EP, :], g_ones[0:EP, 0:NT], g_tot[0:EP, :], 0.0, ALU.mult, ALU.add))
            done(dve.tensor_tensor(g_off[0:EP, :], g_off[0:EP, :], g_tot[0:EP, :], ALU.subtract))
            done(dve.tensor_tensor(g_off[0:EP, :], g_off[0:EP, :], psum[0:EP, 0, 0:NT], ALU.add))
            for b in range(NT):
                done(dve.tensor_scalar(g_mask[0:EP, :], g_q[0:EP, :], float(b), g_off[0:EP, b:b + 1], ALU.is_equal, ALU.mult))
                done(dve.tensor_tensor(g_acc[0:EP, :], g_acc[0:EP, :], g_mask[0:EP, :], ALU.add))
            dve.tensor_scalar(g_pos[0:EP, :], g_acc[0:EP, :], -1.0, None, ALU.add).then_inc(GS("pos"), 1)
            dve.wait_ge(GS("back"), 16)
            dve.tensor_copy(g_attr2, g_all[:, :, 2:2 + RAW]).then_inc(GS("attr"), 1)
            done(dve.tensor_copy(d_int[0:G2, :], g_all[:, :, 1:2].rearrange("p e w -> p (e w)")))
            done(dve.tensor_copy(s_int[0:G2, :], g_all[:, :, 0:1].rearrange("p e w -> p (e w)")))

        def setup_pe(pe):
            pe.wait_ge(SU("ident"), 2)
            pe.wait_ge(SU("width"), 1)
            pe.transpose(psum[0:1, 0, 0:P], red[:, 3:4], ident32[:, :]).then_inc(SU("widthT"), 1)
            pe.wait_ge(SU("w"), NW)
            pe.matmul(psum[0:1, 1, 0:H], beta_col[:, :], tmpw[:, 0:H], start=True, stop=True).then_inc(SU("betaw"), 1)
            pe.wait_ge(SU("flag"), 1)
            with pe.If(pe.value_load(flag[0:1, 0:1], min_val=0, max_val=1) > 0):
                pe.wait_ge(GS("counts"), 1)
                pe.wait_ge(GS("tri"), 2)
                pe.matmul(psum[:, 0, 0:NT], g_tri[0:EP, :], g_cnt[0:EP, :], start=True, stop=True)
                pe.matmul(psum[0:EP, 1, 0:NT], g_ones[0:EP, 0:EP], g_cnt[0:EP, :], start=True, stop=True).then_inc(GS("sums"), 1)
            with pe.Else():
                pe.nop()
            pe.wait_ge(SU("grp"), 1)
            for t in range(TPG):
                i = pe.transpose(psum[:, 2, t * P:(t + 1) * P], d_grp.rearrange("g (p t) -> g t p", t=TPG)[:, t, :], ident32[:, :])
            i.then_inc(SU("relT"), 1)
            for t in range(TPG):
                i = pe.transpose(psum[:, 3, t * P:(t + 1) * P], s_grp.rearrange("g (p t) -> g t p", t=TPG)[:, t, :], ident32[:, :])
            i.then_inc(SU("srcT"), 1)
            pe.transpose(psum[0:1, 0, P:2 * P], red[:, 0:1], ident32[:, :]).then_inc(SU("winT"), 1)

        class Init:

            def __init__(self, S, first, last):
                self.S, self.first, self.last = S, first // 2, last // 2

            def loop(self, eng, body):
                for k in range(2):
                    body(eng, self.first, k)
                with eng.Fori(self.first + 1, self.last) as q:
                    for k in range(2):
                        body(eng, q, k)

            def sp(self, sp):
                S = self.S

                def load(q, k):
                    g = 2 * q + k
                    if later(q):
                        sp.wait_ge(S("atT"), 2 * q)
                        fence(sp)
                    sp.dma_start(at_in[k][:, 0:TPG * RAW],
                                 attr_p.rearrange("(g p t) w -> g p (t w)", p=P, t=TPG)[ds(g, 1), :, :].rearrange("a p w -> (a p) w")).then_inc(S(f"at{k}"), 16)
                    if later(q):
                        sp.wait_ge(S("oht"), 2 * q)
                        fence(sp)
                    sp.dma_start(rel_b[k], rel_rows[ds(g, 1), :].rearrange("a e -> (a e)").partition_broadcast(P)).then_inc(S(f"rb{k}"), 16)

                def store(q, k):
                    g = 2 * q + k
                    sp.wait_ge(S("oht"), 2 * q + k + 1)
                    sp.wait_ge(S("oh"), 2 * q + k + 1)
                    fence(sp)
                    for m01, here in ((onehot, oh0), (onehot_t, oht0)):
                        sp.dma_start(m01[ds(g, 1), :, :].rearrange("a p c -> (a p) c"), here[k].bitcast(F32)).then_inc(S(f"oh{k}"), 16)
                    sp.wait_ge(S("lo"), 2 * q + k + 1)
                    fence(sp)
                    sp.dma_start(state[ds(g, 1), :, :].rearrange("a p c -> (a p) c"), st0[k].rearrange("p t c -> p (t c)")).then_inc(S(f"st{k}"), 16)

                for k in range(2):
                    load(self.first, k)
                with sp.Fori(self.first + 1, self.last) as q:
                    for k in range(2):
                        load(q, k)
                    for k in range(2):
                        store(q - 1, k)
                for k in range(2):
                    store(self.last - 1, k)
                for k in range(2):
                    sp.wait_ge(S(f"st{k}"), 16 * self.last)
                    sp.wait_ge(S(f"oh{k}"), 32 * self.last)
                sp.wait_ge(S("deg"), 2 * self.last)

            def pe(self, pe):
                S = self.S

                def body(pe, q, k):
                    m = 2 * q + k
                    pe.wait_ge(S(f"at{k}"), 16 * q + 16)
                    if later(q):
                        pe.wait_ge(S("atc"), m - k)
                    pe.transpose(psum[0:TPG * RAW + 1, k, 0:P], at_in[k], ident32[:, :]).then_inc(S("atT"), 1)
                    pe.wait_ge(S("atc"), m + 1)
                    if later(q):
                        pe.wait_ge(S("enc"), m - k)
                    pe.matmul(psum[:, 2 + k, :], atT[k][0:TPG * RAW + 1, :], enc_bd[:, :, :].rearrange("a t f -> a (t f)"),
                              start=True, stop=True).then_inc(S("encm"), 1)
                    pe.wait_ge(S("oh"), m + 1)
                    if later(q):
                        pe.wait_ge(S("deg"), m - k)
                    fence(pe)
                    for t in range(TPG):
                        i = pe.matmul(psum[:, 4 + k, 0:P], ones16[:, :], oh0[k][:, t * P:(t + 1) * P],
                                      start=t == 0, stop=t == TPG - 1)
                    i.then_inc(S("degm"), 1)

                pe.wait_ge(S("one"), 2)
                self.loop(pe, body)

            def act(self, act):
                S = self.S

                def body(act, q, k):
                    m = 2 * q + k
                    act.wait_ge(S("atT"), m + 1)
                    if later(q):
                        act.wait_ge(S("encm"), m - k)
                    act.copy(atT[k][0:TPG * RAW + 1, :], psum[0:TPG * RAW + 1, k, 0:P]).then_inc(S("atc"), 1)
                    act.wait_ge(S("encm"), m + 1)
                    if later(q):
                        act.wait_ge(S("lo"), m - k)
                    act.activation(e0[k], psum[:, 2 + k, :], ACT.Silu).then_inc(S("enc"), 1)
                    act.wait_ge(S("enc"), m + 1)
                    if later(q):
                        act.wait_ge(S(f"st{k}"), 16 * q)
                    act.copy(st0[k][:, :, 0:D], e0[k].rearrange("p (t f) -> p t f", t=TPG)).then_inc(S("hi"), 1)

                self.loop(act, body)

            def dve(self, dve):
                S = self.S

                def body(dve, q, k):
                    m = 2 * q + k
                    dve.tensor_copy(rel_now[k], rel_all[:, :, ds(m, 1)].rearrange("p t a -> p (t a)")).then_inc(S("rel"), 1)
                    if later(q):
                        dve.wait_ge(S(f"oh{k}"), 32 * q)
                        dve.wait_ge(S("degm"), 2 * q)
                    dve.wait_ge(S("rel"), m + 1)
                    fence(dve)
                    for t in range(TPG):
                        i = dve.tensor_scalar(oh0[k][:, t * P:(t + 1) * P], node_iota[:, :], rel_now[k][:, t:t + 1],
                                              None, ALU.is_equal, saturate=False)
                    i.then_inc(S("oh"), 1)
                    dve.wait_ge(S(f"rb{k}"), 16 * q + 16)
                    fence(dve)
                    dve.tensor_scalar(oht0[k], rel_b[k], part_iota[:, :], None,
                                      ALU.is_equal, saturate=False).then_inc(S("oht"), 1)
                    dve.wait_ge(S("hi"), m + 1)
                    dve.tensor_tensor(st0[k][:, :, D:2 * D], e0[k].rearrange("p (t f) -> p t f", t=TPG),
                                      st0[k][:, :, 0:D], ALU.subtract).then_inc(S("lo"), 1)
                    dve.wait_ge(S("degm"), m + 1)
                    if later(m):
                        dve.wait_ge(S("deg"), m)
                    fence(dve)
                    w = dve.value_load(win[0:1, ds(m, 1)], min_val=0, max_val=N - P)
                    dve.tensor_tensor(agg[:, ds(w, P)], agg[:, ds(w, P)], psum[:, 4 + k, 0:P], ALU.add).then_inc(S("deg"), 1)

                if self.first == 0:
                    for k in range(2):
                        dve.memset(at_in[k][:, TPG * RAW:TPG * RAW + 1], 1.0).then_inc(S("one"), 1)
                self.loop(dve, body)

        I1, I2 = Init(Z, 0, G1), Init(Z, G1, G2)

        class Edge:

            def __init__(self, S, lo, hi):
                self.S, self.lo, self.hi = S, lo, hi

            def loop(self, eng, body, back, ahead):
                start, end = self.lo // R, -(-(self.hi + back) // R)
                first = -(-(self.lo + back) // R)
                last = (self.hi - R - ahead) // R + 1
                for i in range(start, first):
                    body(i)
                with eng.Fori(first, last) as i:
                    body(i)
                for i in range(last, end):
                    body(i)

            def has(self, i, off):
                return not isinstance(i, int) or self.lo <= R * i + off < self.hi

            def ring(self, s, i, off):
                j = off % R
                return s * len(range(j, G2, R)) + i + off // R + 1

            def gathered(self, s, i, off):
                j = off % R
                n = sum(g % R == j for g in range(self.lo, self.hi))
                before = sum(g % R == j for g in range(self.lo))
                return self.rows_sem(off), 16 * TPG * (s * n + i + off // R + 1 - before)

            def rows_sem(self, off):
                return self.S(f"rows{off % R}" if self.lo == 0 else f"extra_rows{off % R}")

            def skip_per_group(self, eng, *names):
                for x in names:
                    eng.sem_inc(self.S(x), G2 - G1)

            def skip_ring(self, eng, name, per_group):
                for j in range(R):
                    n = sum(g % R == j for g in range(G1, G2))
                    eng.sem_inc(self.S(f"{name}{j}"), per_group * n)

            def skip_sp(self, sp):
                self.skip_ring(sp, "st", 16)
                self.skip_ring(sp, "q", 32)
                self.skip_ring(sp, "oh", 16)
                self.skip_ring(sp, "out", 16)

            def skip_pool(self, pool):
                self.skip_per_group(pool, "idx")

            def skip_pe(self, pe):
                self.skip_per_group(pe, "transposed", "src", "h", "v", "sum")

            def skip_act(self, act):
                self.skip_per_group(act, "h32", "hh", "eT", "sq", "eh")

            def skip_dve(self, dve):
                self.skip_per_group(dve, "hl", "scaled", "new", "resid", "el", "added")
                dve.sem_inc(self.S("newton"), NEWTON_OPS * (G2 - G1))

            def sp(self, sp, s):
                S = self.S
                c = lambda i, off: s * G2 + R * i + off + 1

                def group(ap, i, off):
                    return ap[ds(R * i + off, 1), :, :].rearrange("a p c -> (a p) c")

                def load(i, off):
                    if not self.has(i, off):
                        return
                    k = off % R
                    if self.has(i, off - R):
                        sp.wait_ge(S("resid"), c(i, off - R))
                        sp.wait_ge(S("transposed"), c(i, off - R))
                        sp.wait_ge(S("h"), c(i, off - R))
                        fence(sp)
                    sp.dma_start(st_in[k].rearrange("p t c -> p (t c)"), group(state, i, off)).then_inc(S(f"st{k}"), 16)
                    w = sp.value_load(win[0:1, ds(R * i + off, 1)], min_val=0, max_val=N - P)
                    sp.dma_start(q_win[k], q_table[ds(w, P), :]).then_inc(S(f"q{k}"), 16)
                    sp.dma_start(oht[k].bitcast(F32), group(onehot_t, i, off)).then_inc(S(f"q{k}"), 16)

                def load_sum(i, off):
                    if not self.has(i, off):
                        return
                    k = off % R
                    if self.has(i, off - R):
                        sp.wait_ge(S("sum"), c(i, off - R))
                        fence(sp)
                    sp.dma_start(oh[k].bitcast(F32), group(onehot, i, off)).then_inc(S(f"oh{k}"), 16)

                def store(i, off):
                    if not self.has(i, off):
                        return
                    k = off % R
                    sp.wait_ge(S("el"), c(i, off))
                    fence(sp)
                    sp.dma_start(group(state, i, off), st_out[k].rearrange("p t c -> p (t c)")).then_inc(S(f"out{k}"), 16)

                for g in range(self.lo, self.lo + 3):
                    load(0, g)

                def body(i):
                    for j in range(R):
                        if not isinstance(i, int) or R * i + j >= self.lo:
                            load(i, j + 3)
                        load_sum(i, j - 1)
                        store(i, j - 4)

                self.loop(sp, body, back=5, ahead=3)
                for j in range(R):
                    sp.wait_ge(S(f"out{j}"), 16 * self.ring(s, (self.hi - 1 - j) // R, j))
                    fence(sp)
                sp.wait_ge(S("added"), c(0, self.hi - 1))
                fence(sp)

            def pool(self, pool, s):
                S = self.S
                c = lambda i, off: s * G2 + R * i + off + 1

                def indices(i, off):
                    if not self.has(i, off):
                        return
                    k = off % R
                    if self.has(i, off - R):
                        pool.wait_ge(*self.gathered(s, i, off - R))
                        fence(pool)
                    pool.tensor_copy(idx_now[k], idx_all[:, ds(R * i + off, 1), :].rearrange("p a t -> p (a t)")).then_inc(S("idx"), 1)

                def gather(i, off):
                    if not self.has(i, off):
                        return
                    k = off % R
                    if self.has(i, off - R):
                        pool.wait_ge(S("src"), c(i, off - R))
                    pool.wait_ge(S("idx"), c(i, off))
                    fence(pool)
                    for t in range(TPG):
                        pool.indirect_dma_start(
                            out=rows[k][:, t, :], out_offset=None, in_=p_table,
                            in_offset=bass.IndirectOffsetOnAxis(ap=idx_now[k][:, t:t + 1], axis=0),
                        ).then_inc(self.rows_sem(off), 16)

                indices(0, self.lo)

                def body(i):
                    for j in range(R):
                        if not isinstance(i, int) or R * i + j >= self.lo:
                            indices(i, j + 1)
                        gather(i, j)

                self.loop(pool, body, back=4, ahead=1)

            def pe(self, pe, s):
                S = self.S
                c = lambda i, off: s * G2 + R * i + off + 1

                def turn(i, off):
                    if not self.has(i, off):
                        return
                    k = off % R
                    pe.wait_ge(S(f"st{k}"), 16 * self.ring(s, i, off))
                    if self.has(i, off - 1):
                        pe.wait_ge(S("eT"), c(i, off - 1))
                    for p in range(2):
                        for t in range(TPG):
                            n = p * TPG + t
                            x = pe.transpose(ps_t[:, n * P:(n + 1) * P], st_in[k][:, t, p * D:(p + 1) * D], ident16[:, :])
                    x.then_inc(S("transposed"), 1)

                def hidden(i, off):
                    if not self.has(i, off):
                        return
                    k, k2 = off % R, off % 2
                    pe.wait_ge(S(f"q{k}"), 32 * self.ring(s, i, off))
                    if self.has(i, off - 2):
                        pe.wait_ge(S("hh"), c(i, off - 2))
                    fence(pe)
                    for half in range(2):
                        for p in range(2):
                            pe.matmul(ps_h(k2)[:, half, :], q_win[k][:, p * H + half * D:p * H + half * D + D], oht[k],
                                      start=p == 0, stop=False, skip_group_check=True)
                    pe.wait_ge(*self.gathered(s, i, off))
                    for t in range(TPG):
                        for half in range(2):
                            for p in range(2):
                                x = pe.matmul(ps_h(k2)[:, half, t * P:(t + 1) * P],
                                              rows[k][:, t, p * H + half * D:p * H + half * D + D], ident16[:, :],
                                              start=False, stop=False, skip_group_check=True)
                    x.then_inc(S("src"), 1)
                    pe.wait_ge(S("eT"), c(i, off))
                    for half in range(2):
                        cols = slice(half * D, (half + 1) * D)
                        for w, p in ((w1_hi, 0), (w1_hi, 1), (w1_lo, 0)):
                            x = pe.matmul(ps_h(k2)[:, half, :], w[:, cols], eT[k2][:, p, :],
                                          start=False, stop=w is w1_lo, skip_group_check=True)
                    x.then_inc(S("h"), 1)

                def output(i, off):
                    if not self.has(i, off):
                        return
                    k2 = off % 2
                    if self.has(i, off - 2):
                        pe.wait_ge(S("scaled"), c(i, off - 2))
                    pe.matmul(ps_v(k2), ones16[0:64, :], v_bias[:, :], start=True, stop=False, skip_group_check=True)
                    pe.wait_ge(S("hl"), c(i, off))
                    for t in range(TPG):
                        for half in range(2):
                            for h, w in ((hh, w2_hi), (hh, w2_lo), (hl, w2_hi)):
                                x = pe.matmul(ps_v(k2)[:, t * P:(t + 1) * P], h[k2][:, half, t * P:(t + 1) * P], w[:, half, :],
                                              start=False, stop=half == 1 and h is hl, skip_group_check=True)
                    x.then_inc(S("v"), 1)

                def node_sums(i, off):
                    if not self.has(i, off):
                        return
                    k = off % R
                    pe.wait_ge(S("el"), c(i, off))
                    if self.has(i, off - 1):
                        pe.wait_ge(S("added"), c(i, off - 1))
                    pe.wait_ge(S(f"oh{k}"), 16 * self.ring(s, i, off))
                    fence(pe)
                    for t in range(TPG):
                        for p in range(2):
                            x = pe.matmul(ps_a[:, 0:P], st_out[k][:, t, p * D:(p + 1) * D], oh[k][:, t * P:(t + 1) * P],
                                          start=t == 0 and p == 0, stop=t == TPG - 1 and p == 1, skip_group_check=True)
                    x.then_inc(S("sum"), 1)

                turn(0, self.lo)
                turn(0, self.lo + 1)

                def body(i):
                    for j in range(R):
                        hidden(i, j)
                        if not isinstance(i, int) or R * i + j >= self.lo:
                            turn(i, j + 2)
                        output(i, j - 1)
                        node_sums(i, j - 4)

                self.loop(pe, body, back=5, ahead=2)

            def act(self, act, s):
                S = self.S
                c = lambda i, off: s * G2 + R * i + off + 1

                def silu(i, off):
                    if not self.has(i, off):
                        return
                    k2 = off % 2
                    act.wait_ge(S("h"), c(i, off))
                    if self.has(i, off - 2):
                        act.wait_ge(S("hl"), c(i, off - 2))
                    act.activation(h32[k2], ps_h(k2), ACT.Silu).then_inc(S("h32"), 1)
                    if self.has(i, off - 2):
                        act.wait_ge(S("v"), c(i, off - 2))
                    act.activation(hh[k2], ps_h(k2), ACT.Silu).then_inc(S("hh"), 1)

                def squares(i, off):
                    if not self.has(i, off):
                        return
                    k2 = off % 2
                    act.wait_ge(S("v"), c(i, off))
                    if self.has(i, off - 2):
                        act.wait_ge(S("sq"), c(i, off - 2))
                        act.wait_ge(S("scaled"), c(i, off - 2))
                    for t in range(TPG):
                        x = act.activation(sq[k2][:, t * P:(t + 1) * P], ps_v(k2)[:, t * P:(t + 1) * P], ACT.Square,
                                           accum_out=nv[k2][:, t:t + 1])
                    x.then_inc(S("sq"), 1)

                def turned(i, off):
                    if not self.has(i, off):
                        return
                    k2 = off % 2
                    act.wait_ge(S("transposed"), c(i, off))
                    if self.has(i, off - 2):
                        act.wait_ge(S("h"), c(i, off - 2))
                    act.copy(eT[k2].rearrange("p k e -> p (k e)"), ps_t[:, :]).then_inc(S("eT"), 1)

                def high(i, off):
                    if not self.has(i, off):
                        return
                    k, k2 = off % R, off % 2
                    act.wait_ge(S("new"), c(i, off))
                    if self.has(i, off - R):
                        act.wait_ge(S("sum"), c(i, off - R))
                        act.wait_ge(S(f"out{k}"), 16 * self.ring(s, i, off - R))
                    act.copy(st_out[k][:, :, 0:D], e_new[k2].rearrange("p (t f) -> p t f", t=TPG)).then_inc(S("eh"), 1)

                turned(0, self.lo)
                turned(0, self.lo + 1)

                def body(i):
                    for j in range(R):
                        silu(i, j)
                        squares(i, j - 1)
                        if not isinstance(i, int) or R * i + j >= self.lo:
                            turned(i, j + 2)
                        high(i, j - 3)

                self.loop(act, body, back=7, ahead=2)

            def dve(self, dve, s):
                S = self.S
                c = lambda i, off: s * G2 + R * i + off + 1

                def low(i, off):
                    if not self.has(i, off):
                        return
                    k2 = off % 2
                    dve.wait_ge(S("hh"), c(i, off))
                    dve.wait_ge(S("h32"), c(i, off))
                    if self.has(i, off - 2):
                        dve.wait_ge(S("v"), c(i, off - 2))
                    dve.tensor_tensor(hl[k2], h32[k2], hh[k2], ALU.subtract).then_inc(S("hl"), 1)

                def root(i, off, a, b):
                    if not self.has(i, off):
                        return
                    k2 = off % 2
                    if a == 0:
                        dve.wait_ge(S("sq"), c(i, off))
                        if self.has(i, off - 2):
                            dve.wait_ge(S("scaled"), c(i, off - 2))
                    newton(dve, nv[k2], rs[k2], nt[k2], S("newton"), (c(i, off) - 1) * NEWTON_OPS, a, b)

                def scale(i, off, t):
                    if not self.has(i, off):
                        return
                    k2 = off % 2
                    if t == 0:
                        dve.wait_ge(S("newton"), c(i, off) * NEWTON_OPS)
                        if self.has(i, off - 2):
                            dve.wait_ge(S("el"), c(i, off - 2))
                    x = dve.scalar_tensor_tensor(e_new[k2][:, t * P:(t + 1) * P], ps_v(k2)[:, t * P:(t + 1) * P],
                                                 rs[k2][:, t:t + 1], g_row[:, :], ALU.mult, ALU.mult)
                    if t == TPG - 1:
                        x.then_inc(S("scaled"), 1)

                def add_old(i, off):
                    if not self.has(i, off):
                        return
                    k, k2 = off % R, off % 2
                    dve.wait_ge(S("scaled"), c(i, off))
                    dve.wait_ge(S("resid"), c(i, off))
                    dve.tensor_tensor(e_new[k2], e_new[k2], resid[k], ALU.add).then_inc(S("new"), 1)

                def old(i, off):
                    if not self.has(i, off):
                        return
                    k = off % R
                    dve.wait_ge(S(f"st{k}"), 16 * self.ring(s, i, off))
                    if self.has(i, off - R):
                        dve.wait_ge(S("new"), c(i, off - R))
                    dve.tensor_tensor(resid[k].rearrange("p (t f) -> p t f", t=TPG), st_in[k][:, :, 0:D],
                                      st_in[k][:, :, D:2 * D], ALU.add).then_inc(S("resid"), 1)

                def low_new(i, off):
                    if not self.has(i, off):
                        return
                    k, k2 = off % R, off % 2
                    dve.wait_ge(S("eh"), c(i, off))
                    dve.tensor_tensor(st_out[k][:, :, D:2 * D], e_new[k2].rearrange("p (t f) -> p t f", t=TPG),
                                      st_out[k][:, :, 0:D], ALU.subtract).then_inc(S("el"), 1)

                def add_window(i, off):
                    if not self.has(i, off):
                        return
                    dve.wait_ge(S("sum"), c(i, off))
                    if self.has(i, off - 1):
                        dve.wait_ge(S("added"), c(i, off - 1))
                    fence(dve)
                    w = dve.value_load(win[0:1, ds(R * i + off, 1)], min_val=0, max_val=N - P)
                    dve.tensor_tensor(agg[:, ds(w, P)], agg[:, ds(w, P)], ps_a[:, 0:P], ALU.add).then_inc(S("added"), 1)

                old(0, self.lo)

                def body(i):
                    for j in range(R):
                        low(i, j)
                        root(i, j - 1, 0, 1)
                        add_window(i, j - 4)
                        for t in range(TPG):
                            root(i, j - 1, t + 1, t + 2)
                            scale(i, j - 2, t)
                        root(i, j - 1, 5, 6)
                        add_old(i, j - 2)
                        root(i, j - 1, 6, 7)
                        if not isinstance(i, int) or R * i + j >= self.lo:
                            old(i, j + 1)
                        root(i, j - 1, 7, 8)
                        low_new(i, j - 3)
                        root(i, j - 1, 8, NEWTON_OPS)

                self.loop(dve, body, back=5, ahead=1)

        S1, S2 = Edge(ES, 0, G1), Edge(ES, G1, G2)

        HW_ = CW // 2

        def ps_n(hf, m):
            return psum[:, 2 * hf + m, 0:HW_]

        def ps_u(t):
            return psum[:, 4 + t // 4, (t % 4) * P:(t % 4) * P + P]

        def ps_x(t):
            return psum[:, t % 2, 0:P]

        def ps_p(t):
            return psum[:, 6 + t % 2, :]

        def rows_of(ap, c):
            return ap[ds(c * CW, CW), :].rearrange("(t p) f -> p t f", p=P)

        class Node:

            def __init__(self, S, update, tables, final):
                self.S, self.update, self.tables, self.final = S, update, tables, final
                self.before = NCH if update else 0

            def sp(self, sp, s):
                S = self.S

                def chunk(c):
                    a = s * NCH + c
                    b = a + self.before
                    if self.update:
                        if later(c):
                            sp.wait_ge(S("hid"), 2 * a)
                            fence(sp)
                        sp.dma_start(xTc, x_cols[:, ds(c * CW, CW)]).then_inc(S("ldT"), 16)
                    if later(c):
                        sp.wait_ge(S("xT") if self.tables else S("fin"), CH * b if self.tables else c)
                        fence(sp)
                        sp.wait_ge(S("xst"), 16 * b)
                        fence(sp)
                    sp.dma_start(xc, rows_of(x_rows, c)).then_inc(S("ld"), 16)
                    if self.final:
                        sp.dma_start(x0c[:, 0:CH, :], rows_of(x0_rows, c)).then_inc(S("ld0"), 16)
                        sp.wait_ge(S("fin"), c + 1)
                        fence(sp)
                        sp.dma_start(rows_of(out_pad, c), xc).then_inc(S("xst"), 16)
                    elif self.update:
                        sp.wait_ge(S("xn"), a + 1)
                        fence(sp)
                        sp.dma_start(rows_of(x_rows, c), xc).then_inc(S("xst"), 16)
                    else:
                        sp.sem_inc(S("xst"), 16)
                    if self.tables:
                        for t in range(CH):
                            sp.wait_ge(S("plo"), CH * b + t + 1)
                            fence(sp)
                            for k, table in ((0, p_table), (1, q_table)):
                                sp.dma_start(table[ds(c * CW + t * P, P), :].rearrange("n (s e) -> n s e", s=2),
                                             pq[t % 2][:, :, k, :]).then_inc(S(f"tab{t % 2}"), 16)
                        sp.wait_ge(S("xT"), CH * b + CH)
                        fence(sp)
                        sp.dma_start(x_cols[:, ds(c * CW, CW)], xTn).then_inc(S("xTst"), 16)

                chunk(0)
                with sp.Fori(1, NCH) as c:
                    chunk(c)
                e = s * NCH + NCH + self.before
                sp.wait_ge(S("xst"), 16 * e)
                fence(sp)
                if self.tables:
                    sp.wait_ge(S("xTst"), 16 * e)
                    fence(sp)
                    sp.wait_ge(S("tab0"), 32 * 3 * e)
                    fence(sp)
                    sp.wait_ge(S("tab1"), 32 * 2 * e)
                fence(sp)

            def pe(self, pe, s):
                S = self.S

                def chunk(c):
                    a = s * NCH + c
                    b = a + self.before
                    if self.update:
                        pe.wait_ge(S("ldT"), 16 * a + 16)
                        for hf in range(2):
                            if later(c):
                                pe.wait_ge(S("act1"), 2 * a)
                            fence(pe)
                            for m in range(2):
                                for k in range(2):
                                    rhs = agg[:, ds(c * CW + hf * HW_, HW_)] if k else xTc[:, hf * HW_:(hf + 1) * HW_]
                                    x = pe.matmul(ps_n(hf, m), nw1[:, k, m * P:(m + 1) * P], rhs, start=k == 0, stop=k == 1)
                            x.then_inc(S("hid"), 1)
                        if later(c):
                            pe.wait_ge(S("xn"), a)
                        for t in range(CH):
                            pe.wait_ge(S("act1"), 2 * a + (1 if t < 2 else 2))
                            pe.matmul(ps_u(t), ones16[0:64, :], u_bias[:, :], start=True, stop=False, skip_group_check=True)
                            for k in range(2):
                                x = pe.matmul(ps_u(t), hN[:, k, t * P:(t + 1) * P], nw2[:, k, :], start=False, stop=k == 1,
                                              skip_group_check=True)
                            x.then_inc(S("u"), 1)
                    if self.tables:
                        if self.update:
                            pe.wait_ge(S("xn"), a + 1)
                        else:
                            pe.wait_ge(S("ld"), 16 * b + 16)

                        def turn(t):
                            if t >= 2:
                                pe.wait_ge(S("xT"), CH * b + t - 1)
                            elif later(c):
                                pe.wait_ge(S("xT"), CH * b)
                            pe.transpose(ps_x(t), xc[:, t, :], ident32[:, :]).then_inc(S("xTp"), 1)

                        turn(0)
                        for t in range(CH):
                            if t + 1 < CH:
                                turn(t + 1)
                            pe.wait_ge(S("xT"), CH * b + t + 1)
                            if t >= 2:
                                pe.wait_ge(S("plo"), CH * b + t - 1)
                            elif t == 0 and later(c):
                                pe.wait_ge(S("plo"), CH * b)
                            pe.matmul(ps_p(t), xTn[:, t * P:(t + 1) * P], w_pq[:, :, :].rearrange("p k h -> p (k h)"),
                                      start=True, stop=False, skip_group_check=True)
                            pe.matmul(ps_p(t)[:, 0:H], ones16[0:64, :], p_bias[:, :], start=False, stop=True,
                                      skip_group_check=True).then_inc(S("pq"), 1)

                chunk(0)
                with pe.Fori(1, NCH) as c:
                    chunk(c)

            def act(self, act, s):
                S = self.S

                def chunk(c):
                    a = s * NCH + c
                    b = a + self.before
                    if self.update:
                        if later(c):
                            act.wait_ge(S("u"), CH * a)
                        for hf in range(2):
                            act.wait_ge(S("hid"), 2 * a + hf + 1)
                            for m in range(2):
                                x = act.activation(hN[:, m, hf * HW_:(hf + 1) * HW_], ps_n(hf, m), ACT.Silu, bias=nb1_col[:, m:m + 1])
                            x.then_inc(S("act1"), 1)
                        if later(c):
                            act.wait_ge(S("xn"), a)
                        for t in range(CH):
                            act.wait_ge(S("u"), CH * a + max(t + 1, 4))
                            if t:
                                act.wait_ge(S("usq"), CH * a + t)
                            act.activation(sqn, ps_u(t), ACT.Square, accum_out=stn[:, t:t + 1]).then_inc(S("usq"), 1)
                    if self.tables:
                        if later(c):
                            act.wait_ge(S("xTst"), 16 * b)
                        for t in range(CH):
                            act.wait_ge(S("xTp"), CH * b + t + 1)
                            act.copy(xTn[:, t * P:(t + 1) * P], ps_x(t)).then_inc(S("xT"), 1)
                            if t:
                                self.hi(act, c, b, t - 1)
                        self.hi(act, c, b, CH - 1)

                chunk(0)
                with act.Fori(1, NCH) as c:
                    chunk(c)

            def hi(self, act, c, b, t):
                S = self.S
                act.wait_ge(S("pq"), CH * b + t + 1)
                if later(c) or t >= 2:
                    act.wait_ge(S(f"tab{t % 2}"), 32 * ((3 if t % 2 == 0 else 2) * b + t // 2))
                act.copy(pq[t % 2][:, 0, :, :], ps_p(t).rearrange("p (k h) -> p k h", k=2)).then_inc(S("phi"), 1)

            def dve(self, dve, s):
                S = self.S

                def chunk(c):
                    a = s * NCH + c
                    b = a + self.before
                    if self.update:
                        dve.wait_ge(S("usq"), CH * a + CH)
                        newton(dve, stn[:, 0:CH], nvn[:, 0:CH], ntn[:, 0:CH], S("newton"), NEWTON_OPS * a)
                        dve.wait_ge(S("newton"), NEWTON_OPS * a + NEWTON_OPS)
                        for t in range(CH):
                            x = dve.scalar_tensor_tensor(un[:, t, :], ps_u(t), nvn[:, t:t + 1], ng_row[:, :], ALU.mult, ALU.mult)
                        x.then_inc(S(self.cname), 1)
                        dve.wait_ge(S("ld"), 16 * b + 16)
                        nbeta_all = nbeta_row[:, :].unsqueeze(1).to_broadcast([P, CH, D])
                        base = self.dve_ops() * (c if self.final else a)
                        dve.wait_ge(S(self.cname), base + 1)
                        dve.tensor_tensor(un, un, nbeta_all, ALU.add).then_inc(S(self.cname), 1)
                        dve.wait_ge(S(self.cname), base + 2)
                        dve.tensor_tensor(xc, xc, un, ALU.add).then_inc(S("xn"), 1)
                    if self.final:
                        dve.wait_ge(S("xn"), a + 1)
                        dve.wait_ge(S("ld0"), 16 * c + 16)
                        n = [base + 2]

                        def done(i):
                            i.then_inc(S(self.cname), 1)
                            n[0] = n[0] + 1
                            dve.wait_ge(S(self.cname), n[0])
                            fence(dve)

                        done(dve.tensor_tensor(xc, xc, x0c, ALU.add))
                        for t in range(CH):
                            x = dve.bn_stats(bst[:, t, :], xc[:, t, :])
                        done(x)
                        for t in range(CH):
                            x = dve.bn_aggr(bag[:, t, :], bst[:, t, :])
                        done(x)
                        done(dve.tensor_scalar(stn[:, 0:CH], bag[:, :, 1:2].rearrange("p t s -> p (t s)"), float(D), None, ALU.mult))
                        newton(dve, stn[:, 0:CH], nvn[:, 0:CH], ntn[:, 0:CH], S("newton2"), NEWTON_OPS * c)
                        dve.wait_ge(S("newton2"), NEWTON_OPS * c + NEWTON_OPS)
                        for t in range(CH):
                            x = dve.tensor_scalar(xc[:, t, :], xc[:, t, :], bag[:, t, 0:1], nvn[:, t:t + 1], ALU.subtract, ALU.mult)
                        x.then_inc(S("fin"), 1)
                    if self.tables:
                        for t in range(CH):
                            dve.wait_ge(S("phi"), CH * b + t + 1)
                            dve.tensor_tensor(pq[t % 2][:, 1, :, :], ps_p(t).rearrange("p (k h) -> p k h", k=2),
                                              pq[t % 2][:, 0, :, :], ALU.subtract).then_inc(S("plo"), 1)

                chunk(0)
                with dve.Fori(1, NCH) as c:
                    chunk(c)

            cname = property(lambda self: "step_final" if self.final else "step")

            def dve_ops(self):
                return 6 if self.final else 2

        x0_rows = dram("x0_rows", [NPAD, D], F32)
        out_pad = dram("out_pad", [NPAD, D], F32)
        tables0 = Node(ND, False, True, False)
        node_mid = Node(ND, True, True, False)
        node_end = Node(ND, True, False, True)


        def general_or_not(eng, then, otherwise=lambda: None):
            with eng.If(eng.value_load(flag[0:1, 0:1], min_val=0, max_val=1) > 0):
                then()
            with eng.Else():
                eng.nop()
                otherwise()

        def nothing(eng, *step):
            pass

        def run(eng, setup, tables, init, init_extra, edges, edges_extra, skip, node, last_node, sp=False, dve=False):
            setup(eng)
            eng.wait_ge(phase, 1)
            tables(eng, 0)
            if sp:
                eng.sem_inc(phase, 1)
            eng.wait_ge(phase, 2)
            init(eng)
            if sp:
                eng.sem_inc(phase, 1)
            eng.wait_ge(phase, 3)
            general_or_not(eng, lambda: init_extra(eng))
            if sp:
                eng.dma_start(degree, agg[:, :]).then_inc(SU("deg"), 16)
                eng.wait_ge(SU("deg"), 16)
                eng.sem_inc(phase, 1)

            def step(s, node):
                eng.wait_ge(phase, 4 + 3 * s)
                fence(eng)
                if sp:
                    eng.dma_start(agg[:, :], degree).then_inc(SU("degin"), 16)
                if dve:
                    k = SU("bias")
                    dve_b = s * 5
                    eng.tensor_tensor(beta_sum[:, :], beta_sum[:, :], beta_col[:, :], ALU.add).then_inc(k, 1)
                    eng.tensor_tensor(p_bias32[:, :], p_bias32[:, :], beta_w1[:, :], ALU.add).then_inc(k, 1)
                    eng.wait_ge(k, dve_b + 2)
                    n = [dve_b + 2]

                    def done(i):
                        i.then_inc(k, 1)
                        n[0] = n[0] + 1
                        eng.wait_ge(k, n[0])

                    pair_p_bias(done, eng)
                    eng.wait_ge(SU("degin"), 16 * s + 16)
                    eng.tensor_scalar(agg[:, :], agg[:, :], beta_sum[:, :], None, ALU.mult).then_inc(SU("seeded"), 1)
                    eng.wait_ge(SU("seeded"), s + 1)
                edges(eng, s)
                if sp:
                    eng.sem_inc(phase, 1)
                eng.wait_ge(phase, 4 + 3 * s + 1)
                fence(eng)
                general_or_not(eng, lambda: edges_extra(eng, s), lambda: skip(eng))
                if sp:
                    eng.sem_inc(phase, 1)
                eng.wait_ge(phase, 4 + 3 * s + 2)
                fence(eng)
                node(eng, s)
                if sp:
                    eng.sem_inc(phase, 1)

            with eng.Fori(0, STEPS - 1) as s:
                step(s, node)
            step(STEPS - 1, last_node)
            if sp:
                eng.dma_start(out, out_pad[0:N, :]).then_inc(SU("out"), 16)
                eng.wait_ge(SU("out"), 16)

        def setup_sp2(sp):
            sp.dma_start(x0_rows[0:N, :], x_in).then_inc(SU("x0"), 16)
            sp.wait_ge(SU("dvezero"), 1)
            sp.dma_start(x0_rows[N:NPAD, :], zero[0:NPAD - N, 0:D]).then_inc(SU("x0"), 16)
            sp.wait_ge(SU("x0"), 32)
            setup_sp(sp)

        @block.sync
        def _(sp):
            run(sp, setup_sp2, tables0.sp, I1.sp, I2.sp, S1.sp, S2.sp, S2.skip_sp, node_mid.sp, node_end.sp, sp=True)

        @block.gpsimd
        def _(pool):
            run(pool, setup_pool, nothing, nothing, nothing, S1.pool, S2.pool, S2.skip_pool, nothing, nothing)

        @block.vector
        def _(dve):
            run(dve, setup_dve, tables0.dve, I1.dve, I2.dve, S1.dve, S2.dve, S2.skip_dve, node_mid.dve, node_end.dve, dve=True)

        @block.scalar
        def _(act):
            run(act, nothing, tables0.act, I1.act, I2.act, S1.act, S2.act, S2.skip_act, node_mid.act, node_end.act)

        @block.tensor
        def _(pe):
            run(pe, setup_pe, tables0.pe, I1.pe, I2.pe, S1.pe, S2.pe, S2.skip_pe, node_mid.pe, node_end.pe)


_INS = ['x', 'src', 'dst', 'edge_attr_4', 'L0_gnn_enc_W', 'L0_gnn_enc_b', 'L0_gnn_eW1', 'L0_gnn_eb1',
        'L0_gnn_eW2', 'L0_gnn_eb2', 'L0_gnn_eg', 'L0_gnn_ebeta', 'L0_gnn_nW1', 'L0_gnn_nb1', 'L0_gnn_nW2',
        'L0_gnn_nb2', 'L0_gnn_ng', 'L0_gnn_nbeta']


def kernel(**inputs):
    import numpy as _np
    import concourse.bacc as _bacc
    from concourse import mybir as _mybir
    from concourse.bass_utils import run_bass_kernel_spmd as _run

    nc = _bacc.Bacc("TRN2", target_bir_lowering=False, num_devices=1)
    arrays, args = {}, []
    for name in _INS:
        a = _np.ascontiguousarray(inputs[name])
        arrays[f"in_{name}"] = a
        args.append(nc.dram_tensor(f"in_{name}", a.shape, _mybir.dt.from_np(a.dtype), kind="ExternalInput").ap())
    args.append(nc.dram_tensor("out_0", (N, D), _mybir.dt.float32, kind="ExternalOutput").ap())
    build_program(nc, *args)
    r = _run(nc, [arrays], core_ids=[0])
    return r.results[0]["out_0"]
```

```python
from contextlib import ExitStack

import concourse.bass as bass
from concourse import mybir

F32, F16, F8, I32 = mybir.dt.float32, mybir.dt.float16, mybir.dt.float8e4, mybir.dt.int32
ALU = mybir.AluOpType
ACT = mybir.ActivationFunctionType
AX = mybir.AxisListType
ds = bass.ds

P = 128
N, E = 3125, 50000
D, H, RAW, STEPS, EPS = 128, 256, 4, 4, 1e-5
TPG = 4
GE = TPG * P
G1 = -(-E // GE)
NT = -(-N // P)
NPAD = NT * P
G2 = (E + NT * (GE - 1)) // GE
G2 += G2 % 2
LAST = E - (G1 - 1) * GE
CH = 5
NCH = NT // CH
CW = CH * P
EP, EC = 125, 400
R = 4
SORT = 15616
SCRATCH = SORT + GE * 12
ARENA = SCRATCH + 4400
RSQRT_SEED = float(0x5F3759DF)
NEWTON = 3
NEWTON_OPS = 2 + 3 * NEWTON


def build_program(nc, x_in, src_in, dst_in, attr_in, enc_W, enc_b, eW1, eb1, eW2, eb2, eg, ebeta,
                  nW1, nb1, nW2, nb2, ng, nbeta, out):
    ctx = ExitStack()
    with ctx:
        def sb(name, shape, dt):
            return ctx.enter_context(nc.sbuf_tensor(name, shape, dt))

        def sem(name):
            return ctx.enter_context(nc.semaphore(name))

        def dram(name, shape, dt):
            return nc.dram_tensor(name, shape, dt, kind="Internal").ap()

        p_table = dram("p_table", [NPAD, 2 * H], F16)
        q_table = dram("q_table", [NPAD, 2 * H], F16)
        matrices = dram("matrices", [G2, P, GE // 2], F32)
        state = dram("state", [G2, P, TPG * 2 * D], F16)
        rel_rows = dram("rel_rows", [G2, GE], F16)
        attr_p = dram("attr_p", [G2 * GE, RAW], F32)
        records = dram("records", [G2 * GE, 8], I32)

        agg = sb("agg", [P, NPAD], F32)
        degree = sb("degree", [P, NPAD], F32)
        x0_all = sb("x0_all", [P, NT, D], F32)
        x_all = sb("x_all", [P, NT, D], F32)
        xT_all = sb("xT_all", [P, NPAD], F32)
        idx_all = sb("idx_all", [P, G2, TPG], I32)
        rel_all = sb("rel_all", [P, TPG, P], F32)
        win = sb("win", [1, P], I32)
        flag = sb("flag", [1, 1], I32)
        w1_hi = sb("w1_hi", [P, H], F16)
        w1_lo = sb("w1_lo", [P, H], F16)
        w2_hi = sb("w2_hi", [P, 2, D], F16)
        w2_lo = sb("w2_lo", [P, 2, D], F16)
        v_bias = sb("v_bias", [64, GE], F16)
        g_row = sb("g_row", [P, D], F32)
        nw1 = sb("nw1", [P, 2, H], F32)
        nw2 = sb("nw2", [P, 2, D], F32)
        w_pq = sb("w_pq", [P, 2, H], F32)
        nb1_col = sb("nb1_col", [P, 2], F32)
        u_bias = sb("u_bias", [64, D], F16)
        ng_row = sb("ng_row", [P, D], F32)
        nbeta_row = sb("nbeta_row", [P, D], F32)
        p_bias = sb("p_bias", [64, H], F16)
        p_bias32 = sb("p_bias32", [1, H], F32)
        beta_w1 = sb("beta_w1", [1, H], F32)
        beta_col = sb("beta_col", [P, 1], F32)
        beta_sum = sb("beta_sum", [P, 1], F32)
        ones16 = sb("ones16", [P, P], F16)
        ident16 = sb("ident16", [P, P], F16)
        ident32 = sb("ident32", [P, P], F32)
        node_iota = sb("node_iota", [P, P], F16)
        part_iota = sb("part_iota", [P, 1], F32)
        enc_bd = sb("enc_bd", [TPG * RAW + 1, TPG, D], F32)
        enc16 = sb("enc16", [3 * 32, TPG * D], F16)

        arena = sb("arena", [P, ARENA], F32)
        cut = [0]

        def take(words, dt=F32):
            a = cut[0]
            cut[0] += words
            assert cut[0] <= ARENA, cut[0]
            v = arena[:, a:a + words]
            return v if dt == F32 else v.bitcast(dt)

        h32 = [take(2 * GE).rearrange("p (k e) -> p k e", k=2) for _ in range(2)]
        hh = [take(GE, F16).rearrange("p (k e) -> p k e", k=2) for _ in range(2)]
        hl = [take(GE, F16).rearrange("p (k e) -> p k e", k=2) for _ in range(2)]
        st_in = [take(GE, F16).rearrange("p (t c) -> p t c", t=TPG) for _ in range(R)]
        st_out = [take(GE, F16).rearrange("p (t c) -> p t c", t=TPG) for _ in range(R)]
        resid = [take(GE) for _ in range(R)]
        e_new = [take(GE) for _ in range(2)]
        sq = [take(GE) for _ in range(2)]
        rows = [take(TPG * H, F16).rearrange("p (t c) -> p t c", t=TPG) for _ in range(R)]
        q_win = [take(H, F16) for _ in range(R)]
        eT = [take(GE, F16).rearrange("p (k e) -> p k e", k=2) for _ in range(2)]
        oh = [take(GE // 4, F8) for _ in range(R)]
        oht = [take(GE // 4, F8) for _ in range(R)]
        nv = [take(TPG) for _ in range(2)]
        rs = [take(TPG) for _ in range(2)]
        nt = [take(TPG) for _ in range(2)]
        idx_now = [take(TPG, I32) for _ in range(R)]
        cut[0] = 0
        hN = [take(2 * CW).rearrange("p (k e) -> p k e", k=2) for _ in range(2)]
        un = take(CW).rearrange("p (t f) -> p t f", t=CH)
        sqn = [take(CW) for _ in range(2)]
        stn = [take(8) for _ in range(2)]
        nvn = take(8)
        ntn = take(8)
        bst = take(CH * 6).rearrange("p (t s) -> p t s", t=CH)
        bag = take(CH * 2).rearrange("p (t s) -> p t s", t=CH)
        vf = take(CH)
        nvf = take(CH)
        ntf = take(CH)
        xf = [take(CW).rearrange("p (t f) -> p t f", t=CH) for _ in range(2)]
        pq = [take(2 * H, F16).rearrange("p (s k e) -> p s k e", s=2, k=2) for _ in range(CH)]
        cut[0] = 0
        at_in = [take(TPG * RAW + 1) for _ in range(R)]
        at16 = [take(P // 2, F16) for _ in range(2)]
        e0 = [take(GE) for _ in range(R)]
        st0 = [take(GE, F16).rearrange("p (t c) -> p t c", t=TPG) for _ in range(R)]
        rel_b = [take(GE // 2, F16) for _ in range(R)]
        rel_now = [take(TPG) for _ in range(R)]
        assert cut[0] <= SCRATCH
        both0 = [take(GE // 2) for _ in range(R)]
        oh0 = [x[:, 0:GE // 4].bitcast(F8) for x in both0]
        oht0 = [x[:, GE // 4:GE // 2].bitcast(F8) for x in both0]
        cut[0] = SCRATCH
        d_grp = take(GE)
        s_grp = take(GE)
        d_int = take(GE, I32)
        s_int = take(GE, I32)
        rel16 = take(GE // 2, F16)
        tmpw = take(GE)
        tmpv = take(GE)
        red = take(16)
        zero = take(GE)
        cut[0] = 0
        gp = arena[:, 0:SORT]
        gcut = [0]

        def gtake(words, dt=F32):
            a = gcut[0]
            gcut[0] += words
            assert gcut[0] <= SORT
            v = gp[:, a:a + words]
            return v if dt == F32 else v.bitcast(dt)

        g_rec = gtake(EC * 8, I32).rearrange("p (e w) -> p e w", w=8)
        g_dst = gtake(EC, I32)
        g_src = gtake(EC, I32)
        g_attr = gtake(EC * RAW, I32).rearrange("p (e w) -> p e w", w=RAW)
        g_q = gtake(EC)
        g_mask = gtake(EC)
        g_scan = gtake(EC)
        g_acc = gtake(EC)
        g_pos = gtake(EC, I32)
        g_ones = gtake(EC)
        g_cnt = gtake(NT)
        g_tot = gtake(NT)
        g_off = gtake(NT)
        g_int = gtake(NT, I32)
        g_tri = gtake(P)
        g_fill = gtake(8 * 8, I32)
        g_stage = [gtake(8, I32) for _ in range(2)]
        g_spos = [gtake(2, I32)[:, 0:1] for _ in range(2)]
        g2 = arena[:, SORT:SCRATCH].bitcast(I32)
        g_all = g2[0:G2, 0:GE * 8].rearrange("p (e w) -> p e w", w=8)
        g_attr2 = g2[0:G2, GE * 8:GE * 12].rearrange("p (e w) -> p e w", w=RAW)

        psum = ctx.enter_context(nc.psum_tensor("psum", [P, 8, 512], F32))

        def ps_h(k):
            return psum[:, 2 * k:2 * k + 2, :]

        def ps_v(k):
            return psum[:, 4 + k, :]

        ps_t = psum[:, 6, :].bitcast(F16)
        ps_a = psum[:, 7, :]

        class Sems:

            def __init__(self, prefix):
                self.prefix, self.made = prefix, {}

            def __call__(self, name):
                if name not in self.made:
                    self.made[name] = sem(f"{self.prefix}_{name}")
                return self.made[name]

        SU = Sems("setup")
        GS = Sems("general")
        Z = Sems("init")
        ES = Sems("edge")
        ND = Sems("node")
        fenced = sem("fenced")
        phase = sem("phase")

        block = ctx.enter_context(nc.Block())

        def later(i):
            return not (isinstance(i, int) and i == 0)

        def fence(eng):
            eng.sem_inc(fenced, 1)

        def newton(dve, v, y, tmp, chain, base, a=0, b=NEWTON_OPS):
            for n in range(a, b):
                if n > 0:
                    dve.wait_ge(chain, base + n)
                if n == 0:
                    x = dve.tensor_scalar(v, v, 1.0 / D, EPS, ALU.mult, ALU.add)
                elif n == 1:
                    x = dve.tensor_scalar(y.bitcast(I32), v.bitcast(I32), -0.5, RSQRT_SEED, ALU.mult, ALU.add)
                elif n % 3 == 2:
                    x = dve.tensor_tensor(tmp, y, y, ALU.mult)
                elif n % 3 == 0:
                    x = dve.scalar_tensor_tensor(tmp, tmp, -0.5, v, ALU.mult, ALU.mult)
                else:
                    x = dve.scalar_tensor_tensor(y, tmp, 1.5, y, ALU.add, ALU.mult)
                x.then_inc(chain, 1)

        def setup_sp(sp):
            def load(dst, src, name="w"):
                sp.dma_start(dst, src).then_inc(SU(name), 16)

            sp.wait_ge(SU("pads"), 2)
            load(d_int[0:G1 - 1, :], dst_in[0:(G1 - 1) * GE].rearrange("(g e) -> g e", e=GE), "dst")
            load(d_int[G1 - 1:G1, 0:LAST], dst_in[(G1 - 1) * GE:E].rearrange("(g e) -> g e", g=1), "dst")
            load(s_int[0:G1 - 1, :], src_in[0:(G1 - 1) * GE].rearrange("(g e) -> g e", e=GE), "src")
            load(s_int[G1 - 1:G1, 0:LAST], src_in[(G1 - 1) * GE:E].rearrange("(g e) -> g e", g=1), "src")
            load(w_pq[:, 0, :], eW1[D:2 * D, :], "w")
            load(w_pq[:, 1, :], eW1[2 * D:3 * D, :], "w")
            load(tmpw[:, 0:H], eW1[0:D, :], "w")
            load(tmpv[:, 0:2 * D].rearrange("p (k f) -> p k f", k=2), eW2.rearrange("(k p) f -> p k f", k=2), "w")
            load(nw1[:, :, :], nW1.rearrange("(k p) f -> p k f", k=2), "w")
            load(nw2[:, :, :], nW2.rearrange("(k p) f -> p k f", k=2), "w")
            load(g_row[:, :], eg.partition_broadcast(P), "w")
            load(ng_row[:, :], ng.partition_broadcast(P), "w")
            load(nbeta_row[:, :], nbeta.partition_broadcast(P), "w")
            for k in range(2):
                load(nb1_col[:, k:k + 1], nb1[k * P:(k + 1) * P].rearrange("(p a) -> p a", a=1), "w")
            load(beta_col[:, :], ebeta.rearrange("(p a) -> p a", a=1), "w")
            load(p_bias32[:, :], eb1.rearrange("(a f) -> a f", a=1), "w")
            load(tmpv[0:1, 2 * D:3 * D], eb2.rearrange("(a f) -> a f", a=1), "w")
            load(tmpv[0:1, 3 * D:4 * D], nb2.rearrange("(a f) -> a f", a=1), "w")
            sp.wait_ge(SU("zeroed"), 1)
            for t in range(TPG):
                load(enc_bd[t * RAW:(t + 1) * RAW, t, :], enc_W, "w")
                load(enc_bd[TPG * RAW:TPG * RAW + 1, t, :], enc_b.rearrange("(a f) -> a f", a=1), "w")
            sp.wait_ge(SU("xzero"), 2)
            whole = N // P
            for t in range(0, whole, 4):
                load(x0_all[:, t:t + 4, :], x_in[t * P:(t + 4) * P, :].rearrange("(t p) f -> p t f", p=P), "x")
            load(x0_all[0:N - whole * P, whole, :], x_in[whole * P:N, :], "x")
            sp.wait_ge(SU("flag"), 1)
            with sp.If(sp.value_load(flag[0:1, 0:1], min_val=0, max_val=1) > 0):
                general_sp(sp)
            with sp.Else():
                sp.dma_start(attr_p[0:E, :].rearrange("e w -> (e w)").rearrange("(a b) -> a b", a=100),
                             attr_in.rearrange("e w -> (e w)").rearrange("(a b) -> a b", a=100)).then_inc(SU("attr"), 16)
                sp.dma_start(attr_p[E:G1 * GE, :].rearrange("e w -> (e w)").rearrange("(a b) -> a b", a=16),
                             zero[0:16, 0:(G1 * GE - E) * RAW // 16]).then_inc(SU("attr"), 16)
                sp.wait_ge(SU("attr"), 32)
            sp.wait_ge(SU("rel"), 1)
            sp.dma_start(rel_rows[:, :], rel16[0:G2, :]).then_inc(SU("relrow"), 16)
            sp.wait_ge(SU("relrow"), 16)
            sp.wait_ge(SU("cols"), 3)
            sp.wait_ge(SU("weights"), 1)
            sp.wait_ge(SU("xcopy"), 1)
            sp.sem_inc(phase, 1)

        NW = 16 * (15 + 2 * TPG)

        def general_sp(sp):
            sp.dma_start(g_dst[0:EP, :], dst_in.rearrange("(p e) -> p e", p=EP)).then_inc(GS("in"), 16)
            sp.dma_start(g_src[0:EP, :], src_in.rearrange("(p e) -> p e", p=EP)).then_inc(GS("in"), 16)
            sp.dma_start(g_attr[0:EP, :, :], attr_in.rearrange("(p e) w -> p e w", p=EP).bitcast(I32)).then_inc(GS("in"), 16)
            sp.wait_ge(GS("fill"), 1)
            rows_a = records.rearrange("(a b) w -> a (b w)", b=8)
            for a in range(0, G2 * GE // 8, P):
                n = min(P, G2 * GE // 8 - a)
                sp.dma_start(rows_a[a:a + n, :], g_fill[0:n, :]).then_inc(GS("filled"), 16)
            sp.wait_ge(GS("filled"), 16 * len(range(0, G2 * GE // 8, P)))
            sp.sem_inc(GS("ready"), 1)
            sp.wait_ge(GS("sorted"), 1)
            sp.dma_start(g_all, records.rearrange("(g e) w -> g e w", e=GE)).then_inc(GS("back"), 16)
            sp.wait_ge(GS("attr"), 1)
            sp.dma_start(attr_p.rearrange("(g e) w -> g e w", e=GE).bitcast(I32), g_attr2).then_inc(GS("attr_out"), 16)
            sp.wait_ge(GS("attr_out"), 16)

        def setup_pool(pool):
            pool.memset(d_int[:, :], 1 << 20).then_inc(SU("pads"), 1)
            pool.memset(s_int[:, :], 0).then_inc(SU("pads"), 1)
            pool.memset(enc_bd[:, :, :], 0.0).then_inc(SU("zeroed"), 1)
            pool.memset(ones16[:, :], 1.0).then_inc(SU("const"), 1)
            pool.memset(ident32[:, :], 0.0).then_inc(SU("ident"), 1)
            pool.iota(part_iota[:, :], pattern=[[0, 1]], base=0, channel_multiplier=1,
                      allow_small_or_imprecise_dtypes=True).then_inc(SU("const"), 1)
            pool.iota(node_iota[:, :], pattern=[[1, P]], base=0, channel_multiplier=0,
                      allow_small_or_imprecise_dtypes=True).then_inc(SU("const"), 1)
            pool.wait_ge(SU("ident"), 1)
            pool.affine_select(out=ident32[:, :], in_=ident32[:, :], compare_op=ALU.not_equal, fill=1.0,
                               base=0, pattern=[[-1, P]], channel_multiplier=1).then_inc(SU("ident"), 1)
            pool.wait_ge(SU("flag"), 1)
            with pool.If(pool.value_load(flag[0:1, 0:1], min_val=0, max_val=1) > 0):
                general_pool(pool)
            with pool.Else():
                pool.nop()

        def general_pool(pool):
            pool.memset(g_tri[:, :], 1.0).then_inc(GS("tri"), 1)
            pool.wait_ge(GS("tri"), 1)
            pool.affine_select(out=g_tri[:, :], in_=g_tri[:, :], compare_op=ALU.is_ge, fill=0.0,
                               base=-1, pattern=[[1, P]], channel_multiplier=-1).then_inc(GS("tri"), 1)
            pool.wait_ge(GS("pos"), 1)
            pool.wait_ge(GS("ready"), 1)
            def column_pair(j):
                for k in range(2):
                    if later(j):
                        pool.wait_ge(GS(f"put{k}"), 16 * j)
                    pool.tensor_copy(g_stage[k], g_rec[:, ds(2 * j + k, 1), :].rearrange("p a w -> p (a w)")).then_inc(GS("staged"), 1)
                    pool.tensor_copy(g_spos[k], g_pos[:, ds(2 * j + k, 1)]).then_inc(GS("staged"), 1)
                    pool.wait_ge(GS("staged"), 4 * j + 2 * k + 2)
                    fence(pool)
                    pool.indirect_dma_start(out=records, out_offset=bass.IndirectOffsetOnAxis(ap=g_spos[k][0:EP, :], axis=0),
                                            in_=g_stage[k][0:EP, :], in_offset=None).then_inc(GS(f"put{k}"), 16)

            column_pair(0)
            with pool.Fori(1, EC // 2) as j:
                column_pair(j)
            for k in range(2):
                pool.wait_ge(GS(f"put{k}"), 16 * (EC // 2))
            pool.sem_inc(GS("sorted"), 1)

        def setup_dve(dve):
            chain = SU("dve")
            n = [0]

            def done(i):
                i.then_inc(chain, 1)
                n[0] += 1
                dve.wait_ge(chain, n[0])

            done(dve.memset(red, 0.0))
            dve.memset(zero, 0.0).then_inc(SU("xzero"), 1)
            done(dve.memset(p_bias[:, :], 0.0))
            done(dve.memset(v_bias[:, :], 0.0))
            done(dve.memset(u_bias[:, :], 0.0))
            done(dve.memset(degree[:, :], 0.0))
            dve.memset(x0_all[:, N // P, :], 0.0).then_inc(SU("xzero"), 1)
            done(dve.memset(rel_all[:, :, :], 0.0))
            done(dve.memset(beta_sum[:, :], 0.0))
            dve.wait_ge(SU("dst"), 32)
            dve.wait_ge(SU("ident"), 2)
            done(dve.tensor_copy(ident16[:, :], ident32[:, :]))
            done(dve.tensor_copy(d_grp, d_int))
            done(dve.tensor_reduce(red[:, 0:1], d_grp, AX.X, ALU.min))
            done(dve.tensor_scalar(red[:, 0:1], red[:, 0:1], float(N - P), None, ALU.min))
            done(dve.tensor_reduce(red[0:G1, 1:2], d_grp[0:G1, 0:LAST], AX.X, ALU.max))
            done(dve.tensor_reduce(red[0:G1 - 1, 2:3], d_grp[0:G1 - 1, LAST:GE], AX.X, ALU.max))
            done(dve.tensor_tensor(red[0:G1, 1:2], red[0:G1, 1:2], red[0:G1, 2:3], ALU.max))
            done(dve.tensor_tensor(red[0:G1, 3:4], red[0:G1, 1:2], red[0:G1, 0:1], ALU.subtract))
            dve.sem_inc(SU("width"), 1)
            dve.wait_ge(SU("widthT"), 1)
            done(dve.tensor_reduce(red[0:1, 4:5], psum[0:1, 0, 0:G1], AX.X, ALU.max))
            dve.tensor_scalar(flag[0:1, 0:1], red[0:1, 4:5], float(P - 1), None, ALU.is_gt).then_inc(SU("flag"), 1)
            dve.wait_ge(SU("flag"), 1)
            with dve.If(dve.value_load(flag[0:1, 0:1], min_val=0, max_val=1) > 0):
                general_dve(dve)
            with dve.Else():
                dve.nop()
            c2 = SU("dve2")
            m = [0]

            def done2(i):
                i.then_inc(c2, 1)
                m[0] += 1
                dve.wait_ge(c2, m[0])

            dve.wait_ge(SU("src"), 32)
            done2(dve.tensor_copy(d_grp, d_int))
            done2(dve.tensor_copy(s_grp, s_int))
            done2(dve.tensor_reduce(red[:, 0:1], d_grp, AX.X, ALU.min))
            done2(dve.tensor_scalar(red[:, 0:1], red[:, 0:1], float(N - P), None, ALU.min))
            done2(dve.tensor_scalar(d_grp, d_grp, red[:, 0:1], 255.0, ALU.subtract, ALU.min))
            dve.tensor_copy(rel16.rearrange("g (t p) -> g t p", t=TPG),
                            d_grp.rearrange("g (p t) -> g t p", t=TPG)).then_inc(SU("rel"), 1)
            dve.sem_inc(SU("grp"), 1)
            dve.wait_ge(SU("relT"), 1)
            dve.tensor_copy(rel_all[:, :, 0:G2], psum[:, 2, :].rearrange("p (t g) -> p t g", t=TPG)[:, :, 0:G2]).then_inc(SU("cols"), 1)
            dve.wait_ge(SU("srcT"), 1)
            dve.tensor_copy(idx_all[:, :, :].rearrange("p g t -> p t g"),
                            psum[:, 3, :].rearrange("p (t g) -> p t g", t=TPG)[:, :, 0:G2]).then_inc(SU("cols"), 1)
            dve.wait_ge(SU("winT"), 1)
            dve.tensor_copy(win[0:1, 0:G2], psum[0:1, 0, 128:128 + G2]).then_inc(SU("cols"), 1)
            dve.wait_ge(SU("w"), NW)
            done(dve.tensor_copy(w1_hi[:, :], tmpw[:, 0:H]))
            done(dve.tensor_tensor(w1_lo[:, :], tmpw[:, 0:H], w1_hi[:, :], ALU.subtract))
            w2 = tmpv[:, 0:2 * D].rearrange("p (k f) -> p k f", k=2)

            def centre(w, cols):
                done(dve.tensor_reduce(cols, w, AX.X, ALU.add))
                done(dve.tensor_scalar(cols, cols, -1.0 / D, None, ALU.mult))

            enc = enc_bd[:, :, :].rearrange("a t f -> a (t f)")
            rows17 = TPG * RAW + 1
            done(dve.memset(enc16[:, :], 0.0))
            for row in (0, 64):
                done(dve.tensor_copy(enc16[row:row + rows17, :], enc))
            done(dve.tensor_tensor(enc16[32:32 + rows17, :], enc, enc16[0:rows17, :], ALU.subtract))
            centre(w2, red[:, 5:7])
            for k in range(2):
                done(dve.tensor_scalar(w2[:, k, :], w2[:, k, :], red[:, 5 + k:6 + k], None, ALU.add))
            done(dve.tensor_copy(w2_hi[:, :, :], w2))
            done(dve.tensor_tensor(w2_lo[:, :, :], w2, w2_hi[:, :, :], ALU.subtract))
            centre(nw2[:, :, :], red[:, 7:9])
            for k in range(2):
                done(dve.tensor_scalar(nw2[:, k, :], nw2[:, k, :], red[:, 7 + k:8 + k], None, ALU.add))
            for row, bias, reps in ((2, v_bias, TPG), (3, u_bias, 1)):
                b = tmpv[0:1, row * D:(row + 1) * D]
                centre(b, red[0:1, 9:10])
                done(dve.tensor_scalar(b, b, red[0:1, 9:10], None, ALU.add))
                for r in range(reps):
                    done(dve.tensor_copy(bias[0:1, r * D:(r + 1) * D], b))
                for r in range(reps):
                    done(dve.tensor_tensor(d_row[0:1, 0:D], b, bias[0:1, 0:D], ALU.subtract))
                    done(dve.tensor_copy(bias[32:33, r * D:(r + 1) * D], d_row[0:1, 0:D]))
            dve.wait_ge(SU("betaw"), 1)
            done(dve.tensor_copy(beta_w1[:, :], psum[0:1, 1, 0:H]))
            pair_p_bias(done, dve)
            dve.sem_inc(SU("weights"), 1)

        d_row = sb("d_row", [1, H], F32)

        def pair_p_bias(done, dve):
            done(dve.tensor_copy(p_bias[0:1, :], p_bias32[:, :]))
            done(dve.tensor_tensor(d_row[:, :], p_bias32[:, :], p_bias[0:1, :], ALU.subtract))
            done(dve.tensor_copy(p_bias[32:33, :], d_row[:, :]))

        def general_dve(dve):
            c = GS("dve")
            n = [0]

            def done(i):
                i.then_inc(c, 1)
                n[0] += 1
                dve.wait_ge(c, n[0])

            fill = g_fill.rearrange("p (e w) -> p e w", w=8)
            done(dve.memset(fill, 0))
            dve.memset(fill[:, :, 1:2], 1 << 20).then_inc(GS("fill"), 1)
            done(dve.memset(g_rec, 0))
            done(dve.memset(g_pos, 0))
            done(dve.memset(g_ones, 1.0))
            done(dve.memset(g_acc, 0.0))
            dve.wait_ge(GS("in"), 48)
            done(dve.tensor_copy(g_rec[0:EP, :, 0:1].rearrange("p e w -> p (e w)"), g_src[0:EP, :]))
            done(dve.tensor_copy(g_rec[0:EP, :, 1:2].rearrange("p e w -> p (e w)"), g_dst[0:EP, :]))
            done(dve.tensor_copy(g_rec[0:EP, :, 2:2 + RAW], g_attr[0:EP, :, :]))
            done(dve.tensor_scalar(g_dst[0:EP, :], g_dst[0:EP, :], 7, None, ALU.logical_shift_right))
            done(dve.tensor_copy(g_q[0:EP, :], g_dst[0:EP, :]))
            for b in range(NT):
                done(dve.tensor_scalar(g_mask[0:EP, :], g_q[0:EP, :], float(b), None, ALU.is_equal))
                done(dve.tensor_tensor_scan(g_scan[0:EP, :], g_ones[0:EP, :], g_mask[0:EP, :], 0.0, ALU.mult, ALU.add))
                done(dve.tensor_copy(g_cnt[0:EP, b:b + 1], g_scan[0:EP, EC - 1:EC]))
                done(dve.tensor_tensor(g_scan[0:EP, :], g_scan[0:EP, :], g_mask[0:EP, :], ALU.mult))
                done(dve.tensor_tensor(g_acc[0:EP, :], g_acc[0:EP, :], g_scan[0:EP, :], ALU.add))
            dve.sem_inc(GS("counts"), 1)
            dve.wait_ge(GS("sums"), 1)
            done(dve.tensor_scalar(g_tot[0:EP, :], psum[0:EP, 1, 0:NT], float(GE - 1), None, ALU.add))
            done(dve.tensor_copy(g_int[0:EP, :], g_tot[0:EP, :]))
            done(dve.tensor_scalar(g_int[0:EP, :], g_int[0:EP, :], 9, 9, ALU.logical_shift_right, ALU.logical_shift_left))
            done(dve.tensor_copy(g_tot[0:EP, :], g_int[0:EP, :]))
            done(dve.tensor_tensor_scan(g_off[0:EP, :], g_ones[0:EP, 0:NT], g_tot[0:EP, :], 0.0, ALU.mult, ALU.add))
            done(dve.tensor_tensor(g_off[0:EP, :], g_off[0:EP, :], g_tot[0:EP, :], ALU.subtract))
            done(dve.tensor_tensor(g_off[0:EP, :], g_off[0:EP, :], psum[0:EP, 0, 0:NT], ALU.add))
            for b in range(NT):
                done(dve.tensor_scalar(g_mask[0:EP, :], g_q[0:EP, :], float(b), g_off[0:EP, b:b + 1], ALU.is_equal, ALU.mult))
                done(dve.tensor_tensor(g_acc[0:EP, :], g_acc[0:EP, :], g_mask[0:EP, :], ALU.add))
            dve.tensor_scalar(g_pos[0:EP, :], g_acc[0:EP, :], -1.0, None, ALU.add).then_inc(GS("pos"), 1)
            dve.wait_ge(GS("back"), 16)
            dve.tensor_copy(g_attr2, g_all[:, :, 2:2 + RAW]).then_inc(GS("attr"), 1)
            done(dve.tensor_copy(d_int[0:G2, :], g_all[:, :, 1:2].rearrange("p e w -> p (e w)")))
            done(dve.tensor_copy(s_int[0:G2, :], g_all[:, :, 0:1].rearrange("p e w -> p (e w)")))

        def setup_act(act):
            act.wait_ge(SU("x"), 16 * (N // P // 4 + 1))
            act.copy(x_all[:, :, :], x0_all[:, :, :]).then_inc(SU("xcopy"), 1)

        def setup_pe(pe):
            pe.wait_ge(SU("ident"), 2)
            pe.wait_ge(SU("width"), 1)
            pe.transpose(psum[0:1, 0, 0:P], red[:, 3:4], ident32[:, :]).then_inc(SU("widthT"), 1)
            pe.wait_ge(SU("flag"), 1)
            with pe.If(pe.value_load(flag[0:1, 0:1], min_val=0, max_val=1) > 0):
                pe.wait_ge(GS("counts"), 1)
                pe.wait_ge(GS("tri"), 2)
                pe.matmul(psum[:, 0, 0:NT], g_tri[0:EP, :], g_cnt[0:EP, :], start=True, stop=True)
                pe.matmul(psum[0:EP, 1, 0:NT], g_ones[0:EP, 0:EP], g_cnt[0:EP, :], start=True, stop=True).then_inc(GS("sums"), 1)
            with pe.Else():
                pe.nop()
            pe.wait_ge(SU("grp"), 1)
            for t in range(TPG):
                i = pe.transpose(psum[:, 2, t * P:(t + 1) * P], d_grp.rearrange("g (p t) -> g t p", t=TPG)[:, t, :], ident32[:, :])
            i.then_inc(SU("relT"), 1)
            for t in range(TPG):
                i = pe.transpose(psum[:, 3, t * P:(t + 1) * P], s_grp.rearrange("g (p t) -> g t p", t=TPG)[:, t, :], ident32[:, :])
            i.then_inc(SU("srcT"), 1)
            pe.transpose(psum[0:1, 0, P:2 * P], red[:, 0:1], ident32[:, :]).then_inc(SU("winT"), 1)
            pe.wait_ge(SU("w"), NW)
            pe.matmul(psum[0:1, 1, 0:H], beta_col[:, :], tmpw[:, 0:H], start=True, stop=True).then_inc(SU("betaw"), 1)

        class Groups:

            def __init__(self, S, lo, hi):
                self.S, self.lo, self.hi = S, lo, hi

            def loop(self, eng, body, back, ahead):
                start, end = self.lo // R, -(-(self.hi + back) // R)
                first = -(-(self.lo + back) // R)
                last = (self.hi - R - ahead) // R + 1
                for i in range(start, first):
                    body(i)
                with eng.Fori(first, last) as i:
                    body(i)
                for i in range(last, end):
                    body(i)

            def has(self, i, off):
                return not isinstance(i, int) or self.lo <= R * i + off < self.hi

            def runs(self, i, j):
                return not isinstance(i, int) or R * i + j >= self.lo

        class Init(Groups):

            def group(self, ap, i, off):
                return ap[ds(R * i + off, 1), :, :].rearrange("a p c -> (a p) c")

            def sp(self, sp):
                S = self.S
                c = lambda i, off: R * i + off + 1
                ring = lambda i, off: i + off // R + 1

                def load(i, off):
                    if not self.has(i, off):
                        return
                    k = off % R
                    if self.has(i, off - R):
                        sp.wait_ge(S("oht"), c(i, off - R))
                        fence(sp)
                    sp.dma_start(at_in[k][:, 0:TPG * RAW],
                                 self.group(attr_p.rearrange("(g p t) w -> g p (t w)", p=P, t=TPG), i, off)).then_inc(S(f"at{k}"), 16)
                    sp.dma_start(rel_b[k], rel_rows[ds(R * i + off, 1), :].rearrange("a e -> (a e)").partition_broadcast(P)).then_inc(S(f"rb{k}"), 16)

                def store(i, off):
                    if not self.has(i, off):
                        return
                    k = off % R
                    sp.wait_ge(S("oht"), c(i, off))
                    fence(sp)
                    sp.dma_start(self.group(matrices, i, off), both0[k]).then_inc(S(f"oh{k}"), 16)

                for g in range(self.lo, self.lo + 3):
                    load(0, g)

                def body(i):
                    for j in range(R):
                        if self.runs(i, j):
                            load(i, j + 3)
                        store(i, j - 2)

                self.loop(sp, body, back=2, ahead=3)
                for j in range(R):
                    n = ring((self.hi - 1 - j) // R, j)
                    sp.wait_ge(S(f"st{j}"), 16 * n)
                    sp.wait_ge(S(f"oh{j}"), 16 * n)
                sp.wait_ge(S("deg"), self.hi)

            def pe(self, pe):
                S = self.S
                c = lambda i, off: R * i + off + 1
                ring = lambda i, off: i + off // R + 1

                def turn(i, off):
                    if not self.has(i, off):
                        return
                    k = off % R
                    pe.wait_ge(S(f"at{k}"), 16 * ring(i, off))
                    if self.has(i, off - 2):
                        pe.wait_ge(S("atlo"), c(i, off - 2))
                    pe.transpose(psum[0:TPG * RAW + 1, off % 2, 0:P], at_in[k], ident32[:, :]).then_inc(S("atT"), 1)

                def encode(i, off):
                    if not self.has(i, off):
                        return
                    pe.wait_ge(S("atlo"), c(i, off))
                    if self.has(i, off - 2):
                        pe.wait_ge(S("enc"), c(i, off - 2))
                    pe.matmul(psum[:, 2 + off % 2, :], at16[off % 2][0:96, :], enc16[:, :],
                              start=True, stop=True).then_inc(S("encm"), 1)

                def count(i, off):
                    if not self.has(i, off):
                        return
                    k = off % R
                    pe.wait_ge(S("oh"), c(i, off))
                    if self.has(i, off - 2):
                        pe.wait_ge(S("deg"), c(i, off - 2))
                    fence(pe)
                    for t in range(TPG):
                        x = pe.matmul(psum[:, 4 + off % 2, 0:P], ones16[:, :], oh0[k][:, t * P:(t + 1) * P],
                                      start=t == 0, stop=t == TPG - 1)
                    x.then_inc(S("degm"), 1)

                def body(i):
                    for j in range(R):
                        if self.runs(i, j):
                            turn(i, j + 1)
                        encode(i, j)
                        count(i, j - 1)

                pe.wait_ge(S("one"), R + 2)
                turn(0, self.lo)
                self.loop(pe, body, back=3, ahead=1)

            def act(self, act):
                S = self.S
                c = lambda i, off: R * i + off + 1
                ring = lambda i, off: i + off // R + 1

                def turned(i, off):
                    if not self.has(i, off):
                        return
                    act.wait_ge(S("atT"), c(i, off))
                    if self.has(i, off - 2):
                        act.wait_ge(S("encm"), c(i, off - 2))
                    for row in (0, 32):
                        x = act.copy(at16[off % 2][row:row + TPG * RAW + 1, :], psum[0:TPG * RAW + 1, off % 2, 0:P])
                    x.then_inc(S("atc"), 1)

                def silu(i, off):
                    if not self.has(i, off):
                        return
                    act.wait_ge(S("encm"), c(i, off))
                    if self.has(i, off - R):
                        act.wait_ge(S("lo"), c(i, off - R))
                    act.activation(e0[off % R], psum[:, 2 + off % 2, :], ACT.Silu).then_inc(S("enc"), 1)

                def high(i, off):
                    if not self.has(i, off):
                        return
                    k = off % R
                    act.wait_ge(S("enc"), c(i, off))
                    if self.has(i, off - R):
                        act.wait_ge(S(f"st{k}"), 16 * ring(i, off - R))
                    act.copy(st0[k][:, :, 0:D], e0[k].rearrange("p (t f) -> p t f", t=TPG)).then_inc(S("hi"), 1)

                def store(i, off):
                    if not self.has(i, off):
                        return
                    k = off % R
                    act.wait_ge(S("lo"), c(i, off))
                    fence(act)
                    act.dma_start(self.group(state, i, off), st0[k].rearrange("p t c -> p (t c)")).then_inc(S(f"st{k}"), 16)

                act.wait_ge(S("one"), R + 2)
                turned(0, self.lo)

                def body(i):
                    for j in range(R):
                        if self.runs(i, j):
                            turned(i, j + 1)
                        silu(i, j)
                        high(i, j - 1)
                        store(i, j - 2)

                self.loop(act, body, back=5, ahead=1)

            def pool(self, pool):
                S = self.S
                c = lambda i, off: R * i + off + 1

                def low(i, off):
                    if not self.has(i, off):
                        return
                    k = off % R
                    pool.wait_ge(S("hi"), c(i, off))
                    pool.tensor_tensor(st0[k][:, :, D:2 * D], e0[k].rearrange("p (t f) -> p t f", t=TPG),
                                       st0[k][:, :, 0:D], ALU.subtract).then_inc(S("lo"), 1)

                def body(i):
                    for j in range(R):
                        low(i, j)

                self.loop(pool, body, back=0, ahead=0)

            def dve(self, dve):
                S = self.S
                c = lambda i, off: R * i + off + 1
                ring = lambda i, off: i + off // R + 1

                def rel(i, off):
                    if not self.has(i, off):
                        return
                    if self.has(i, off - R):
                        dve.wait_ge(S("oh"), c(i, off - R))
                    dve.tensor_copy(rel_now[off % R], rel_all[:, :, ds(R * i + off, 1)].rearrange("p t a -> p (t a)")).then_inc(S("rel"), 1)

                def matrices_of(i, off):
                    if not self.has(i, off):
                        return
                    k = off % R
                    if self.has(i, off - R):
                        dve.wait_ge(S(f"oh{k}"), 16 * ring(i, off - R))
                        dve.wait_ge(S("degm"), c(i, off - R))
                    dve.wait_ge(S("rel"), c(i, off))
                    fence(dve)
                    for t in range(TPG):
                        x = dve.tensor_scalar(oh0[k][:, t * P:(t + 1) * P], node_iota[:, :], rel_now[k][:, t:t + 1],
                                              None, ALU.is_equal, saturate=False)
                    x.then_inc(S("oh"), 1)
                    dve.wait_ge(S(f"rb{k}"), 16 * ring(i, off))
                    fence(dve)
                    dve.tensor_scalar(oht0[k], rel_b[k], part_iota[:, :], None,
                                      ALU.is_equal, saturate=False).then_inc(S("oht"), 1)

                def window(i, off):
                    if self.has(i, off):
                        return dve.value_load(win[0:1, ds(R * i + off, 1)], min_val=0, max_val=N - P)

                def add_counts(i, off, w):
                    if not self.has(i, off):
                        return
                    if self.has(i, off - 1):
                        dve.wait_ge(S("deg"), c(i, off - 1))
                    dve.wait_ge(S("degm"), c(i, off))
                    dve.tensor_tensor(degree[:, ds(w, P)], degree[:, ds(w, P)], psum[:, 4 + off % 2, 0:P], ALU.add).then_inc(S("deg"), 1)

                def low_attributes(i, off):
                    if not self.has(i, off):
                        return
                    if self.has(i, off - 2):
                        dve.wait_ge(S("encm"), c(i, off - 2))
                    dve.wait_ge(S("atc"), c(i, off))
                    dve.tensor_tensor(at16[off % 2][64:64 + TPG * RAW + 1, :], psum[0:TPG * RAW + 1, off % 2, 0:P],
                                       at16[off % 2][0:TPG * RAW + 1, :], ALU.subtract).then_inc(S("atlo"), 1)

                if self.lo == 0:
                    for k in range(R):
                        dve.memset(at_in[k][:, TPG * RAW:TPG * RAW + 1], 1.0).then_inc(S("one"), 1)
                    for k in range(2):
                        dve.memset(at16[k][0:96, :], 0.0).then_inc(S("one"), 1)
                    dve.wait_ge(S("one"), R + 2)
                rel(0, self.lo)
                low_attributes(0, self.lo)

                def body(i):
                    for j in range(R):
                        if self.runs(i, j):
                            rel(i, j + 1)
                            low_attributes(i, j + 1)
                        matrices_of(i, j)
                        w = window(i, j - 2)
                        add_counts(i, j - 2, w)

                self.loop(dve, body, back=4, ahead=1)

        I1, I2 = Init(Z, 0, G1), Init(Z, G1, G2)

        class Edge(Groups):

            def last_step(self, s):
                return isinstance(s, int) and s == STEPS - 1

            def ring(self, s, i, off):
                j = off % R
                return s * len(range(j, G2, R)) + i + off // R + 1

            def gathered(self, s, i, off):
                j = off % R
                n = sum(g % R == j for g in range(self.lo, self.hi))
                before = sum(g % R == j for g in range(self.lo))
                return self.rows_sem(off), 16 * TPG * (s * n + i + off // R + 1 - before)

            def rows_sem(self, off):
                return self.S(f"rows{off % R}" if self.lo == 0 else f"extra_rows{off % R}")

            def skip_per_group(self, eng, *names):
                for x in names:
                    eng.sem_inc(self.S(x), G2 - G1)

            def skip_ring(self, eng, name, per_group):
                for j in range(R):
                    n = sum(g % R == j for g in range(G1, G2))
                    eng.sem_inc(self.S(f"{name}{j}"), per_group * n)

            def skip_sp(self, sp):
                self.skip_ring(sp, "st", 16)
                self.skip_ring(sp, "q", 32)
                self.skip_ring(sp, "oh", 16)
                self.skip_ring(sp, "out", 16)

            def skip_pool(self, pool):
                self.skip_per_group(pool, "idx")

            def skip_pe(self, pe):
                self.skip_per_group(pe, "transposed", "src", "h", "v", "sum")

            def skip_act(self, act):
                self.skip_per_group(act, "h32", "hh", "eT", "sq", "eh")

            def skip_dve(self, dve):
                self.skip_per_group(dve, "hl", "scaled", "new", "resid", "el", "added")
                dve.sem_inc(self.S("newton"), NEWTON_OPS * (G2 - G1))

            def sp(self, sp, s):
                S = self.S
                c = lambda i, off: s * G2 + R * i + off + 1

                def group(ap, i, off):
                    return ap[ds(R * i + off, 1), :, :].rearrange("a p c -> (a p) c")

                def load(i, off):
                    if not self.has(i, off):
                        return
                    k = off % R
                    if self.has(i, off - R):
                        sp.wait_ge(S("resid"), c(i, off - R))
                        sp.wait_ge(S("transposed"), c(i, off - R))
                        sp.wait_ge(S("h"), c(i, off - R))
                        fence(sp)
                    sp.dma_start(st_in[k].rearrange("p t c -> p (t c)"), group(state, i, off)).then_inc(S(f"st{k}"), 16)
                    w = sp.value_load(win[0:1, ds(R * i + off, 1)], min_val=0, max_val=N - P)
                    sp.dma_start(q_win[k], q_table[ds(w, P), :]).then_inc(S(f"q{k}"), 16)
                    sp.dma_start(oht[k].bitcast(F32), group(matrices, i, off)[:, GE // 4:GE // 2]).then_inc(S(f"q{k}"), 16)

                def load_sum(i, off):
                    if not self.has(i, off):
                        return
                    k = off % R
                    if self.has(i, off - R):
                        sp.wait_ge(S("sum"), c(i, off - R))
                        fence(sp)
                    sp.dma_start(oh[k].bitcast(F32), group(matrices, i, off)[:, 0:GE // 4]).then_inc(S(f"oh{k}"), 16)

                def store(i, off):
                    if not self.has(i, off) or self.last_step(s):
                        return
                    k = off % R
                    sp.wait_ge(S("el"), c(i, off))
                    fence(sp)
                    sp.dma_start(group(state, i, off), st_out[k].rearrange("p t c -> p (t c)")).then_inc(S(f"out{k}"), 16)

                for g in range(self.lo, self.lo + 3):
                    load(0, g)

                def body(i):
                    for j in range(R):
                        if self.has(i, j):
                            load(i, j + 3)
                            load_sum(i, j - 1)
                            store(i, j - 4)

                self.loop(sp, body, back=5, ahead=3)
                last = self.hi - 1
                load_sum(0, last)
                for g in range(last - 3, last + 1):
                    store(0, g)
                if not self.last_step(s):
                    for j in range(R):
                        sp.wait_ge(S(f"out{j}"), 16 * self.ring(s, (self.hi - 1 - j) // R, j))
                        fence(sp)
                sp.wait_ge(S("added"), c(0, self.hi - 1))
                fence(sp)

            def pool(self, pool, s):
                S = self.S
                c = lambda i, off: s * G2 + R * i + off + 1

                def indices(i, off):
                    if not self.has(i, off):
                        return
                    k = off % R
                    if self.has(i, off - R):
                        pool.wait_ge(*self.gathered(s, i, off - R))
                        fence(pool)
                    pool.tensor_copy(idx_now[k], idx_all[:, ds(R * i + off, 1), :].rearrange("p a t -> p (a t)")).then_inc(S("idx"), 1)

                def gather(i, off):
                    if not self.has(i, off):
                        return
                    k = off % R
                    if self.has(i, off - R):
                        pool.wait_ge(S("src"), c(i, off - R))
                    pool.wait_ge(S("idx"), c(i, off))
                    fence(pool)
                    for t in range(TPG):
                        pool.indirect_dma_start(
                            out=rows[k][:, t, :], out_offset=None, in_=p_table,
                            in_offset=bass.IndirectOffsetOnAxis(ap=idx_now[k][:, t:t + 1], axis=0),
                        ).then_inc(self.rows_sem(off), 16)

                indices(0, self.lo)

                def body(i):
                    for j in range(R):
                        if self.has(i, j):
                            indices(i, j + 1)
                            gather(i, j)

                self.loop(pool, body, back=4, ahead=1)

            def pe(self, pe, s):
                S = self.S
                c = lambda i, off: s * G2 + R * i + off + 1

                def turn(i, off):
                    if not self.has(i, off):
                        return
                    k = off % R
                    pe.wait_ge(S(f"st{k}"), 16 * self.ring(s, i, off))
                    if self.has(i, off - 1):
                        pe.wait_ge(S("eT"), c(i, off - 1))
                    for p in range(2):
                        for t in range(TPG):
                            n = p * TPG + t
                            x = pe.transpose(ps_t[:, n * P:(n + 1) * P], st_in[k][:, t, p * D:(p + 1) * D], ident16[:, :])
                    x.then_inc(S("transposed"), 1)

                def hidden(i, off):
                    if not self.has(i, off):
                        return
                    k, k2 = off % R, off % 2
                    pe.wait_ge(S(f"q{k}"), 32 * self.ring(s, i, off))
                    if self.has(i, off - 2):
                        pe.wait_ge(S("hh"), c(i, off - 2))
                    fence(pe)
                    for half in range(2):
                        for p in range(2):
                            pe.matmul(ps_h(k2)[:, half, :], q_win[k][:, p * H + half * D:p * H + half * D + D], oht[k],
                                      start=p == 0, stop=False, skip_group_check=True)
                    pe.wait_ge(*self.gathered(s, i, off))
                    for t in range(TPG):
                        for half in range(2):
                            for p in range(2):
                                x = pe.matmul(ps_h(k2)[:, half, t * P:(t + 1) * P],
                                              rows[k][:, t, p * H + half * D:p * H + half * D + D], ident16[:, :],
                                              start=False, stop=False, skip_group_check=True)
                    x.then_inc(S("src"), 1)
                    pe.wait_ge(S("eT"), c(i, off))
                    for half in range(2):
                        cols = slice(half * D, (half + 1) * D)
                        for w, p in ((w1_hi, 0), (w1_hi, 1), (w1_lo, 0)):
                            x = pe.matmul(ps_h(k2)[:, half, :], w[:, cols], eT[k2][:, p, :],
                                          start=False, stop=w is w1_lo, skip_group_check=True)
                    x.then_inc(S("h"), 1)

                def output(i, off):
                    if not self.has(i, off):
                        return
                    k2 = off % 2
                    if self.has(i, off - 2):
                        pe.wait_ge(S("scaled"), c(i, off - 2))
                    pe.matmul(ps_v(k2), ones16[0:64, :], v_bias[:, :], start=True, stop=False, skip_group_check=True)
                    pe.wait_ge(S("hl"), c(i, off))
                    for t in range(TPG):
                        for half in range(2):
                            for h, w in ((hh, w2_hi), (hh, w2_lo), (hl, w2_hi)):
                                x = pe.matmul(ps_v(k2)[:, t * P:(t + 1) * P], h[k2][:, half, t * P:(t + 1) * P], w[:, half, :],
                                              start=False, stop=half == 1 and h is hl, skip_group_check=True)
                    x.then_inc(S("v"), 1)

                def node_sums(i, off):
                    if not self.has(i, off):
                        return
                    k = off % R
                    pe.wait_ge(S("el"), c(i, off))
                    if self.has(i, off - 1):
                        pe.wait_ge(S("added"), c(i, off - 1))
                    pe.wait_ge(S(f"oh{k}"), 16 * self.ring(s, i, off))
                    fence(pe)
                    for t in range(TPG):
                        for p in range(2):
                            x = pe.matmul(ps_a[:, 0:P], st_out[k][:, t, p * D:(p + 1) * D], oh[k][:, t * P:(t + 1) * P],
                                          start=t == 0 and p == 0, stop=t == TPG - 1 and p == 1, skip_group_check=True)
                    x.then_inc(S("sum"), 1)

                turn(0, self.lo)
                turn(0, self.lo + 1)

                def body(i):
                    for j in range(R):
                        if self.has(i, j):
                            hidden(i, j)
                            turn(i, j + 2)
                            output(i, j - 1)
                            node_sums(i, j - 4)

                self.loop(pe, body, back=5, ahead=2)
                output(0, self.hi - 1)
                for g in range(self.hi - 4, self.hi):
                    node_sums(0, g)

            def act(self, act, s):
                S = self.S
                c = lambda i, off: s * G2 + R * i + off + 1

                def silu(i, off):
                    if not self.has(i, off):
                        return
                    k2 = off % 2
                    act.wait_ge(S("h"), c(i, off))
                    if self.has(i, off - 2):
                        act.wait_ge(S("hl"), c(i, off - 2))
                    act.activation(h32[k2], ps_h(k2), ACT.Silu).then_inc(S("h32"), 1)
                    if self.has(i, off - 2):
                        act.wait_ge(S("v"), c(i, off - 2))
                    act.activation(hh[k2], ps_h(k2), ACT.Silu).then_inc(S("hh"), 1)

                def squares(i, off):
                    if not self.has(i, off):
                        return
                    k2 = off % 2
                    act.wait_ge(S("v"), c(i, off))
                    if self.has(i, off - 2):
                        act.wait_ge(S("sq"), c(i, off - 2))
                        act.wait_ge(S("scaled"), c(i, off - 2))
                    for t in range(TPG):
                        x = act.activation(sq[k2][:, t * P:(t + 1) * P], ps_v(k2)[:, t * P:(t + 1) * P], ACT.Square,
                                           accum_out=nv[k2][:, t:t + 1])
                    x.then_inc(S("sq"), 1)

                def turned(i, off):
                    if not self.has(i, off):
                        return
                    k2 = off % 2
                    act.wait_ge(S("transposed"), c(i, off))
                    if self.has(i, off - 2):
                        act.wait_ge(S("h"), c(i, off - 2))
                    act.copy(eT[k2].rearrange("p k e -> p (k e)"), ps_t[:, :]).then_inc(S("eT"), 1)

                def high(i, off):
                    if not self.has(i, off):
                        return
                    k, k2 = off % R, off % 2
                    act.wait_ge(S("new"), c(i, off))
                    if self.has(i, off - R):
                        act.wait_ge(S("sum"), c(i, off - R))
                        if not self.last_step(s):
                            act.wait_ge(S(f"out{k}"), 16 * self.ring(s, i, off - R))
                    act.copy(st_out[k][:, :, 0:D], e_new[k2].rearrange("p (t f) -> p t f", t=TPG)).then_inc(S("eh"), 1)

                turned(0, self.lo)
                turned(0, self.lo + 1)

                def body(i):
                    for j in range(R):
                        if self.has(i, j):
                            silu(i, j)
                            squares(i, j - 1)
                            turned(i, j + 2)
                            high(i, j - 3)

                self.loop(act, body, back=7, ahead=2)
                last = self.hi - 1
                high(0, last - 2)
                squares(0, last)
                high(0, last - 1)
                high(0, last)

            def dve(self, dve, s):
                S = self.S
                c = lambda i, off: s * G2 + R * i + off + 1

                def low(i, off):
                    if not self.has(i, off):
                        return
                    k2 = off % 2
                    dve.wait_ge(S("hh"), c(i, off))
                    dve.wait_ge(S("h32"), c(i, off))
                    if self.has(i, off - 2):
                        dve.wait_ge(S("v"), c(i, off - 2))
                    dve.tensor_tensor(hl[k2], h32[k2], hh[k2], ALU.subtract).then_inc(S("hl"), 1)

                def root(i, off, a, b):
                    if not self.has(i, off):
                        return
                    k2 = off % 2
                    if a == 0:
                        dve.wait_ge(S("sq"), c(i, off))
                        if self.has(i, off - 2):
                            dve.wait_ge(S("scaled"), c(i, off - 2))
                    newton(dve, nv[k2], rs[k2], nt[k2], S("newton"), (c(i, off) - 1) * NEWTON_OPS, a, b)

                def scale(i, off, t):
                    if not self.has(i, off):
                        return
                    k2 = off % 2
                    if t == 0:
                        dve.wait_ge(S("newton"), c(i, off) * NEWTON_OPS)
                        if self.has(i, off - 2):
                            dve.wait_ge(S("el"), c(i, off - 2))
                    x = dve.scalar_tensor_tensor(e_new[k2][:, t * P:(t + 1) * P], ps_v(k2)[:, t * P:(t + 1) * P],
                                                 rs[k2][:, t:t + 1], g_row[:, :], ALU.mult, ALU.mult)
                    if t == TPG - 1:
                        x.then_inc(S("scaled"), 1)

                def add_old(i, off):
                    if not self.has(i, off):
                        return
                    k, k2 = off % R, off % 2
                    dve.wait_ge(S("scaled"), c(i, off))
                    dve.wait_ge(S("resid"), c(i, off))
                    dve.tensor_tensor(e_new[k2], e_new[k2], resid[k], ALU.add).then_inc(S("new"), 1)

                def old(i, off):
                    if not self.has(i, off):
                        return
                    k = off % R
                    dve.wait_ge(S(f"st{k}"), 16 * self.ring(s, i, off))
                    if self.has(i, off - R):
                        dve.wait_ge(S("new"), c(i, off - R))
                    dve.tensor_tensor(resid[k].rearrange("p (t f) -> p t f", t=TPG), st_in[k][:, :, 0:D],
                                      st_in[k][:, :, D:2 * D], ALU.add).then_inc(S("resid"), 1)

                def low_new(i, off):
                    if not self.has(i, off):
                        return
                    k, k2 = off % R, off % 2
                    dve.wait_ge(S("eh"), c(i, off))
                    dve.tensor_tensor(st_out[k][:, :, D:2 * D], e_new[k2].rearrange("p (t f) -> p t f", t=TPG),
                                      st_out[k][:, :, 0:D], ALU.subtract).then_inc(S("el"), 1)

                def window(i, off):
                    if self.has(i, off):
                        return dve.value_load(win[0:1, ds(R * i + off, 1)], min_val=0, max_val=N - P)

                def add_window(i, off, w):
                    if not self.has(i, off):
                        return
                    if self.has(i, off - 1):
                        dve.wait_ge(S("added"), c(i, off - 1))
                    dve.wait_ge(S("sum"), c(i, off))
                    dve.tensor_tensor(agg[:, ds(w, P)], agg[:, ds(w, P)], ps_a[:, 0:P], ALU.add).then_inc(S("added"), 1)

                old(0, self.lo)

                def body(i):
                    for j in range(R):
                        if not self.has(i, j):
                            continue
                        low(i, j)
                        w = window(i, j - 4)
                        root(i, j - 1, 0, 1)
                        add_window(i, j - 4, w)
                        for t in range(TPG):
                            root(i, j - 1, t + 1, t + 2)
                            scale(i, j - 2, t)
                        root(i, j - 1, 5, 6)
                        low_new(i, j - 3)
                        root(i, j - 1, 6, 7)
                        add_old(i, j - 2)
                        root(i, j - 1, 7, 8)
                        old(i, j + 1)
                        root(i, j - 1, 8, NEWTON_OPS)

                self.loop(dve, body, back=5, ahead=1)
                last = self.hi - 1
                for t in range(TPG):
                    scale(0, last - 1, t)
                low_new(0, last - 2)
                add_old(0, last - 1)
                add_window(0, last - 3, window(0, last - 3))
                w = window(0, last - 2)
                root(0, last, 0, 6)
                low_new(0, last - 1)
                root(0, last, 6, 8)
                root(0, last, 8, NEWTON_OPS)
                for t in range(TPG):
                    scale(0, last, t)
                add_window(0, last - 2, w)
                add_old(0, last)
                add_window(0, last - 1, window(0, last - 1))
                low_new(0, last)
                add_window(0, last, window(0, last))

        S1, S2 = Edge(ES, 0, G1), Edge(ES, G1, G2)

        HALF = CW // 2
        QUARTERS = [(half, m) for half in range(2) for m in range(2)]

        def ps_n(c, j):
            return psum[:, j % 2, 0:HALF]

        def ps_u(t):
            return psum[:, 4 + t // 4, (t % 4) * P:(t % 4) * P + P]

        def ps_p(t):
            return psum[:, (2, 6, 7)[t % 3], :]

        class Node:

            def __init__(self, S, update, tables, final):
                self.S, self.update, self.tables, self.final = S, update, tables, final

            def counts(self, s, c):
                a = s * NCH + c
                return a, a + (NCH if self.update else 0)

            def schedule(self, hidden, output, tables):
                hidden(0)
                for c in range(NCH):
                    if c + 1 < NCH:
                        hidden(c + 1)
                    output(c, lambda: tables(c - 1) if c else None)
                tables(NCH - 1)

            def sp(self, sp, s):
                S = self.S
                if self.tables:
                    for c in range(NCH):
                        _, b = self.counts(s, c)
                        for t in range(CH):
                            sp.wait_ge(S("plo"), CH * b + t + 1)
                            fence(sp)
                            for k, table in ((0, p_table), (1, q_table)):
                                sp.dma_start(table[c * CW + t * P:c * CW + (t + 1) * P, :].rearrange("n (s e) -> n s e", s=2),
                                             pq[t][:, :, k, :]).then_inc(S(f"tab{t}"), 16)
                    for t in range(CH):
                        sp.wait_ge(S(f"tab{t}"), 32 * (self.counts(s, 0)[1] + NCH))
                        fence(sp)
                if self.final:
                    for c in range(NCH):
                        sp.wait_ge(S("fin"), c + 1)
                        whole = min((c + 1) * CH, N // P) - c * CH
                        sp.dma_start(out[c * CW:c * CW + whole * P, :].rearrange("(t p) f -> p t f", p=P),
                                     xf[c % 2][:, 0:whole, :]).then_inc(S(f"xst{c % 2}"), 16)
                        if whole < CH:
                            sp.dma_start(out[N // P * P:N, :], xf[c % 2][0:N % P, whole, :]).then_inc(S("xlast"), 16)
                    sp.wait_ge(S("xst0"), 48)
                    sp.wait_ge(S("xst1"), 32)
                    sp.wait_ge(S("xlast"), 16)

            def pe(self, pe, s):
                S = self.S

                def hidden(c):
                    if not self.update:
                        return
                    a, _ = self.counts(s, c)
                    for j, (half, m) in enumerate(QUARTERS):
                        if 4 * c + j >= 2:
                            pe.wait_ge(S("act1"), 4 * a + j - 1)
                        cols = slice(c * CW + half * HALF, c * CW + (half + 1) * HALF)
                        for k, rhs in enumerate((xT_all, agg)):
                            x = pe.matmul(ps_n(c, j), nw1[:, k, m * P:(m + 1) * P], rhs[:, cols], start=k == 0, stop=k == 1)
                        x.then_inc(S("hid"), 1)

                def output(c, after):
                    if not self.update:
                        return after()
                    a, _ = self.counts(s, c)
                    if c:
                        pe.wait_ge(S("scaled"), a)
                    for t in range(CH):
                        pe.wait_ge(S("act1"), 4 * a + (2 if t < 2 else 4))
                        pe.matmul(ps_u(t), ones16[0:64, :], u_bias[:, :], start=True, stop=False, skip_group_check=True)
                        for k in range(2):
                            x = pe.matmul(ps_u(t), hN[c % 2][:, k, t * P:(t + 1) * P], nw2[:, k, :], start=False, stop=k == 1,
                                          skip_group_check=True)
                        x.then_inc(S("u"), 1)
                    after()

                def tables(c):
                    if not self.tables:
                        return
                    a, b = self.counts(s, c)
                    if self.update:
                        pe.wait_ge(S("xn"), a + 1)
                    for t in range(CH):
                        if t == CH - 1:
                            pe.wait_ge(S("xT"), 2 * b + 1)
                        elif t == 0 and c:
                            pe.wait_ge(S("xT"), 2 * b)
                        x = pe.transpose(psum[:, 3, (t % 4) * P:(t % 4 + 1) * P], x_all[:, c * CH + t, :], ident32[:, :])
                        if t >= CH - 2:
                            x.then_inc(S("xTp"), 1)
                    for t in range(CH):
                        pe.wait_ge(S("xT"), 2 * b + 1 + (t == CH - 1))
                        if t >= 3:
                            pe.wait_ge(S("plo"), CH * b + t - 2)
                        elif t < 2 and c:
                            pe.wait_ge(S("plo"), CH * b + t - 1)
                        cols = slice(c * CW + t * P, c * CW + (t + 1) * P)
                        pe.matmul(ps_p(t), xT_all[:, cols], w_pq[:, :, :].rearrange("p k h -> p (k h)"),
                                  start=True, stop=False, skip_group_check=True)
                        pe.matmul(ps_p(t)[:, 0:H], ones16[0:64, :], p_bias[:, :], start=False, stop=True,
                                  skip_group_check=True).then_inc(S("pq"), 1)

                self.schedule(hidden, output, tables)

            def act(self, act, s):
                S = self.S

                def hidden(c):
                    if not self.update:
                        return
                    a, _ = self.counts(s, c)
                    if c >= 2:
                        act.wait_ge(S("u"), CH * (a - 1))
                    for j, (half, m) in enumerate(QUARTERS):
                        act.wait_ge(S("hid"), 4 * a + j + 1)
                        act.activation(hN[c % 2][:, m, half * HALF:(half + 1) * HALF], ps_n(c, j), ACT.Silu,
                                       bias=nb1_col[:, m:m + 1]).then_inc(S("act1"), 1)

                def output(c, after):
                    if not self.update:
                        return after()
                    a, _ = self.counts(s, c)
                    if c >= 2:
                        act.wait_ge(S("usq"), a - 1)
                        act.wait_ge(S("scaled"), a - 1)
                    for t in range(CH):
                        act.wait_ge(S("u"), CH * a + max(t + 1, 4))
                        x = act.activation(sqn[c % 2][:, t * D:(t + 1) * D], ps_u(t), ACT.Square,
                                           accum_out=stn[c % 2][:, t:t + 1])
                    x.then_inc(S("usq"), 1)
                    after()

                def tables(c):
                    if not self.tables:
                        return
                    _, b = self.counts(s, c)
                    for part, tiles in enumerate((CH - 1, 1)):
                        act.wait_ge(S("xTp"), 2 * b + part + 1)
                        first = c * CW + part * (CH - 1) * P
                        act.copy(xT_all[:, first:first + tiles * P], psum[:, 3, 0:tiles * P]).then_inc(S("xT"), 1)
                    for t in range(CH):
                        act.wait_ge(S("pq"), CH * b + t + 1)
                        if c:
                            act.wait_ge(S(f"tab{t}"), 32 * b)
                        act.copy(pq[t][:, 0, :, :], ps_p(t).rearrange("p (k h) -> p k h", k=2)).then_inc(S("phi"), 1)

                self.schedule(hidden, output, tables)

            def dve(self, dve, s):
                S = self.S

                def update(c, low):
                    a, _ = self.counts(s, c)
                    dve.wait_ge(S("usq"), a + 1)
                    y, k = nvn[:, 0:CH], c % 2
                    for t in range(CH):
                        newton(dve, stn[k][:, 0:CH], y, ntn[:, 0:CH], S("newton"), NEWTON_OPS * a, 2 * t, 2 * t + 2)
                        low(t)
                    newton(dve, stn[k][:, 0:CH], y, ntn[:, 0:CH], S("newton"), NEWTON_OPS * a, 2 * CH, NEWTON_OPS)
                    dve.wait_ge(S("newton"), NEWTON_OPS * a + NEWTON_OPS)
                    for t in range(CH):
                        x = dve.scalar_tensor_tensor(un[:, t, :], ps_u(t), nvn[:, t:t + 1], ng_row[:, :], ALU.mult, ALU.mult)
                    x.then_inc(S("scaled"), 1)
                    xc = x_all[:, c * CH:(c + 1) * CH, :]
                    dve.wait_ge(S("scaled"), a + 1)
                    dve.tensor_tensor(un, un, nbeta_row[:, :].unsqueeze(1).to_broadcast([P, CH, D]), ALU.add).then_inc(S("shifted"), 1)
                    dve.wait_ge(S("shifted"), a + 1)
                    dve.tensor_tensor(xc, xc, un, ALU.add).then_inc(S("xn"), 1)

                def last_norm(c):
                    a, _ = self.counts(s, c)
                    xk = xf[c % 2]
                    steps = 4 * c

                    def done(n, x):
                        x.then_inc(S("final"), 1)
                        dve.wait_ge(S("final"), steps + n)

                    dve.wait_ge(S("xn"), a + 1)
                    if c >= 2:
                        dve.wait_ge(S(f"xst{c % 2}"), 16 * (c // 2))
                    done(1, dve.tensor_tensor(xk, x_all[:, c * CH:(c + 1) * CH, :], x0_all[:, c * CH:(c + 1) * CH, :], ALU.add))
                    for t in range(CH):
                        x = dve.bn_stats(bst[:, t, :], xk[:, t, :])
                    done(2, x)
                    for t in range(CH):
                        x = dve.bn_aggr(bag[:, t, :], bst[:, t, :])
                    done(3, x)
                    done(4, dve.tensor_scalar(vf, bag[:, :, 1:2].rearrange("p t s -> p (t s)"), float(D), None, ALU.mult))
                    newton(dve, vf, nvf, ntf, S("newton2"), NEWTON_OPS * c)
                    dve.wait_ge(S("newton2"), NEWTON_OPS * c + NEWTON_OPS)
                    for t in range(CH):
                        x = dve.tensor_scalar(xk[:, t, :], xk[:, t, :], bag[:, t, 0:1], nvf[:, t:t + 1], ALU.subtract, ALU.mult)
                    x.then_inc(S("fin"), 1)

                def low(c, t):
                    if not self.tables or c < 0:
                        return
                    _, b = self.counts(s, c)
                    dve.wait_ge(S("phi"), CH * b + t + 1)
                    dve.tensor_tensor(pq[t][:, 1, :, :], ps_p(t).rearrange("p (k h) -> p k h", k=2),
                                      pq[t][:, 0, :, :], ALU.subtract).then_inc(S("plo"), 1)

                for c in range(NCH):
                    if self.update:
                        update(c, lambda t: low(c - 1, t))
                    else:
                        for t in range(CH):
                            low(c - 1, t)
                    if self.final:
                        last_norm(c)
                for t in range(CH):
                    low(NCH - 1, t)

        tables0 = Node(ND, False, True, False)
        node_mid = Node(ND, True, True, False)
        node_end = Node(ND, True, False, True)


        def general_or_not(eng, then, otherwise=lambda: None):
            with eng.If(eng.value_load(flag[0:1, 0:1], min_val=0, max_val=1) > 0):
                then()
            with eng.Else():
                eng.nop()
                otherwise()

        def nothing(eng, *step):
            pass

        def run(eng, setup, tables, init, init_extra, edges, edges_extra, skip, node, last_node, sp=False, dve=False):
            setup(eng)
            eng.wait_ge(phase, 1)
            tables(eng, 0)
            if sp:
                eng.sem_inc(phase, 1)
            eng.wait_ge(phase, 2)
            init(eng)
            if sp:
                eng.sem_inc(phase, 1)

            def extra_groups():
                eng.wait_ge(phase, 3)
                init_extra(eng)

            general_or_not(eng, extra_groups)
            if sp:
                eng.sem_inc(phase, 1)

            def step(s, node):
                eng.wait_ge(phase, 4 + 3 * s)
                fence(eng)
                if dve:
                    k = SU("bias")
                    dve_b = s * 5
                    eng.tensor_tensor(beta_sum[:, :], beta_sum[:, :], beta_col[:, :], ALU.add).then_inc(k, 1)
                    eng.tensor_tensor(p_bias32[:, :], p_bias32[:, :], beta_w1[:, :], ALU.add).then_inc(k, 1)
                    eng.wait_ge(k, dve_b + 2)
                    n = [dve_b + 2]

                    def done(i):
                        i.then_inc(k, 1)
                        n[0] = n[0] + 1
                        eng.wait_ge(k, n[0])

                    pair_p_bias(done, eng)
                    eng.tensor_scalar(agg[:, :], degree[:, :], beta_sum[:, :], None, ALU.mult).then_inc(SU("seeded"), 1)
                    eng.wait_ge(SU("seeded"), s + 1)
                edges(eng, s)
                if sp:
                    eng.sem_inc(phase, 1)

                eng.wait_ge(phase, 4 + 3 * s + 1)
                fence(eng)

                def extra_groups():
                    edges_extra(eng, s)
                    if sp:
                        eng.sem_inc(phase, 1)

                def no_extra_groups():
                    if sp:
                        eng.sem_inc(phase, 1)
                    skip(eng)

                general_or_not(eng, extra_groups, no_extra_groups)
                eng.wait_ge(phase, 4 + 3 * s + 2)
                fence(eng)
                node(eng, s)
                if sp:
                    eng.sem_inc(phase, 1)

            with eng.Fori(0, STEPS - 1) as s:
                step(s, node)
            step(STEPS - 1, last_node)

        @block.sync
        def _(sp):
            run(sp, setup_sp, tables0.sp, I1.sp, I2.sp, S1.sp, S2.sp, S2.skip_sp, node_mid.sp, node_end.sp, sp=True)

        @block.gpsimd
        def _(pool):
            run(pool, setup_pool, nothing, I1.pool, I2.pool, S1.pool, S2.pool, S2.skip_pool, nothing, nothing)

        @block.vector
        def _(dve):
            run(dve, setup_dve, tables0.dve, I1.dve, I2.dve, S1.dve, S2.dve, S2.skip_dve, node_mid.dve, node_end.dve, dve=True)

        @block.scalar
        def _(act):
            run(act, setup_act, tables0.act, I1.act, I2.act, S1.act, S2.act, S2.skip_act, node_mid.act, node_end.act)

        @block.tensor
        def _(pe):
            run(pe, setup_pe, tables0.pe, I1.pe, I2.pe, S1.pe, S2.pe, S2.skip_pe, node_mid.pe, node_end.pe)


_INS = ['x', 'src', 'dst', 'edge_attr_4', 'L0_gnn_enc_W', 'L0_gnn_enc_b', 'L0_gnn_eW1', 'L0_gnn_eb1',
        'L0_gnn_eW2', 'L0_gnn_eb2', 'L0_gnn_eg', 'L0_gnn_ebeta', 'L0_gnn_nW1', 'L0_gnn_nb1', 'L0_gnn_nW2',
        'L0_gnn_nb2', 'L0_gnn_ng', 'L0_gnn_nbeta']


def kernel(**inputs):
    import numpy as _np
    import concourse.bacc as _bacc
    from concourse import mybir as _mybir
    from concourse.bass_utils import run_bass_kernel_spmd as _run

    nc = _bacc.Bacc("TRN2", target_bir_lowering=False, num_devices=1)
    arrays, args = {}, []
    for name in _INS:
        a = _np.ascontiguousarray(inputs[name])
        arrays[f"in_{name}"] = a
        args.append(nc.dram_tensor(f"in_{name}", a.shape, _mybir.dt.from_np(a.dtype), kind="ExternalInput").ap())
    args.append(nc.dram_tensor("out_0", (N, D), _mybir.dt.float32, kind="ExternalOutput").ap())
    build_program(nc, *args)
    r = _run(nc, [arrays], core_ids=[0])
    return r.results[0]["out_0"]
```
